# Optimizing a Trainium2 kernel written in Bass

```python
import numpy as np
import jax
import jax.numpy as jnp

def _softmax(x, axis=-1):
    return jax.nn.softmax(x, axis=axis)

def _gelu(x):
    return jax.nn.gelu(x, approximate=True)

def _silu(x):
    return jax.nn.silu(x)

def _sigmoid(x):
    return jax.nn.sigmoid(x)

def _layernorm(x, axis=-1, eps=1e-05):
    m = jnp.mean(x, axis=axis, keepdims=True)
    v = jnp.var(x, axis=axis, keepdims=True)
    return (x - m) / jnp.sqrt(v + eps)

def _scatter_add(tgt, idx, src, axis=0):
    return tgt.at[idx].add(src)

def _segment_sum(src, seg, n):
    return jax.ops.segment_sum(src, seg, n)
kernel_name = 'mk_adaln_d2_jaxref_r8_193ed4'

def setup_inputs(seed: int=0):
    np.random.seed(seed)
    _w = jnp.asarray

    def _L0_attn_setup():
        import jax, jax.numpy as jnp
        import numpy as np
        D_MODEL = 128
        N_HEADS = 16
        D_HIDDEN = 512
        BATCH = 2
        N_CTX = 256

        def _split_heads(t, n_heads):
            B, S, D = t.shape
            return t.reshape(B, S, n_heads, D // n_heads).transpose(0, 2, 1, 3)
        key = jax.random.key(seed)
        ks = jax.random.split(key, 4)
        scale = 0.02
        x = jax.random.normal(ks[0], (BATCH, N_CTX, D_MODEL), dtype=jnp.float32)
        Wk = jax.random.normal(ks[1], (D_MODEL, D_MODEL), dtype=jnp.float32) * scale
        bk = jnp.zeros((D_MODEL,), dtype=jnp.float32)
        Wv = jax.random.normal(ks[2], (D_MODEL, D_HIDDEN), dtype=jnp.float32) * scale
        bv = jnp.zeros((D_HIDDEN,), dtype=jnp.float32)
        Wf = jax.random.normal(ks[3], (D_HIDDEN, D_MODEL), dtype=jnp.float32) * scale
        bf = jnp.zeros((D_MODEL,), dtype=jnp.float32)
        return {'x': x, 'Wk': Wk, 'bk': bk, 'Wv': Wv, 'bv': bv, 'Wf': Wf, 'bf': bf}
    _L0_attn_in = _L0_attn_setup()

    def _L0_ffn_setup():
        import jax, jax.numpy as jnp
        import numpy as np
        D_MODEL = 128
        H_SHARED = 256
        H_ROUTED = 128
        N_EXPERTS = 8
        TOP_K = 2
        key = jax.random.key(seed)
        ks = jax.random.split(key, 8)
        B, T = (2, 256)
        sc_d = 1.0 / np.sqrt(D_MODEL)
        sc_hs = 1.0 / np.sqrt(H_SHARED)
        sc_hr = 1.0 / np.sqrt(H_ROUTED)
        return {'x': jax.random.normal(ks[0], (B, T, D_MODEL), dtype=jnp.float32), 'router_w': jax.random.normal(ks[1], (N_EXPERTS, D_MODEL), dtype=jnp.float32) * sc_d, 'router_bias': jnp.zeros((N_EXPERTS,), dtype=jnp.float32), 'sw1': jax.random.normal(ks[2], (D_MODEL, H_SHARED), dtype=jnp.float32) * sc_d, 'sw3': jax.random.normal(ks[3], (D_MODEL, H_SHARED), dtype=jnp.float32) * sc_d, 'sw2': jax.random.normal(ks[4], (H_SHARED, D_MODEL), dtype=jnp.float32) * sc_hs, 'ew1': jax.random.normal(ks[5], (N_EXPERTS, D_MODEL, H_ROUTED), dtype=jnp.float32) * sc_d, 'ew2': jax.random.normal(ks[6], (N_EXPERTS, H_ROUTED, D_MODEL), dtype=jnp.float32) * sc_hr}
    _L0_ffn_in = _L0_ffn_setup()
    _L0_c = _w((lambda *s: np.random.randn(*s).astype(np.float32) * 0.05)(4, 128))
    _L0_wmod = _w((lambda *s: np.random.randn(*s).astype(np.float32) * 0.05)(128, 6 * 128) * 128 ** (-0.5))

    def _L1_attn_setup():
        import math
        import jax, jax.numpy as jnp
        import numpy as np
        B, T, C = (2, 256, 128)
        H, N1, N2, N3 = (16, 6, 4, 6)
        HD = C // H

        def _rotary(T_, hd, dtype):
            inv_freq = 1.0 / 10000.0 ** (jnp.arange(0, hd, 2, dtype=jnp.float32) / hd)
            freqs = jnp.outer(jnp.arange(T_, dtype=jnp.float32), inv_freq)
            return (jnp.cos(freqs)[None, :, None, :].astype(dtype), jnp.sin(freqs)[None, :, None, :].astype(dtype))

        def _apply_rot(x, cos, sin):
            x1, x2 = (x[..., :x.shape[-1] // 2], x[..., x.shape[-1] // 2:])
            return jnp.concatenate([x1 * cos + x2 * sin, -x1 * sin + x2 * cos], axis=-1).astype(x.dtype)

        def _causal_bias(L, S, dtype):
            mask = jnp.triu(jnp.ones((L, S), bool), k=1)
            return jnp.where(mask, jnp.asarray(-jnp.inf, dtype), jnp.asarray(0.0, dtype))

        def _sdpa(q, k, v, scale):
            scores = jnp.einsum('bhtd,bhsd->bhts', q, k) * scale + _causal_bias(q.shape[-2], k.shape[-2], q.dtype)
            return jnp.einsum('bhts,bhsd->bhtd', jax.nn.softmax(scores, axis=-1), v)

        def _hyp_attn(q, k, v, curv):
            eps = 1e-06
            tq = jnp.sqrt(1.0 / curv + jnp.sum(q * q, axis=-1, keepdims=True))
            tk = jnp.sqrt(1.0 / curv + jnp.sum(k * k, axis=-1, keepdims=True))
            inner = jnp.einsum('bhtd,bhsd->bhts', q, k) - tq * jnp.swapaxes(tk, -1, -2)
            arg = jnp.maximum(-curv * inner, 1.0 + 1e-07)
            dis = jnp.sqrt(1.0 / curv) * jnp.arccosh(arg)
            scores = 1.0 / (eps + dis) + _causal_bias(q.shape[-2], k.shape[-2], q.dtype)
            return jnp.einsum('bhts,bhsd->bhtd', jax.nn.softmax(scores, axis=-1), v)
        key = jax.random.key(seed)
        k1, k2, k3 = jax.random.split(key, 3)
        return {'x': jax.random.normal(k1, (B, T, C), jnp.float32), 'qkv_w': jax.random.normal(k2, (3 * C, C), jnp.float32) * C ** (-0.5), 'proj_w': jax.random.normal(k3, (C, C), jnp.float32) * C ** (-0.5), 'proj_b': jnp.zeros((C,), jnp.float32), 'curvature': jnp.ones((1, N2, 1, 1), jnp.float32)}
    _L1_attn_in = _L1_attn_setup()

    def _L1_ffn_setup():
        import jax, jax.numpy as jnp
        import numpy as np
        B, S, D = (1, 256, 128)
        E, F = (16, 128)
        NG, TKG, K = (4, 2, 4)
        NSH = 2
        SCALE = 2.5
        STD = 0.02
        EPG = E // NG

        def _route(x_flat, router_w, bias):
            logits = x_flat.astype(jnp.float32) @ router_w.T
            scores = jax.nn.sigmoid(logits)
            s = scores + bias[None, :]
            sg = s.reshape(-1, NG, EPG)
            group_score = jax.lax.top_k(sg, 2)[0].sum(-1)
            gidx = jax.lax.top_k(group_score, TKG)[1]
            gmask = jnp.sum(jax.nn.one_hot(gidx, NG, dtype=jnp.float32), axis=1) > 0
            emask = jnp.repeat(gmask, EPG, axis=1)
            masked = jnp.where(emask, s, -1.0)
            topk_idx = jax.lax.top_k(masked, K)[1]
            tw = jnp.take_along_axis(scores, topk_idx, axis=1)
            tw = tw / (tw.sum(-1, keepdims=True) + 1e-20)
            tw = tw * SCALE
            return (topk_idx, tw)
        key = jax.random.key(seed)
        ks = jax.random.split(key, 8)
        return {'hidden_states': jax.random.normal(ks[0], (B, S, D), jnp.float32), 'router_w': jax.random.normal(ks[1], (E, D), jnp.float32) * STD, 'bias': jnp.zeros((E,), jnp.float32), 'gate_w': jax.random.normal(ks[2], (E, D, F), jnp.float32) * STD, 'up_w': jax.random.normal(ks[3], (E, D, F), jnp.float32) * STD, 'down_w': jax.random.normal(ks[4], (E, F, D), jnp.float32) * STD, 'sh_gate_w': jax.random.normal(ks[5], (D, NSH * F), jnp.float32) * STD, 'sh_up_w': jax.random.normal(ks[6], (D, NSH * F), jnp.float32) * STD, 'sh_down_w': jax.random.normal(ks[7], (NSH * F, D), jnp.float32) * STD}
    _L1_ffn_in = _L1_ffn_setup()
    _L1_c = _w((lambda *s: np.random.randn(*s).astype(np.float32) * 0.05)(4, 128))
    _L1_wmod = _w((lambda *s: np.random.randn(*s).astype(np.float32) * 0.05)(128, 6 * 128) * 128 ** (-0.5))
    _d = {'L0_attn_x': _L0_attn_in['x'], 'L0_attn_Wk': _L0_attn_in['Wk'], 'L0_attn_bk': _L0_attn_in['bk'], 'L0_attn_Wv': _L0_attn_in['Wv'], 'L0_attn_bv': _L0_attn_in['bv'], 'L0_attn_Wf': _L0_attn_in['Wf'], 'L0_attn_bf': _L0_attn_in['bf'], 'L0_ffn_router_w': _L0_ffn_in['router_w'], 'L0_ffn_router_bias': _L0_ffn_in['router_bias'], 'L0_ffn_sw1': _L0_ffn_in['sw1'], 'L0_ffn_sw3': _L0_ffn_in['sw3'], 'L0_ffn_sw2': _L0_ffn_in['sw2'], 'L0_ffn_ew1': _L0_ffn_in['ew1'], 'L0_ffn_ew2': _L0_ffn_in['ew2'], 'L0_c': _L0_c, 'L0_wmod': _L0_wmod, 'L1_attn_qkv_w': _L1_attn_in['qkv_w'], 'L1_attn_proj_w': _L1_attn_in['proj_w'], 'L1_attn_proj_b': _L1_attn_in['proj_b'], 'L1_attn_curvature': _L1_attn_in['curvature'], 'L1_ffn_router_w': _L1_ffn_in['router_w'], 'L1_ffn_bias': _L1_ffn_in['bias'], 'L1_ffn_gate_w': _L1_ffn_in['gate_w'], 'L1_ffn_up_w': _L1_ffn_in['up_w'], 'L1_ffn_down_w': _L1_ffn_in['down_w'], 'L1_ffn_sh_gate_w': _L1_ffn_in['sh_gate_w'], 'L1_ffn_sh_up_w': _L1_ffn_in['sh_up_w'], 'L1_ffn_sh_down_w': _L1_ffn_in['sh_down_w'], 'L1_c': _L1_c, 'L1_wmod': _L1_wmod}
    _x0 = _d['L0_attn_x']
    _d['L0_attn_x'] = jax.random.normal(jax.random.fold_in(jax.random.key(seed), 1), (4, 1024, 128), dtype=_x0.dtype)
    del _x0
    return _d

def reference(L0_attn_x, L0_attn_Wk, L0_attn_bk, L0_attn_Wv, L0_attn_bv, L0_attn_Wf, L0_attn_bf, L0_ffn_router_w, L0_ffn_router_bias, L0_ffn_sw1, L0_ffn_sw3, L0_ffn_sw2, L0_ffn_ew1, L0_ffn_ew2, L0_c, L0_wmod, L1_attn_qkv_w, L1_attn_proj_w, L1_attn_proj_b, L1_attn_curvature, L1_ffn_router_w, L1_ffn_bias, L1_ffn_gate_w, L1_ffn_up_w, L1_ffn_down_w, L1_ffn_sh_gate_w, L1_ffn_sh_up_w, L1_ffn_sh_down_w, L1_c, L1_wmod):

    def _L0_attn_ref(x, Wk, bk, Wv, bv, Wf, bf):
        import jax, jax.numpy as jnp
        import numpy as np
        D_MODEL = 128
        N_HEADS = 16
        D_HIDDEN = 512
        BATCH = 2
        N_CTX = 256

        def _split_heads(t, n_heads):
            B, S, D = t.shape
            return t.reshape(B, S, n_heads, D // n_heads).transpose(0, 2, 1, 3)
        B, S, D = x.shape
        H = N_HEADS
        Q = _split_heads(x, H)
        K = _split_heads(x @ Wk + bk, H)
        V = _split_heads(x @ Wv + bv, H)
        causal = jnp.tril(jnp.ones((S, S), dtype=bool))
        mask = jnp.where(causal, 0.0, -jnp.inf).astype(x.dtype)
        scores = jnp.einsum('bhqd,bhkd->bhqk', Q, K) + mask
        attn = jax.nn.softmax(scores, axis=-1)
        o = jnp.einsum('bhqk,bhkd->bhqd', attn, V)
        o = o.transpose(0, 2, 1, 3).reshape(B, S, -1)
        return x + jax.nn.gelu(o, approximate=False) @ Wf + bf

    def _L0_ffn_ref(x, router_w, router_bias, sw1, sw3, sw2, ew1, ew2):
        import jax, jax.numpy as jnp
        import numpy as np
        D_MODEL = 128
        H_SHARED = 256
        H_ROUTED = 128
        N_EXPERTS = 8
        TOP_K = 2
        B, T, C = x.shape
        xf = x.reshape(-1, C)
        shared_out = jax.nn.silu(xf @ sw1) * (xf @ sw3) @ sw2
        s = jax.nn.sigmoid((xf @ router_w.T).astype(jnp.float32))
        sel_scores = s + router_bias.astype(jnp.float32)
        _, topk_idx = jax.lax.top_k(sel_scores, TOP_K)
        s_sel = jnp.take_along_axis(s, topk_idx, axis=1)
        denom = s_sel.sum(axis=1, keepdims=True)
        gates = jnp.where(denom > 1e-09, s_sel / (denom + 1e-09), 1.0 / TOP_K).astype(x.dtype)
        one_hot = jax.nn.one_hot(topk_idx, N_EXPERTS, dtype=x.dtype)
        comb = jnp.einsum('nke,nk->ne', one_hot, gates)
        h = jax.nn.gelu(jnp.einsum('nd,edh->neh', xf, ew1), approximate=False)
        y = jnp.einsum('neh,ehd->ned', h, ew2)
        routed_out = jnp.einsum('ned,ne->nd', y, comb)
        return (shared_out + routed_out).reshape(B, T, C)

    def _L1_attn_ref(x, qkv_w, proj_w, proj_b, curvature):
        import math
        import jax, jax.numpy as jnp
        import numpy as np
        B, T, C = (2, 256, 128)
        H, N1, N2, N3 = (16, 6, 4, 6)
        HD = C // H

        def _rotary(T_, hd, dtype):
            inv_freq = 1.0 / 10000.0 ** (jnp.arange(0, hd, 2, dtype=jnp.float32) / hd)
            freqs = jnp.outer(jnp.arange(T_, dtype=jnp.float32), inv_freq)
            return (jnp.cos(freqs)[None, :, None, :].astype(dtype), jnp.sin(freqs)[None, :, None, :].astype(dtype))

        def _apply_rot(x, cos, sin):
            x1, x2 = (x[..., :x.shape[-1] // 2], x[..., x.shape[-1] // 2:])
            return jnp.concatenate([x1 * cos + x2 * sin, -x1 * sin + x2 * cos], axis=-1).astype(x.dtype)

        def _causal_bias(L, S, dtype):
            mask = jnp.triu(jnp.ones((L, S), bool), k=1)
            return jnp.where(mask, jnp.asarray(-jnp.inf, dtype), jnp.asarray(0.0, dtype))

        def _sdpa(q, k, v, scale):
            scores = jnp.einsum('bhtd,bhsd->bhts', q, k) * scale + _causal_bias(q.shape[-2], k.shape[-2], q.dtype)
            return jnp.einsum('bhts,bhsd->bhtd', jax.nn.softmax(scores, axis=-1), v)

        def _hyp_attn(q, k, v, curv):
            eps = 1e-06
            tq = jnp.sqrt(1.0 / curv + jnp.sum(q * q, axis=-1, keepdims=True))
            tk = jnp.sqrt(1.0 / curv + jnp.sum(k * k, axis=-1, keepdims=True))
            inner = jnp.einsum('bhtd,bhsd->bhts', q, k) - tq * jnp.swapaxes(tk, -1, -2)
            arg = jnp.maximum(-curv * inner, 1.0 + 1e-07)
            dis = jnp.sqrt(1.0 / curv) * jnp.arccosh(arg)
            scores = 1.0 / (eps + dis) + _causal_bias(q.shape[-2], k.shape[-2], q.dtype)
            return jnp.einsum('bhts,bhsd->bhtd', jax.nn.softmax(scores, axis=-1), v)
        Bx, Tx, Cx = x.shape
        qkv = x @ qkv_w.T
        q, k, v = jnp.split(qkv, 3, axis=-1)
        q = q.reshape(Bx, Tx, H, HD)
        k = k.reshape(Bx, Tx, H, HD)
        v = v.reshape(Bx, Tx, H, HD)
        cos, sin = _rotary(Tx, HD, x.dtype)
        q = _apply_rot(q, cos, sin)
        k = _apply_rot(k, cos, sin)
        q, k, v = (jnp.swapaxes(t, 1, 2) for t in (q, k, v))
        outs = []
        outs.append(_sdpa(q[:, :N1], k[:, :N1], v[:, :N1], 1.0 / math.sqrt(HD)))
        outs.append(_hyp_attn(q[:, N1:N1 + N2], k[:, N1:N1 + N2], v[:, N1:N1 + N2], curvature))
        qn = q[:, N1 + N2:] / jnp.maximum(jnp.linalg.norm(q[:, N1 + N2:], axis=-1, keepdims=True), 1e-12)
        kn = k[:, N1 + N2:] / jnp.maximum(jnp.linalg.norm(k[:, N1 + N2:], axis=-1, keepdims=True), 1e-12)
        outs.append(_sdpa(qn, kn, v[:, N1 + N2:], math.sqrt(HD)))
        y = jnp.concatenate(outs, axis=1)
        y = jnp.swapaxes(y, 1, 2).reshape(Bx, Tx, Cx)
        return y @ proj_w.T + proj_b

    def _L1_ffn_ref(hidden_states, router_w, bias, gate_w, up_w, down_w, sh_gate_w, sh_up_w, sh_down_w):
        import jax, jax.numpy as jnp
        import numpy as np
        B, S, D = (1, 256, 128)
        E, F = (16, 128)
        NG, TKG, K = (4, 2, 4)
        NSH = 2
        SCALE = 2.5
        STD = 0.02
        EPG = E // NG

        def _route(x_flat, router_w, bias):
            logits = x_flat.astype(jnp.float32) @ router_w.T
            scores = jax.nn.sigmoid(logits)
            s = scores + bias[None, :]
            sg = s.reshape(-1, NG, EPG)
            group_score = jax.lax.top_k(sg, 2)[0].sum(-1)
            gidx = jax.lax.top_k(group_score, TKG)[1]
            gmask = jnp.sum(jax.nn.one_hot(gidx, NG, dtype=jnp.float32), axis=1) > 0
            emask = jnp.repeat(gmask, EPG, axis=1)
            masked = jnp.where(emask, s, -1.0)
            topk_idx = jax.lax.top_k(masked, K)[1]
            tw = jnp.take_along_axis(scores, topk_idx, axis=1)
            tw = tw / (tw.sum(-1, keepdims=True) + 1e-20)
            tw = tw * SCALE
            return (topk_idx, tw)
        x = hidden_states.reshape(-1, D)
        topk_idx, tw = _route(x, router_w, bias)
        combine = (jax.nn.one_hot(topk_idx, E, dtype=tw.dtype) * tw[..., None]).sum(1)
        h = jnp.einsum('td,edf->etf', x, gate_w)
        u = jnp.einsum('td,edf->etf', x, up_w)
        y = jnp.einsum('etf,efd->etd', jax.nn.silu(h) * u, down_w)
        routed = jnp.einsum('etd,te->td', y, combine)
        sh = jax.nn.silu(x @ sh_gate_w) * (x @ sh_up_w) @ sh_down_w
        return (routed + sh).reshape(hidden_states.shape)
    x = L0_attn_x
    mod = (_silu(L0_c) @ L0_wmod).reshape(L0_c.shape[0], 6, 1, -1)
    sa, ca, ga, sb, cb, gb = (mod[:, 0], mod[:, 1], mod[:, 2], mod[:, 3], mod[:, 4], mod[:, 5])
    ga = (2 * (ga >= 0) - 1) * jnp.maximum(jnp.abs(ga), 0.25)
    gb = (2 * (gb >= 0) - 1) * jnp.maximum(jnp.abs(gb), 0.25)
    h = _layernorm(x, axis=-1) * (1 + ca) + sa
    x = x + ga * _L0_attn_ref(h, L0_attn_Wk, L0_attn_bk, L0_attn_Wv, L0_attn_bv, L0_attn_Wf, L0_attn_bf)
    h = _layernorm(x, axis=-1) * (1 + cb) + sb
    x = x + gb * _L0_ffn_ref(h, L0_ffn_router_w, L0_ffn_router_bias, L0_ffn_sw1, L0_ffn_sw3, L0_ffn_sw2, L0_ffn_ew1, L0_ffn_ew2)
    mod = (_silu(L1_c) @ L1_wmod).reshape(L1_c.shape[0], 6, 1, -1)
    sa, ca, ga, sb, cb, gb = (mod[:, 0], mod[:, 1], mod[:, 2], mod[:, 3], mod[:, 4], mod[:, 5])
    ga = (2 * (ga >= 0) - 1) * jnp.maximum(jnp.abs(ga), 0.25)
    gb = (2 * (gb >= 0) - 1) * jnp.maximum(jnp.abs(gb), 0.25)
    h = _layernorm(x, axis=-1) * (1 + ca) + sa
    x = x + ga * _L1_attn_ref(h, L1_attn_qkv_w, L1_attn_proj_w, L1_attn_proj_b, L1_attn_curvature)
    h = _layernorm(x, axis=-1) * (1 + cb) + sb
    x = x + gb * _L1_ffn_ref(h, L1_ffn_router_w, L1_ffn_bias, L1_ffn_gate_w, L1_ffn_up_w, L1_ffn_down_w, L1_ffn_sh_gate_w, L1_ffn_sh_up_w, L1_ffn_sh_down_w)
    return x

_drawn_inputs = setup_inputs


def setup_inputs(seed=0):
    import zlib

    import numpy as np

    out = dict(_drawn_inputs(seed))
    spreads = {'L0_attn_bk': (0.0, 0.8),
     'L0_attn_bv': (0.0, 0.771),
     'L0_attn_bf': (0.0, 0.1),
     'L0_ffn_router_bias': (0.0, 0.1),
     'L1_attn_proj_b': (0.0, 0.32),
     'L1_attn_curvature': (1.0, 0.6),
     'L1_ffn_bias': (0.0, 0.8)}
    factors = {'L0_attn_Wk': 8.0,
     'L0_attn_Wv': 8.0,
     'L0_attn_Wf': 6.627,
     'L1_ffn_router_w': 8.0,
     'L1_ffn_gate_w': 8.0,
     'L1_ffn_up_w': 8.0,
     'L1_ffn_down_w': 8.0,
     'L1_ffn_sh_gate_w': 8.0,
     'L1_ffn_sh_up_w': 8.0,
     'L1_ffn_sh_down_w': 8.0}
    for name, (base, spread) in spreads.items():
        noise = np.random.default_rng([zlib.crc32(name.encode()), seed]).standard_normal(out[name].shape)
        drawn = base * np.exp(spread * noise) if base else spread * noise
        out[name] = jnp.asarray(drawn.astype(out[name].dtype))
    for name, factor in factors.items():
        out[name] = (out[name] * factor).astype(out[name].dtype)
    return out
```

```python
from contextlib import ExitStack

import numpy as np

import concourse.bass as bass
from concourse import mybir

P = 128
B, N, D = 4, 1024, 128
NT = N // P
CH = 512
NC = N // CH
HEADS, HD = 16, 8
UNITS = HEADS // 4
SLOTS = 3
PAIRS = 3 * HD * 3
MAXROW = PAIRS
TROW = PAIRS + 3
K_MAX, K_HYP = PAIRS + 3, PAIRS + 3 + 9
LN_EPS = 1e-5
MASK = -1e38
ARG_GAP = float(np.float32(1.0 + 1e-07) - np.float32(1.0))
HYP_EPS = 1e-06
HYP_UNIT = 2
HEAD_ORDER = [0, 1, 2, 3, 4, 5, 10, 11, 6, 7, 8, 9, 12, 13, 14, 15]
N_SDPA, N_HYP = 6, 4

F32, BF16 = mybir.dt.float32, mybir.dt.bfloat16
ALU, ACT, AX = mybir.AluOpType, mybir.ActivationFunctionType, mybir.AxisListType

STEPS = []
for _c in range(NC):
    for _kb in range(4 * (_c + 1)):
        _q0 = max(_c * CH, _kb * P)
        STEPS.append((_c, _kb, _q0, (_c + 1) * CH - _q0, _kb >= 4 * _c))
NS = len(STEPS)
PIECES = []
for _qb in range(NT):
    for _half in range(_qb // 4 + 1):
        _w = min(CH, (_qb + 1) * P - _half * CH)
        PIECES.append((_qb, _half * CH, _w, 2 * _qb + _half))
NP_ = len(PIECES)
PER_STEP = 5


def pieces_at(s):
    every = [(j, p) for p in range(NP_) for j in range(4)]
    return every[PER_STEP * s:PER_STEP * (s + 1)]


OPS = 16 * 18
OPS_HYP = OPS + 16 * (1 + 18)


class Ffn:

    def __init__(self, name, experts, gated):
        self.name, self.experts, self.gated = name, experts, gated
        self.work = [("shared", f, c) for f in range(2) for c in range(NC)]
        self.work += [("expert", e, c) for e in range(experts) for c in range(NC)]


FFN = [Ffn("f0", 8, False), Ffn("f1", 16, True)]


def adaln_kernel(nc, ins, out):
    with ExitStack() as ctx:
        def sb(name, shape, dt=F32):
            return ctx.enter_context(nc.sbuf_tensor(name, shape, dt))

        def sem(name):
            s = ctx.enter_context(nc.semaphore(name))
            loop_sems.append(s)
            return s

        loop_sems = []
        ps = ctx.enter_context(nc.psum_tensor("ps", [P, 8, CH], F32))

        w = {}
        setup_loads = []

        def weight(name, shape, src, dt=F32):
            w[name] = sb("w_" + name, shape, dt)
            setup_loads.append((w[name][:], src))

        def blocks(a):
            return a.rearrange("(k p) m -> p k m", p=P)

        def experts(a):
            return a.rearrange("e p m -> p e m")

        weight("wk", [P, D], ins["Wk"])
        weight("wv", [P, 512], ins["Wv"])
        weight("wf", [P, 4, D], blocks(ins["Wf"]))
        weight("q", [P, D], ins["wq"])
        weight("qs", [P, D], ins["wqs"])
        weight("k", [P, D], ins["wk1"])
        weight("ks", [P, D], ins["wks"])
        weight("v", [P, D], ins["wv1"])
        weight("proj", [P, D], ins["proj"])
        for l, p in ((0, "L0"), (1, "L1")):
            e = FFN[l].experts
            weight(f"router{l}", [P, e], ins[p + "_router"])
            weight(f"rbias{l}", [P, e], ins[p + "_rbias"].rearrange("(a e) -> a e", a=1).broadcast_to([P, e]))
            weight(f"shg{l}", [P, 256], ins[p + "_shg"])
            weight(f"shu{l}", [P, 256], ins[p + "_shu"])
            weight(f"shd{l}", [P, 2, D], blocks(ins[p + "_shd"]))
            weight(f"gate{l}", [P, e, P], experts(ins[p + "_gate"]))
            if l:
                weight("up1", [P, e, P], experts(ins["L1_up"]))
            weight(f"down{l}", [P, e, D], experts(ins[p + "_down"]))
        weight("cols", [P, 16], ins["cols"])
        weight("tri", [P, 16, 16], ins["tri"].rearrange("(a e) f -> a e f", a=1).broadcast_to([P, 16, 16]))
        weight("ident", [P, P], ins["ident"])
        weight("heads8", [P, P], ins["heads8"])
        weight("maskt", [P, P], ins["maskt"])
        weight("c", [P, 2 * B], ins["c"])
        weight("rows", [96, 56], ins["rows"])
        cols = w["cols"]
        (C_BK, C_BF, C_PB, C_CURV, C_QS, C_COS, C_NOTCOS, C_BV, C_ONE) = (0, 1, 2, 3, 4, 5, 6, 8, 7)

        identb = sb("identb", [P, P], BF16)
        maskkq = sb("maskkq", [P, P], BF16)
        maskqk = sb("maskqk", [P, P], BF16)
        ones32 = sb("ones32", [P, 32])
        sel32 = sb("sel32", [96, 32, P], BF16)
        consts = sb("consts", [P, 8])
        mod = sb("mod", [P, 2, 6, B])
        modb = sb("modb", [P, 2, 6])
        hyp = sb("hyp", [P, 8])
        curvb = sb("curvb", [P, 4])

        xT = sb("xT", [P, N])
        hT = sb("hT", [P, N])
        xn = sb("xn", [P, NT, D])
        kT = sb("kT", [P, N])
        st = sb("st", [P, NT, 6])
        mv = sb("mv", [P, NT, 2])
        sd = sb("sd", [P, 2, NT])
        qop = sb("qop", [P, SLOTS, 4, N], BF16)
        kop = sb("kop", [P, SLOTS, 4, N], BF16)
        vt = sb("vt", [P, NT, HEADS * 32])
        pr = sb("pr", [P, 3, 4, CH])
        wb = sb("wb", [P, 2, 4, CH])
        osb = sb("osb", [P, 2, CH])
        rsb = sb("rsb", [P, 2, CH])
        on = sb("on", [P, UNITS, N])
        mx = sb("mx", [P, 2, 4, NT, 2])
        nm = sb("nm", [P, 2, 32])
        nr = sb("nr", [P, 3, 32])
        nmp = sb("nmp", [P, 96], BF16)
        mrow = sb("mrow", [96, P], BF16)
        rec = sb("rec", [P, 4, 4])
        wmod = pr[:].rearrange("p a b c -> p (a b c)")[:, 0:6 * D]
        cos, sin = on[:, 1, :], on[:, 2, :]
        lg = osb[:].rearrange("p a b -> p (a b)").rearrange("p (i t e) -> p i t e", i=8, t=NT)


        def selg(e):
            return wb[0:3 * e].rearrange("p a b c -> p (a b c)").bitcast(BF16)[:, 0:e * P].rearrange(
                "p (e n) -> p e n", n=P)

        gT = rsb[0:48, 0, :].bitcast(BF16)
        gp = rsb[:, 1, 0:NT * 24].bitcast(BF16).rearrange("p (t e) -> p t e", t=NT)
        parts = wb[:].rearrange("p a b c -> p (a b c)").bitcast(BF16)[:, 0:6 * N].rearrange(
            "p (s i n) -> p s i n", s=2, i=3)
        tparts = pr[:, 1:3].rearrange("p a b c -> p (a b c)").bitcast(BF16)[:, 0:6 * N].rearrange(
            "p (s i n) -> p s i n", s=2, i=3)
        tmp = xn[:].rearrange("p t d -> p (t d)")
        cmpa = pr[:, 0].rearrange("p a b -> p (a b)")
        cmpb = pr[:, 1].rearrange("p a b -> p (a b)")
        fa, fh, ft = pr[:, 2, 0:2], pr[:, 2, 2:4], pr[:, 1, 0:2]

        nbc = on
        wb_t = wb[:].rearrange("p a b c -> p (a b c)")[:, 3 * N:4 * N]
        rsb_t = osb[:].rearrange("p a b -> p (a b)")

        scratch = nc.dram_tensor("parts_scratch", [2, 2, 3, P, N], BF16, kind="Internal").ap()
        tscratch = nc.dram_tensor("time_scratch", [2, 3, 32, N], BF16, kind="Internal").ap()

        s_load = ctx.enter_context(nc.semaphore("s_load"))
        s_small = ctx.enter_context(nc.semaphore("s_small"))
        s_cast = ctx.enter_context(nc.semaphore("s_cast"))
        s_pool = ctx.enter_context(nc.semaphore("s_pool"))
        s_silu = ctx.enter_context(nc.semaphore("s_silu"))
        s_turn = ctx.enter_context(nc.semaphore("s_turn"))
        s_mm = ctx.enter_context(nc.semaphore("s_mm"))
        s_modc = ctx.enter_context(nc.semaphore("s_modc"))
        s_wmod = ctx.enter_context(nc.semaphore("s_wmod"))
        s_sdve = ctx.enter_context(nc.semaphore("s_sdve"))
        s_hyp = ctx.enter_context(nc.semaphore("s_hyp"))
        with nc.Block() as block:
            @block.sync
            def _(sp):
                for dst, src in setup_loads:
                    sp.dma_start(dst, src).then_inc(s_load, 16)
                sp.dma_start(curvb[:], ins["curv"].rearrange("(a e) -> a e", a=1).broadcast_to([P, 4])).then_inc(
                    s_small, 16)
                for l, name in ((0, "L0_wmod"), (1, "L1_wmod")):
                    if l:
                        sp.wait_ge(s_mm, 1)
                    sp.dma_start(wmod, ins[name]).then_inc(s_wmod, 16)

            @block.gpsimd
            def _(pool):
                nc.gpsimd.memset(ones32[:], 1.0)
                nc.gpsimd.memset(kop[:], 1.0)
                nc.gpsimd.memset(consts[:, 0:1], LN_EPS)
                nc.gpsimd.memset(consts[:, 2:3], HYP_EPS)
                nc.gpsimd.memset(consts[:, 1:2], 1.0).then_inc(s_pool, 1)
                pool.wait_ge(s_load, 16 * len(setup_loads))
                for e in range(32):
                    last = nc.gpsimd.tensor_copy(sel32[:, e, :], w["rows"][0:96, 24 + e:25 + e].broadcast_to([96, P]))
                last.then_inc(s_pool, 1)

            @block.scalar
            def _(act):
                act.wait_ge(s_load, 16 * len(setup_loads))
                nc.scalar.activation(w["c"][:], w["c"][:], ACT.Silu).then_inc(s_silu, 1)
                act.wait_ge(s_sdve, 1)
                nc.scalar.activation(hyp[:, 1:2], hyp[:, 0:1], ACT.Sqrt).then_inc(s_hyp, 1)
                act.wait_ge(s_small, 16)
                act.wait_ge(s_sdve, 2)
                nc.scalar.activation(hyp[:, 4:8], hyp[:, 4:8], ACT.Sqrt).then_inc(s_hyp, 1)

            @block.tensor
            def _(pe):
                pe.wait_ge(s_silu, 1)
                pe.wait_ge(s_load, 16 * len(setup_loads))
                pe.transpose(ps[:, 7, 0:P], w["maskt"][:], w["ident"][:]).then_inc(s_turn, 1)
                for l in range(2):
                    pe.wait_ge(s_wmod, 16 * (l + 1))
                    for j in range(6):
                        mm = pe.matmul(ps[:, l, B * j:B * j + B], wmod[:, j * D:(j + 1) * D],
                                       w["c"][:, l * B:(l + 1) * B], start=True, stop=True)
                    mm.then_inc(s_mm, 1)

            @block.vector
            def _(dve):
                chain = [0]

                def link(i):
                    chain[0] += 1
                    i.then_inc(s_modc, 1)
                    dve.wait_ge(s_modc, chain[0])

                dve.wait_ge(s_load, 16 * len(setup_loads))
                nc.vector.tensor_copy(identb[:], w["ident"][:])
                nc.vector.tensor_copy(maskkq[:], w["maskt"][:])
                nc.vector.reciprocal(hyp[:, 0:1], cols[:, C_CURV:C_CURV + 1]).then_inc(s_sdve, 1)
                dve.wait_ge(s_small, 16)
                nc.vector.reciprocal(hyp[:, 4:8], curvb[:]).then_inc(s_sdve, 1)
                dve.wait_ge(s_turn, 1)
                nc.vector.tensor_copy(maskqk[:], ps[:, 7, 0:P])
                for l in range(2):
                    dve.wait_ge(s_mm, l + 1)
                    m = mod[:, l].rearrange("p j b -> p (j b)")
                    link(nc.vector.tensor_copy(m, ps[:, l, 0:6 * B]))
                    for j in (1, 4):
                        link(nc.vector.tensor_scalar(mod[:, l, j], mod[:, l, j], 1.0, None, ALU.add))
                    for j in (2, 5):
                        g = mod[:, l, j]
                        link(nc.vector.tensor_scalar(nr[:, 0, 0:B], g, 0.0, 2.0, ALU.is_ge, ALU.mult))
                        link(nc.vector.tensor_scalar(nr[:, 1, 0:B], nr[:, 0, 0:B], -1.0, None, ALU.add))
                        link(nc.vector.tensor_scalar(nr[:, 2, 0:B], g, -1.0, None, ALU.mult))
                        link(nc.vector.tensor_tensor(nr[:, 0, 0:B], nr[:, 2, 0:B], g, ALU.max))
                        link(nc.vector.scalar_tensor_tensor(out=g, in0=nr[:, 0, 0:B], scalar=0.25,
                                                            in1=nr[:, 1, 0:B], op0=ALU.max, op1=ALU.mult))

        x_in, x_out, s_out_tok = sem("x_in"), sem("x_out"), sem("s_out_tok")
        x_tok, x_ready = sem("x_tok"), sem("x_ready")
        ln_tok = [sem(f"ln{n}_tok") for n in range(4)]
        ln_var = [sem(f"ln{n}_var") for n in range(4)]
        ln_std = [sem(f"ln{n}_std") for n in range(4)]
        ln_norm = [sem(f"ln{n}_norm") for n in range(4)]
        ln_back = [sem(f"ln{n}_back") for n in range(4)]
        h_ready = [sem(f"h{n}_ready") for n in range(4)]
        dve_chain, act_chain, pool_chain = sem("dve_chain"), sem("act_chain"), sem("pool_chain")
        mod_ready = sem("mod_ready")

        class Attn:

            def __init__(self, l):
                n = f"a{l}_"
                self.proj = sem(n + "proj")
                self.proj_used = sem(n + "proj_used")
                self.parts = sem(n + "parts")
                self.stored = [sem(n + f"stored{i}") for i in range(2)]
                self.v = sem(n + "v")
                self.vps = sem(n + "vps")
                self.ops = [sem(n + f"ops{u}") for u in range(UNITS)]
                self.maxrow = [sem(n + f"maxrow{u}") for u in range(UNITS)]
                self.piece = sem(n + "piece")
                self.reduced = sem(n + "reduced")
                self.nmp = sem(n + "nmp")
                self.mps = sem(n + "mps")
                self.mrow = sem(n + "mrow")
                self.scores = sem(n + "scores")
                self.exps = sem(n + "exps")
                self.pv = sem(n + "pv")
                self.o_out = sem(n + "o_out")
                self.s_out = sem(n + "s_out")
                self.rs = sem(n + "rs")
                self.on = sem(n + "on")
                self.gelu = sem(n + "gelu")
                self.final = sem(n + "final")
                self.x = sem(n + "x")

        at = [Attn(0), Attn(1)]
        v_ones, tables, sel_ready = sem("v_ones"), sem("tables"), sem("sel_ready")
        sq_ready, ss_ready, factors_used, norm_ready, t_parts, t_stored = (
            sem("sq_ready"), sem("ss_ready"), sem("factors_used"), sem("norm_ready"), sem("t_parts"), sem("t_stored"))
        ss_cl, hyp_inv_n = sem("ss_cl"), sem("hyp_inv_n")
        hyp_mx, hyp_s, hyp_bc, hyp_bcout = sem("hyp_mx"), sem("hyp_s"), sem("hyp_bc"), sem("hyp_bcout")
        hyp_z, hyp_r, hyp_zr, hyp_inv, hyp_sub = (
            sem("hyp_z"), sem("hyp_r"), sem("hyp_zr"), sem("hyp_inv"), sem("hyp_sub"))
        o_turn, y_tok, y_turn, y_T = sem("o_turn"), sem("y_tok"), sem("y_turn"), sem("y_T")

        class FfnSems:
            def __init__(self, l):
                n = f"f{l}_"
                self.logits, self.score = sem(n + "logits"), sem(n + "score")
                self.parts, self.gps, self.gates = sem(n + "parts"), sem(n + "gps"), sem(n + "gates")
                self.up, self.act, self.hid, self.down = (
                    sem(n + "up"), sem(n + "act"), sem(n + "hid"), sem(n + "down"))
                self.x = sem(n + "x")

        fs = [FfnSems(0), FfnSems(1)]

        x_for = [(x_ready, 2), (at[0].x, 2), (fs[0].x, 2), (at[1].x, 2)]
        HALVES = 2 * NS

        def chunk(t, c):
            return t[:, c * CH:(c + 1) * CH]

        def tensor_program(pe):
            def turn_tiles(src, bank, done, first=None):
                for t in range(NT):
                    if first:
                        first(t)
                    mm = pe.transpose(ps[:, bank + t // 4, (t % 4) * P:(t % 4 + 1) * P], src(t), w["ident"][:])
                    if t % 4 == 3:
                        mm.then_inc(done, 1)

            def layer_norm(n):
                pe.wait_ge(*x_for[n])
                turn_tiles(lambda t: xT[:, t * P:(t + 1) * P], 0, ln_tok[n])
                turn_tiles(lambda t: xn[:, t, :], 2, ln_back[n],
                           lambda t: pe.wait_ge(ln_norm[n], t + 1))

            def project(wt, c, bank, done):
                pe.matmul(ps[:, bank, :], wt, chunk(hT, c), start=True, stop=True).then_inc(done, 1)

            def attention(l):
                a = at[l]
                pe.wait_ge(h_ready[2 * l], NC)
                if l == 0:
                    for c in range(NC):
                        project(w["wk"][:], c, 4 + c, a.proj)
                    for t in range(NT):
                        if t >= 2:
                            pe.wait_ge(a.v, t - 1)
                        pe.matmul(ps[:, 6 + t % 2, :], hT[:, t * P:(t + 1) * P], w["wv"][:],
                                  start=True, stop=True).then_inc(a.vps, 1)
                else:
                    for i, (n0, n1) in enumerate((("q", "qs"), ("k", "ks"))):
                        for c in range(NC):
                            if i:
                                pe.wait_ge(a.proj_used, c + 1)
                            project(w[n0][:], c, 4 + c, a.proj)
                            project(w[n1][:], c, 6 + c, a.proj)
                    for i in range(2):
                        for c in range(NC):
                            pe.wait_ge(sq_ready, 2 * i + c + 1)
                            if i:
                                pe.wait_ge(ss_cl, c + 1)
                            pe.matmul(ps[:, c, :], w["heads8"][:], rsb[:, c, :], start=True,
                                      stop=True).then_inc(ss_ready, 1)
                    for t in range(NT):
                        if t == 0:
                            pe.wait_ge(a.proj_used, 4)
                        mm = pe.matmul(ps[:, 4 + t // 4, (t % 4) * P:(t % 4 + 1) * P], hT[:, t * P:(t + 1) * P],
                                       w["v"][:], start=True, stop=True)
                        if t % 4 == 3:
                            mm.then_inc(a.vps, 1)

                def has_max(u):
                    return l == 0 or u < 3

                def is_hyp(u):
                    return l == 1 and u == HYP_UNIT

                def piece(u, i, j, p):
                    qb, k0, wd, _ = PIECES[p]
                    g = 4 * NP_ * u + i
                    if i == 0:
                        pe.wait_ge(a.ops[u], OPS_HYP if is_hyp(u) else OPS)
                        if u == 0:
                            pe.wait_ge(a.v if l == 0 else a.proj_used, NT if l == 0 else 4)
                        else:
                            pe.wait_ge(a.mrow, u)
                    if g >= 2:
                        pe.wait_ge(a.reduced, g - 1)
                    k = K_HYP if is_hyp(u) else PAIRS
                    o = ps[:, 6 + g % 2, 0:wd]
                    diag = k0 + wd == (qb + 1) * P
                    mm = pe.matmul(o, qop[0:k, u % SLOTS, j, qb * P:(qb + 1) * P],
                                   kop[0:k, u % SLOTS, j, k0:k0 + wd], start=True, stop=not diag)
                    if diag:
                        mm = pe.matmul(o[:, wd - P:wd], identb[:], maskqk[:], start=False, stop=True)
                    mm.then_inc(a.piece, 1)

                def turn_max(u):
                    pe.wait_ge(a.nmp, u + 1)
                    pe.matmul(ps[0:96, 6, 0:P], nmp[:], identb[:], start=True, stop=True).then_inc(a.mps, 1)

                def spread_max():
                    pe.wait_ge(a.mrow, HYP_UNIT + 1)
                    for i, (j, c) in enumerate([(j, c) for j in range(4) for c in range(NC)]):
                        if i >= 2:
                            pe.wait_ge(hyp_bcout, i - 1)
                        for q in range(4):
                            mm = pe.matmul(ps[:, 6 + i % 2, q * P:(q + 1) * P], sel32[:, NT * j + 4 * c + q, :],
                                           mrow[:], start=True, stop=True)
                        mm.then_inc(hyp_bc, 1)

                def scores(u, s):
                    c, kb, q0, wd, diag = STEPS[s]
                    k = K_HYP if is_hyp(u) else (PAIRS if not has_max(u) else K_MAX)
                    o0 = q0 - c * CH
                    g = NS * u + s
                    for j in range(4):
                        if j % 2 == 0:
                            if g == 0:
                                pe.wait_ge(h_ready[2 * l], NC)
                                if l:
                                    pe.wait_ge(ss_cl, 4)
                            elif l and HYP_UNIT * NS <= g - 1 < (HYP_UNIT + 1) * NS:
                                pe.wait_ge(hyp_z, 2 * (g - 1 - HYP_UNIT * NS) + j // 2 + 1)
                            else:
                                pe.wait_ge(a.exps, 2 * (g - 1) + j // 2 + 1)
                        o = ps[:, j, o0:o0 + wd]
                        masked = diag and not is_hyp(u)
                        mm = pe.matmul(o, kop[0:k, u % SLOTS, j, kb * P:(kb + 1) * P],
                                       qop[0:k, u % SLOTS, j, q0:q0 + wd], start=True, stop=not masked)
                        if masked:
                            mm = pe.matmul(o[:, 0:P], identb[:], maskkq[:], start=False, stop=True)
                        if j % 2:
                            mm.then_inc(a.scores, 1)

                def values(u, s):
                    c, kb, q0, wd, _ = STEPS[s]
                    o0 = q0 - c * CH
                    g = NS * u + s
                    last = kb == 4 * c + 3
                    pe.wait_ge(a.exps, 2 * (g + 1))
                    if kb == 0:
                        if g == 0:
                            pe.wait_ge(a.v, NT if l == 0 else 2)
                        else:
                            pe.wait_ge(a.o_out, NC * u + c)
                            if l == 0:
                                pe.wait_ge(a.s_out, NC * u + c)
                    for j in range(4):
                        h = 4 * u + j
                        mm = pe.matmul(ps[32 * j:32 * j + 32, 4, o0:o0 + wd], vt[:, kb, 32 * h:32 * h + 32],
                                       pr[:, g % 3, j, o0:o0 + wd], start=kb == 0, stop=last,
                                       tile_position=(0, 32 * j))
                    if l == 0:
                        for j in range(4):
                            mm = pe.matmul(ps[32 * j:32 * j + 32, 5, o0:o0 + wd], ones32[:],
                                           pr[:, g % 3, j, o0:o0 + wd], start=kb == 0, stop=last,
                                           tile_position=(0, 32 * j))
                    mm.then_inc(a.pv, 1)

                def turn_outputs(u, c):
                    i = NC * u + c
                    pe.wait_ge(a.o_out, i + 1)
                    if i:
                        pe.wait_ge(y_tok, i)
                    for t in range(4):
                        mm = pe.transpose(ps[:, 5, t * P:(t + 1) * P], osb[:, i % 2, t * P:(t + 1) * P],
                                          w["ident"][:])
                    mm.then_inc(o_turn, 1)

                for i in range(4 * NP_):
                    piece(0, i, i % 4, i // 4)
                turn_max(0)
                for u in range(UNITS):
                    if is_hyp(u):
                        spread_max()
                    if has_max(u) and not is_hyp(u):
                        pe.wait_ge(a.maxrow[u], 48)
                    else:
                        pe.wait_ge(a.ops[u], OPS_HYP if is_hyp(u) else OPS)
                    more = u + 1 < UNITS and has_max(u + 1)
                    scores(u, 0)
                    for s in range(NS):
                        if s + 1 < NS:
                            scores(u, s + 1)
                        if more:
                            for n, (j, p) in enumerate(pieces_at(s)):
                                piece(u + 1, PER_STEP * s + n, j, p)
                            if s == NS - 2:
                                turn_max(u + 1)
                        values(u, s)
                        if l and s == 6:
                            turn_outputs(u, 0)
                        if l and s == 2 and u:
                            turn_outputs(u - 1, 1)
                if l:
                    turn_outputs(UNITS - 1, 1)
                    for t in range(NT):
                        pe.wait_ge(y_tok, 7 if t < 4 else 8)
                        if t == 0:
                            pe.wait_ge(a.exps, HALVES * UNITS)
                        mm = pe.transpose(ps[:, t // 4, (t % 4) * P:(t % 4 + 1) * P], kT[:, t * P:(t + 1) * P],
                                          w["ident"][:])
                        if t % 4 == 3:
                            mm.then_inc(y_turn, 1)
                    for c in range(NC):
                        pe.wait_ge(y_T, c + 1)
                        pe.matmul(ps[:, 2 + c, :], w["proj"][:], chunk(hT, c), start=True,
                                  stop=True).then_inc(a.final, 1)
                else:
                    pe.wait_ge(a.exps, HALVES * UNITS)
                    for c in range(NC):
                        for u in range(UNITS):
                            if c == 0:
                                pe.wait_ge(a.gelu, u + 1)
                            mm = pe.matmul(ps[:, c, :], w["wf"][:, u, :], on[:, u, c * CH:(c + 1) * CH],
                                           start=u == 0, stop=u == UNITS - 1)
                        mm.then_inc(a.final, 1)

            def ffn(l):
                f, g = FFN[l], fs[l]
                E = f.experts
                pe.wait_ge(h_ready[2 * l + 1], NC)
                for t in range(NT):
                    mm = pe.matmul(ps[:, 7, t * E:(t + 1) * E], hT[:, t * P:(t + 1) * P], w[f"router{l}"][:],
                                   start=True, stop=True)
                mm.then_inc(g.logits, 1)

                def gates():
                    pe.wait_ge(g.parts, 1)
                    for t in range(NT):
                        mm = pe.matmul(ps[0:3 * E, 6 + t // 4, (t % 4) * P:(t % 4 + 1) * P], gp[:, t, 0:3 * E],
                                       identb[:], start=True, stop=True)
                    mm.then_inc(g.gps, 1)
                    pe.wait_ge(g.gates, 1)
                    pe.wait_ge(sel_ready, l + 1)

                def up(i):
                    kind, e, c = f.work[i]
                    if i >= 2:
                        pe.wait_ge(g.hid, i - 1)
                    h = chunk(hT, c)
                    if kind == "shared":
                        pe.matmul(ps[:, 2 + i % 2, :], w[f"shg{l}"][:, e * P:(e + 1) * P], h, start=True, stop=True)
                        mm = pe.matmul(ps[:, 4 + i % 2, :], w[f"shu{l}"][:, e * P:(e + 1) * P], h,
                                       start=True, stop=True)
                    else:
                        pe.matmul(ps[:, 2 + i % 2, :], w[f"gate{l}"][:, e, :], h, start=True, stop=True)
                        if f.gated:
                            pe.matmul(ps[:, 4 + i % 2, :], w["up1"][:, e, :], h, start=True, stop=True)
                        mm = pe.matmul(ps[:, 6 + i % 2, :], selg(E)[:, e, :], chunk(gT, c)[0:3 * E],
                                       start=True, stop=True)
                    mm.then_inc(g.up, 1)

                def down(i):
                    kind, e, c = f.work[i]
                    pe.wait_ge(g.hid, i + 1)
                    wt = w[f"shd{l}"][:, e, :] if kind == "shared" else w[f"down{l}"][:, e, :]
                    pe.matmul(ps[:, c, :], wt, fh[:, i % 2, :], start=i < NC,
                              stop=i >= len(f.work) - NC).then_inc(g.down, 1)

                up(0)
                up(1)
                for i in range(len(f.work)):
                    down(i)
                    if i + 2 < len(f.work):
                        if i + 2 == 2 * NC:
                            gates()
                        up(i + 2)

            pe.wait_ge(x_in, 16)
            turn_tiles(lambda t: xn[:, t, :], 0, x_tok)
            for l in range(2):
                layer_norm(2 * l)
                attention(l)
                layer_norm(2 * l + 1)
                ffn(l)
            pe.wait_ge(fs[1].x, 2)
            turn_tiles(lambda t: xT[:, t * P:(t + 1) * P], 2, s_out_tok)

        def scalar_program(act):
            chain = [0]

            def link(i):
                chain[0] += 1
                i.then_inc(act_chain, 1)
                act.wait_ge(act_chain, chain[0])

            def layer_norm(n):
                l, j = n // 2, 3 * (n % 2)
                act.wait_ge(ln_var[n], 1)
                nc.scalar.activation(sd[:, 0, :], mv[:, :, 1], ACT.Sqrt, bias=consts[:, 0:1]).then_inc(ln_std[n], 1)
                if n == 0:
                    act.wait_ge(mod_ready, 1)
                for c in range(NC):
                    act.wait_ge(ln_back[n], c + 1)
                    nc.scalar.activation(chunk(hT, c), ps[:, 2 + c, :], ACT.Identity, scale=modb[:, l, j + 1:j + 2],
                                         bias=modb[:, l, j:j + 1]).then_inc(h_ready[n], 1)

            def prepare(l):
                a = at[l]
                if l == 0:
                    for c in range(NC):
                        act.wait_ge(a.proj, c + 1)
                        nc.scalar.activation(chunk(kT, c), ps[:, 4 + c, :], ACT.Identity,
                                             bias=cols[:, C_BK:C_BK + 1]).then_inc(a.proj_used, 1)
                    return
                for i, src in enumerate((on[:, 0, :], kT[:])):
                    for c in range(NC):
                        act.wait_ge(norm_ready, 2 * i + c + 1)
                        if i:
                            act.wait_ge(ss_ready, c + 1)
                        nc.scalar.activation(rsb[:, c, :], chunk(src, c), ACT.Square).then_inc(sq_ready, 1)
                    for c in range(NC):
                        act.wait_ge(ss_cl, 2 * i + c + 1)
                        r, t = chunk(on[:, 2, :], c), chunk(on[64:96, 3, :], c)
                        if i:
                            act.wait_ge(factors_used, 1)
                        nc.scalar.activation(r, chunk(on[:, 1, :], c), ACT.Ln)
                        link(nc.scalar.activation(t, chunk(wb_t[64:96], c), ACT.Ln))
                        nc.scalar.activation(r, r, ACT.Exp, scale=-0.5)
                        nc.scalar.activation(t, t, ACT.Exp, scale=-0.5).then_inc(hyp_inv_n, 1)

            def attention(l):
                a = at[l]

                def is_hyp(u):
                    return l == 1 and u == HYP_UNIT

                def sums_out(u, c):
                    i = NC * u + c
                    act.wait_ge(a.pv, NS * u + 4 + 8 * c)
                    if i >= 2:
                        act.wait_ge(a.on, i - 1)
                    nc.scalar.activation(rsb[:, i % 2, :], ps[:, 5, :], ACT.Ln).then_inc(a.s_out, 1)
                    act.wait_ge(a.s_out, i + 1)
                    nc.scalar.activation(rsb[:, i % 2, :], rsb[:, i % 2, :], ACT.Exp, scale=-1.0).then_inc(a.rs, 1)

                def hyp_max():
                    z, x, y = nr[:, 0, :], nr[:, 1, :], nr[:, 2, :]
                    act.wait_ge(hyp_mx, 1)
                    link(nc.scalar.activation(z, z, ACT.Ln))
                    nc.scalar.activation(z, z, ACT.Exp, scale=0.5).then_inc(hyp_s, 1)
                    act.wait_ge(hyp_mx, 2)
                    link(nc.scalar.activation(z, z, ACT.Ln, bias=consts[:, 1:2]))
                    for j in range(4):
                        ins_ = nc.scalar.activation(z[:, NT * j:NT * (j + 1)], z[:, NT * j:NT * (j + 1)], ACT.Ln,
                                                    scale=hyp[:, 4 + j:5 + j], bias=consts[:, 2:3])
                    link(ins_)
                    nc.scalar.activation(z, z, ACT.Exp, scale=-1.0).then_inc(hyp_s, 1)

                def hyp_step(s):
                    c, kb, q0, wd, _ = STEPS[s]
                    o0 = q0 - c * CH
                    g = NS * HYP_UNIT + s
                    z = pr[:, g % 3, :, o0:o0 + wd]
                    act.wait_ge(hyp_z, 2 * s + 2)
                    act.wait_ge(hyp_r, s + 1)
                    link(nc.scalar.activation(z, z, ACT.Ln))
                    nc.scalar.activation(z, z, ACT.Exp, scale=0.5).then_inc(hyp_zr, 1)
                    act.wait_ge(hyp_inv, s + 1)
                    link(nc.scalar.activation(z, z, ACT.Ln, bias=consts[:, 1:2]))
                    for j in range(4):
                        ins_ = nc.scalar.activation(z[:, j], z[:, j], ACT.Ln, scale=hyp[:, 4 + j:5 + j],
                                                    bias=consts[:, 2:3])
                    link(ins_)
                    nc.scalar.activation(z, z, ACT.Exp, scale=-1.0).then_inc(hyp_zr, 1)
                    act.wait_ge(hyp_sub, s + 1)
                    nc.scalar.activation(z, z, ACT.Exp).then_inc(a.exps, 2)

                for u in range(UNITS):
                    if is_hyp(u):
                        hyp_max()
                    for s in range(NS):
                        g = NS * u + s
                        c, kb, q0, wd, _ = STEPS[s]
                        o0 = q0 - c * CH
                        if is_hyp(u):
                            hyp_step(s)
                            continue
                        for half in range(2):
                            act.wait_ge(a.scores, 2 * g + half + 1)
                            if g >= 3:
                                act.wait_ge(a.pv, g - 2)
                            elif l == 1 and half == 0 and g == 0:
                                act.wait_ge(t_stored, 32)
                            j = 2 * half
                            nc.scalar.activation(pr[:, g % 3, j:j + 2, o0:o0 + wd], ps[:, j:j + 2, o0:o0 + wd],
                                                 ACT.Exp).then_inc(a.exps, 1)
                        if l == 0:
                            if s == 4:
                                sums_out(u, 0)
                            if s == 0 and u:
                                sums_out(u - 1, 1)
                if l == 0:
                    sums_out(UNITS - 1, 1)
                    for u in range(UNITS):
                        act.wait_ge(a.on, NC * (u + 1))
                        nc.scalar.activation(on[:, u, :], on[:, u, :], ACT.Gelu,
                                             bias=cols[:, C_BV + u:C_BV + u + 1]).then_inc(a.gelu, 1)
                else:
                    for c in range(NC):
                        act.wait_ge(y_turn, c + 1)
                        nc.scalar.copy(chunk(hT, c), ps[:, c, :]).then_inc(y_T, 1)

            def ffn(l):
                f, g = FFN[l], fs[l]
                E = f.experts
                act.wait_ge(g.logits, 1)
                nc.scalar.activation(lg[:, 0, :, 0:E], ps[:, 7, 0:NT * E].rearrange("p (t e) -> p t e", e=E),
                                     ACT.Sigmoid).then_inc(g.score, 1)
                for i, (kind, e, c) in enumerate(f.work):
                    if i == 2 * NC:
                        act.wait_ge(g.gps, 1)
                        nc.scalar.copy(gT[0:3 * E, :].rearrange("p (a b) -> p a b", a=2),
                                       ps[0:3 * E, 6:8, :]).then_inc(g.gates, 1)
                    act.wait_ge(g.up, i + 1)
                    if i >= 2:
                        act.wait_ge(g.hid, i - 1)
                    fn = ACT.Silu if l or kind == "shared" else ACT.Gelu
                    nc.scalar.activation(fa[:, i % 2, :], ps[:, 2 + i % 2, :], fn).then_inc(g.act, 1)

            for l in range(2):
                layer_norm(2 * l)
                prepare(l)
                attention(l)
                layer_norm(2 * l + 1)
                ffn(l)

        def vector_program(dve):
            chain = [0]

            def link(i):
                chain[0] += 1
                i.then_inc(dve_chain, 1)
                dve.wait_ge(dve_chain, chain[0])

            def layer_norm(n):
                def tile(t):
                    return ps[:, t // 4, (t % 4) * P:(t % 4 + 1) * P]

                for t in range(NT):
                    if t % 4 == 0:
                        dve.wait_ge(ln_tok[n], t // 4 + 1)
                    ins_ = nc.vector.bn_stats(st[:, t, :], tile(t))
                link(ins_)
                for t in range(NT):
                    ins_ = nc.vector.bn_aggr(mv[:, t, :], st[:, t, :])
                ins_.then_inc(ln_var[n], 1)
                dve.wait_ge(ln_std[n], 1)
                link(nc.vector.reciprocal(sd[:, 1, :], sd[:, 0, :]))
                for t in range(NT):
                    nc.vector.tensor_scalar(xn[:, t, :], tile(t), mv[:, t, 0:1], sd[:, 1, t:t + 1], ALU.subtract,
                                            ALU.mult).then_inc(ln_norm[n], 1)

            def split(src, dst, r):
                link(nc.vector.tensor_copy(dst(0), src))
                link(nc.vector.tensor_tensor(r, src, dst(0), ALU.subtract))
                link(nc.vector.tensor_copy(dst(1), r))
                return nc.vector.tensor_tensor(dst(2), r, dst(1), ALU.subtract)

            def prepare(l):
                a = at[l]
                if l == 0:
                    dve.wait_ge(h_ready[0], NC)
                    split(hT[:], lambda i: parts[:, 0, i, :], tmp).then_inc(a.parts, 1)
                    dve.wait_ge(a.parts, 1)
                    dve.wait_ge(a.proj_used, NC)
                    split(kT[:], lambda i: parts[:, 1, i, :], tmp).then_inc(a.parts, 1)
                    for t in range(NT):
                        dve.wait_ge(a.vps, t + 1)
                        nc.vector.tensor_copy(vt[:, t, :], ps[:, 6 + t % 2, :]).then_inc(a.v, 1)
                    return
                q0, q1 = on[:, 0, :], on[:, 1, :]
                dsts = (q0, kT[:])
                dve.wait_ge(tables, 32)
                for i in range(2):
                    for c in range(NC):
                        dve.wait_ge(a.proj, 4 * i + 2 * c + 2)
                        nc.vector.tensor_tensor(chunk(dsts[i], c), ps[:, 4 + c, :], chunk(cos, c), ALU.mult)
                        ins_ = nc.vector.tensor_tensor(chunk(tmp, c), ps[:, 6 + c, :], chunk(sin, c), ALU.mult)
                        ins_.then_inc(a.proj_used, 1)
                        dve.wait_ge(a.proj_used, 2 * i + c + 1)
                        nc.vector.tensor_tensor(chunk(dsts[i], c), chunk(dsts[i], c), chunk(tmp, c),
                                                ALU.add).then_inc(norm_ready, 1)
                for i in range(2):
                    for c in range(NC):
                        dve.wait_ge(ss_ready, 2 * i + c + 1)
                        link(nc.vector.tensor_scalar(chunk(q1, c), ps[:, c, :], 1e-24, None, ALU.max))
                        nc.vector.tensor_scalar(chunk(wb_t[64:96], c), ps[64:96, c, :], hyp[64:96, 0:1], None,
                                                ALU.add).then_inc(ss_cl, 1)
                    dve.wait_ge(hyp_inv_n, 2 * i + 2)
                    A, R, T, U = wb_t[64:96], on[64:96, 3, :], rsb_t[64:96], tmp[64:96]
                    link(nc.vector.tensor_tensor(T, A, R, ALU.mult))
                    link(nc.vector.tensor_tensor(U, T, T, ALU.mult))
                    link(nc.vector.tensor_tensor(U, A, U, ALU.subtract))
                    link(nc.vector.scalar_tensor_tensor(out=U, in0=U, scalar=0.5, in1=R, op0=ALU.mult,
                                                        op1=ALU.mult))
                    link(nc.vector.tensor_tensor(T, T, U, ALU.add))
                    if i == 0:
                        link(nc.vector.tensor_scalar(T, T, cols[64:96, C_CURV:C_CURV + 1], -1.0, ALU.mult,
                                                     ALU.mult))
                    link(split(T, lambda k: tparts[64:96, i, k, :], U))
                    F = on[:, 2, :]
                    link(nc.vector.tensor_scalar(F, F, cols[:, C_COS:C_COS + 1], cols[:, C_NOTCOS:C_NOTCOS + 1],
                                                 ALU.mult, ALU.add))
                    if i == 0:
                        ins_ = nc.vector.scalar_tensor_tensor(out=q0, in0=q0, scalar=cols[:, C_QS:C_QS + 1], in1=F,
                                                              op0=ALU.mult, op1=ALU.mult)
                    else:
                        ins_ = nc.vector.tensor_tensor(kT[:], kT[:], F, ALU.mult)
                    ins_.then_inc(factors_used, 1)
                    dve.wait_ge(factors_used, i + 1)
                    split(dsts[i], lambda k: parts[:, i, k, :], tmp).then_inc(a.parts, 1)
                    dve.wait_ge(a.parts, i + 1)
                dve.wait_ge(v_ones, 1)
                for c in range(NC):
                    dve.wait_ge(a.vps, c + 1)
                    for t in range(4):
                        ins_ = nc.vector.tensor_copy(
                            vt[:, 4 * c + t, :].rearrange("p (h e) -> p h e", e=32)[:, :, 0:HD],
                            ps[:, 4 + c, t * P:(t + 1) * P].rearrange("p (h e) -> p h e", e=HD))
                    ins_.then_inc(a.v, 1)

            def attention(l):
                a = at[l]

                def is_hyp(u):
                    return l == 1 and u == HYP_UNIT

                def reduce(u, i, j, p):
                    qb, k0, wd, col = PIECES[p]
                    g = 4 * NP_ * u + i
                    dve.wait_ge(a.piece, g + 1)
                    nc.vector.tensor_reduce(mx[:, u % 2, j, qb, col % 2:col % 2 + 1], ps[:, 6 + g % 2, 0:wd], AX.X,
                                            ALU.max, negate=True).then_inc(a.reduced, 1)

                def maxima(u):
                    m = nm[:, u % 2, :]
                    m3 = m.rearrange("p (j q) -> p j q", q=NT)
                    dve.wait_ge(a.reduced, 4 * NP_ * (u + 1))
                    nc.vector.tensor_copy(m3[:, :, 0:4], mx[:, u % 2, :, 0:4, 0])
                    link(nc.vector.tensor_tensor(m3[:, :, 4:NT], mx[:, u % 2, :, 4:NT, 0], mx[:, u % 2, :, 4:NT, 1],
                                                 ALU.min))
                    if is_hyp(u):
                        x, y = nr[:, 1, :], nr[:, 2, :]
                        link(nc.vector.tensor_scalar(x, m, ARG_GAP, None, ALU.max))
                        nc.vector.scalar_tensor_tensor(out=nr[:, 0, :], in0=x, scalar=2.0, in1=x, op0=ALU.add,
                                                       op1=ALU.mult).then_inc(hyp_mx, 1)
                        dve.wait_ge(hyp_s, 1)
                        nc.vector.tensor_tensor(nr[:, 0, :], nr[:, 0, :], x, ALU.add).then_inc(hyp_mx, 1)
                        dve.wait_ge(hyp_s, 2)
                        link(nc.vector.tensor_scalar(m, nr[:, 0, :], -1.0, None, ALU.mult))
                    if u:
                        dve.wait_ge(a.mps, u)
                    split(m, lambda k: nmp[:, 32 * k:32 * k + 32], nr[:, 1, :]).then_inc(a.nmp, 1)
                    dve.wait_ge(a.mps, u + 1)
                    if u:
                        dve.wait_ge(a.maxrow[u - 1], 48)
                    nc.vector.tensor_copy(mrow[:], ps[0:96, 6, 0:P]).then_inc(a.mrow, 1)

                def outputs_out(u, c):
                    i = NC * u + c
                    dve.wait_ge(a.pv, NS * u + 4 + 8 * c)
                    if i >= 2:
                        dve.wait_ge(o_turn if l else a.on, i - 1)
                    nc.vector.tensor_copy(osb[:, i % 2, :], ps[:, 4, :]).then_inc(a.o_out, 1)

                def to_tokens(u, c):
                    i = NC * u + c
                    dve.wait_ge(o_turn, i + 1)
                    o = ps[:, 5, :].rearrange("p (t j e) -> p t j e", t=4, j=4)
                    link(nc.vector.reciprocal(rec[:], o[:, :, :, HD]))
                    y = kT[:].rearrange("p (t u j e) -> p t u j e", t=NT, u=UNITS, j=4)
                    for j in range(4):
                        ins_ = nc.vector.tensor_tensor(y[:, 4 * c:4 * c + 4, u, j, :], o[:, :, j, 0:HD],
                                                       rec[:, :, j:j + 1].broadcast_to([P, 4, HD]), ALU.mult)
                    ins_.then_inc(y_tok, 1)

                def hyp_step(s):
                    c, kb, q0, wd, diag = STEPS[s]
                    o0 = q0 - c * CH
                    g = NS * HYP_UNIT + s
                    z = pr[:, g % 3, :, o0:o0 + wd]
                    x = wb[:, s % 2, :, o0:o0 + wd]
                    if g >= 3:
                        dve.wait_ge(a.pv, g - 2)
                    for half in range(2):
                        dve.wait_ge(a.scores, 2 * g + half + 1)
                        j = 2 * half
                        nc.vector.tensor_scalar(x[:, j:j + 2], ps[:, j:j + 2, o0:o0 + wd], -1.0, ARG_GAP, ALU.mult,
                                                ALU.max).then_inc(hyp_z, 1)
                    dve.wait_ge(hyp_z, 2 * s + 2)
                    nc.vector.scalar_tensor_tensor(out=z, in0=x, scalar=2.0, in1=x, op0=ALU.add,
                                                   op1=ALU.mult).then_inc(hyp_r, 1)

                def hyp_shift(s):
                    c, kb, q0, wd, diag = STEPS[s]
                    o0 = q0 - c * CH
                    g = NS * HYP_UNIT + s
                    z = pr[:, g % 3, :, o0:o0 + wd]
                    dve.wait_ge(hyp_zr, 2 * s + 2)
                    ins_ = nc.vector.tensor_tensor(z, z, nbc[:, :, q0:q0 + wd], ALU.add)
                    if diag:
                        link(ins_)
                        for j in range(4):
                            ins_ = nc.vector.tensor_tensor(z[:, j, 0:P], z[:, j, 0:P], w["maskt"][:], ALU.add)
                    ins_.then_inc(hyp_sub, 1)

                def has_max(u):
                    return l == 0 or u < 3

                for i in range(4 * NP_):
                    reduce(0, i, i % 4, i // 4)
                maxima(0)
                for u in range(UNITS):
                    more = u + 1 < UNITS and has_max(u + 1)
                    if is_hyp(u):
                        for i, (j, c) in enumerate([(j, c) for j in range(4) for c in range(NC)]):
                            dve.wait_ge(hyp_bc, i + 1)
                            nc.vector.tensor_copy(nbc[:, j, c * CH:(c + 1) * CH],
                                                  ps[:, 6 + i % 2, :]).then_inc(hyp_bcout, 1)
                        dve.wait_ge(hyp_bcout, 8)
                        hyp_step(0)
                    for s in range(NS):
                        if s == 0 and u:
                            outputs_out(u - 1, 1)
                        if s == 4:
                            outputs_out(u, 0)
                        if is_hyp(u):
                            if s + 1 < NS:
                                hyp_step(s + 1)
                            hyp_shift(s)
                        if more:
                            for n, (j, p) in enumerate(pieces_at(s)):
                                reduce(u + 1, PER_STEP * s + n, j, p)
                            if s == NS - 3:
                                maxima(u + 1)
                        if l and s == 3 and u:
                            to_tokens(u - 1, 1)
                        if l and s == 7:
                            to_tokens(u, 0)
                outputs_out(UNITS - 1, 1)
                if l:
                    to_tokens(UNITS - 1, 1)
                j = 2
                for c in range(NC):
                    dve.wait_ge(a.final, c + 1)
                    y, res = ps[:, (2 if l else 0) + c, :], chunk(xT, c)
                    if l == 0:
                        link(nc.vector.scalar_tensor_tensor(out=chunk(tmp, c), in0=y, scalar=cols[:, C_BF:C_BF + 1],
                                                            in1=chunk(hT, c), op0=ALU.add, op1=ALU.add))
                        nc.vector.scalar_tensor_tensor(out=res, in0=chunk(tmp, c), scalar=modb[:, l, j:j + 1],
                                                       in1=res, op0=ALU.mult, op1=ALU.add).then_inc(a.x, 1)
                    else:
                        link(nc.vector.tensor_scalar(chunk(tmp, c), y, cols[:, C_PB:C_PB + 1], None, ALU.add))
                        nc.vector.scalar_tensor_tensor(out=res, in0=chunk(tmp, c), scalar=modb[:, l, j:j + 1],
                                                       in1=res, op0=ALU.mult, op1=ALU.add).then_inc(a.x, 1)

            def top(dst, src, T, E, k):
                a4 = cmpa[:, 0:T * E * E].rearrange("p (t e f) -> p t e f", t=T, e=E)
                b4 = cmpb[:, 0:T * E * E].rearrange("p (t e f) -> p t e f", t=T, e=E)
                other = src.unsqueeze(2).broadcast_to([P, T, E, E])
                own = src.unsqueeze(3).broadcast_to([P, T, E, E])
                nc.vector.tensor_tensor(a4, other, own, ALU.is_gt)
                link(nc.vector.tensor_tensor(b4, other, own, ALU.is_equal))
                link(nc.vector.tensor_tensor(b4, b4, w["tri"][:, 0:E, 0:E].unsqueeze(1).broadcast_to([P, T, E, E]),
                                             ALU.mult))
                link(nc.vector.tensor_tensor(a4, a4, b4, ALU.add))
                link(nc.vector.tensor_reduce(dst, a4, AX.X, ALU.add))
                link(nc.vector.tensor_scalar(dst, dst, k - 0.5, None, ALU.is_lt))

            def route(l):
                f, g = FFN[l], fs[l]
                E = f.experts
                s, sb_, m, t0, t1 = (lg[:, i, :, 0:E] for i in range(5))
                den, rc, ok = lg[:, 5, :, 0:1], lg[:, 6, :, 0:1], lg[:, 7, :, 0:1]

                def wide(x, e=E):
                    return x.broadcast_to([P, NT, e])

                dve.wait_ge(g.score, 1)
                link(nc.vector.tensor_tensor(sb_, s, w[f"rbias{l}"][:].unsqueeze(1).broadcast_to([P, NT, E]),
                                             ALU.add))
                if l == 0:
                    top(m, sb_, NT, E, 2)
                else:
                    sg = lg[:, 1].rearrange("p t (g e) -> p (t g) e", e=4)
                    mg = lg[:, 2].rearrange("p t (g e) -> p (t g) e", e=4)
                    top(mg, sg, 4 * NT, 4, 2)
                    link(nc.vector.tensor_tensor(mg, mg, sg, ALU.mult))
                    gs = lg[:, 3, :, 0:4]
                    link(nc.vector.tensor_reduce(gs, lg[:, 2].rearrange("p t (g e) -> p t g e", e=4), AX.X, ALU.add))
                    gm = lg[:, 4, :, 0:4]
                    top(gm, gs, NT, 4, 2)
                    link(nc.vector.tensor_scalar(gs, gm, -1.0, None, ALU.add))
                    s4 = lg[:, 1].rearrange("p t (g e) -> p t g e", e=4)
                    link(nc.vector.tensor_tensor(s4, s4, gm.unsqueeze(3).broadcast_to([P, NT, 4, 4]), ALU.mult))
                    link(nc.vector.tensor_tensor(s4, s4, gs.unsqueeze(3).broadcast_to([P, NT, 4, 4]), ALU.add))
                    top(m, sb_, NT, E, 4)
                link(nc.vector.tensor_tensor(t0, s, m, ALU.mult))
                link(nc.vector.tensor_reduce(den, t0, AX.X, ALU.add))
                link(nc.vector.tensor_scalar(rc, den, 1e-20 if l else 1e-09, None, ALU.add))
                link(nc.vector.reciprocal(rc, rc))
                if l:
                    link(nc.vector.tensor_tensor(t0, t0, wide(rc), ALU.mult))
                    link(nc.vector.tensor_scalar(t0, t0, 2.5, None, ALU.mult))
                else:
                    link(nc.vector.tensor_scalar(ok, den, 1e-09, None, ALU.is_gt))
                    link(nc.vector.tensor_tensor(rc, rc, ok, ALU.mult))
                    link(nc.vector.tensor_tensor(t0, t0, wide(rc), ALU.mult))
                    link(nc.vector.tensor_scalar(ok, ok, -0.5, 0.5, ALU.mult, ALU.add))
                    link(nc.vector.tensor_tensor(m, m, wide(ok), ALU.mult))
                    link(nc.vector.tensor_tensor(t0, t0, m, ALU.add))
                split(t0, lambda k: gp[:, :, k * E:(k + 1) * E], t1).then_inc(g.parts, 1)

            def ffn(l):
                f, g = FFN[l], fs[l]
                for i, (kind, e, c) in enumerate(f.work):
                    if i == 2 * NC:
                        route(l)
                    dve.wait_ge(g.act, i + 1)
                    if i >= 2:
                        dve.wait_ge(g.down, i - 1)
                    hid, a_ = fh[:, i % 2, :], fa[:, i % 2, :]
                    if kind == "shared":
                        nc.vector.tensor_tensor(hid, a_, ps[:, 4 + i % 2, :], ALU.mult).then_inc(g.hid, 1)
                    elif not f.gated:
                        nc.vector.tensor_tensor(hid, a_, ps[:, 6 + i % 2, :], ALU.mult).then_inc(g.hid, 1)
                    else:
                        link(nc.vector.tensor_tensor(ft[:, i % 2, :], a_, ps[:, 4 + i % 2, :], ALU.mult))
                        nc.vector.tensor_tensor(hid, ft[:, i % 2, :], ps[:, 6 + i % 2, :], ALU.mult).then_inc(
                            g.hid, 1)
                for c in range(NC):
                    dve.wait_ge(g.down, len(f.work) - NC + c + 1)
                    nc.vector.scalar_tensor_tensor(out=chunk(xT, c), in0=ps[:, c, :], scalar=modb[:, l, 5:6],
                                                   in1=chunk(xT, c), op0=ALU.mult, op1=ALU.add).then_inc(g.x, 1)

            for c in range(NC):
                dve.wait_ge(x_tok, c + 1)
                nc.vector.tensor_copy(chunk(xT, c), ps[:, c, :]).then_inc(x_ready, 1)
            for l in range(2):
                layer_norm(2 * l)
                prepare(l)
                attention(l)
                layer_norm(2 * l + 1)
                ffn(l)
            for c in range(NC):
                dve.wait_ge(s_out_tok, c + 1)
                nc.vector.tensor_copy(xn[:, 4 * c:4 * c + 4, :].rearrange("p t d -> p (t d)"),
                                      ps[:, 2 + c, :]).then_inc(x_out, 1)

        def pool_program(pool):
            def select_gates(l):
                pool.wait_ge(at[l].x, NC)
                e, at0 = FFN[l].experts, 8 * l
                for i in range(e):
                    ins_ = nc.gpsimd.tensor_copy(selg(e)[:, i, :],
                                                 w["rows"][0:3 * e, at0 + i:at0 + i + 1].broadcast_to([3 * e, P]))
                ins_.then_inc(sel_ready, 1)

            for i in range(NC * UNITS):
                u, c = i // NC, i % NC
                pool.wait_ge(at[0].o_out, i + 1)
                pool.wait_ge(at[0].rs, i + 1)
                nc.gpsimd.tensor_tensor(on[:, u, c * CH:(c + 1) * CH], osb[:, i % 2, :], rsb[:, i % 2, :],
                                        ALU.mult).then_inc(at[0].on, 1)
            pool.wait_ge(at[0].pv, NS * UNITS)
            nc.gpsimd.memset(vt[:], 1.0).then_inc(v_ones, 1)
            select_gates(0)
            for s in range(NS):
                c, kb, q0, wd, _ = STEPS[s]
                o0 = q0 - c * CH
                g = NS * HYP_UNIT + s
                z = pr[:, g % 3, :, o0:o0 + wd]
                pool.wait_ge(hyp_zr, 2 * s + 1)
                nc.gpsimd.tensor_tensor(z, z, wb[:, s % 2, :, o0:o0 + wd], ALU.add).then_inc(hyp_inv, 1)
            select_gates(1)

        def sync_program(sp, b):
            sp.dma_start(xn[:], ins["x"][b].rearrange("(t p) d -> p t d", p=P)).then_inc(x_in, 16)

            def load_unit(l, u):
                a = at[l]
                for side, op in enumerate((qop, kop)):
                    for i in range(3):
                        off = (l * 2 + side) * 3 * P * N + 4 * u * HD * N + (i * P * N if side else 0)
                        for j in range(3):
                            s1 = bass.AP(scratch.tensor, off + (0 if side else j * P * N),
                                         [[N, HD], [HD * N, 4], [1, N]])
                            r0 = (3 * i + j) * HD
                            sp.dma_start(op[r0:r0 + HD, u % SLOTS, :, :], s1).then_inc(a.ops[u], 16)

            for l in range(2):
                a = at[l]
                if l:
                    sp.wait_ge(at[0].x, NC)
                    sp.dma_start(cos, ins["cos"]).then_inc(tables, 16)
                    sp.dma_start(sin, ins["sin"]).then_inc(tables, 16)
                for side in range(2):
                    sp.wait_ge(a.parts, side + 1)
                    sp.dma_start(scratch[l, side].rearrange("i p n -> p i n"), parts[:, side]).then_inc(
                        a.stored[side], 16)
                    if l:
                        sp.dma_start(tscratch[side].rearrange("i p n -> p i n"), tparts[64:96, side]).then_inc(
                            t_stored, 16)
                for side in range(2):
                    sp.wait_ge(a.stored[side], 16)
                if l:
                    sp.wait_ge(t_stored, 32)
                for u in range(3):
                    load_unit(l, u)
                    if l and u == HYP_UNIT:
                        sp.dma_start(qop[MAXROW:MAXROW + 3, u % SLOTS, :, :], ins["onerow"]).then_inc(a.ops[u], 16)
                        for side, op in enumerate((qop, kop)):
                            for i in range(3):
                                for j in range(3):
                                    part = i if side else j
                                    s1 = bass.AP(tscratch.tensor, (side * 3 + part) * 32 * N,
                                                 [[0, 1], [HD * N, 4], [1, N]])
                                    r0 = TROW + 3 * i + j
                                    sp.dma_start(op[r0:r0 + 1, u % SLOTS, :, :], s1).then_inc(a.ops[u], 16)
                for u in range(UNITS):
                    if l == 0 or u < 2:
                        sp.wait_ge(a.mrow, u + 1)
                        for i in range(3):
                            sp.dma_start(qop[MAXROW + i:MAXROW + i + 1, u % SLOTS, :, :].rearrange(
                                "p j (q n) -> p (j q) n", n=P), mrow[32 * i:32 * i + 32, :]).then_inc(
                                    a.maxrow[u], 16)
                    if u == 1:
                        sp.wait_ge(a.pv, NS)
                        load_unit(l, 3)
            for c in range(NC):
                sp.wait_ge(x_out, c + 1)
                sp.dma_start(out[b, c * CH:(c + 1) * CH, :].rearrange("(t p) d -> p t d", p=P),
                             xn[:, 4 * c:4 * c + 4, :]).then_inc(x_in, 16)
            sp.wait_ge(x_in, 48)


        with nc.Fori(0, B) as b:
            with nc.Block() as block:
                @block.sync
                def _(sp):
                    sync_program(sp, b)

                @block.tensor
                def _(pe):
                    tensor_program(pe)

                @block.scalar
                def _(act):
                    scalar_program(act)

                @block.vector
                def _(dve):
                    nc.vector.tensor_copy(modb[:], mod[:, :, :, bass.ds(b, 1)].rearrange(
                        "p l j b -> p l (j b)")).then_inc(mod_ready, 1)
                    vector_program(dve)

                @block.gpsimd
                def _(pool):
                    pool_program(pool)
            first, last = loop_sems[0].num, loop_sems[-1].num
            assert last - first + 1 == len(loop_sems)
            nc.all_engine_barrier(sems_to_clear=range(first, last + 1))


def kernel(**inputs):
    import concourse.bacc as _bacc
    from concourse.bass_utils import run_bass_kernel_spmd as _run

    a = {k: np.asarray(v) for k, v in inputs.items()}
    order = np.array([h * HD + d for h in HEAD_ORDER for d in range(HD)])
    swap = order.reshape(HEADS, 2, HD // 2)[:, ::-1].reshape(-1)
    qkv = a["L1_attn_qkv_w"]
    q, k, v = qkv[0:D], qkv[D:2 * D], qkv[2 * D:3 * D]

    inv_freq = (np.float32(1.0) / np.float32(10000.0) ** (np.arange(0, HD, 2, dtype=np.float32) / np.float32(HD)))
    freqs = np.outer(inv_freq.astype(np.float32), np.arange(N, dtype=np.float32)).astype(np.float32)
    cos, sin = (f(freqs.astype(np.float64)).astype(np.float32) for f in (np.cos, np.sin))
    half = HD // 2

    cols = np.zeros((P, 16), np.float32)
    pos = np.arange(P) // HD
    hyper = (pos >= 8) & (pos < 12)
    cosine = ((pos >= 6) & (pos < 8)) | (pos >= 12)
    curv = a["L1_attn_curvature"].reshape(-1)
    cols[:, 0], cols[:, 1], cols[:, 2] = a["L0_attn_bk"], a["L0_attn_bf"], a["L1_attn_proj_b"]
    cols[:, 3] = 1.0
    cols[hyper, 3] = np.repeat(curv, HD)
    cols[:, 4] = 1.0 / np.sqrt(HD)
    cols[cosine, 4] = np.sqrt(HD)
    cols[hyper, 4] = np.repeat(curv, HD)
    cols[:, 5], cols[:, 6] = cosine, ~cosine
    cols[:, 8:12] = a["L0_attn_bv"].reshape(4, P).T

    r = np.arange(P)
    rows = np.zeros((96, 56), np.float32)
    for n, at0 in ((8, 0), (16, 8), (32, 24)):
        rows[:, at0:at0 + n] = np.arange(96)[:, None] % n == np.arange(n)[None, :]

    arrays = {
        "x": a["L0_attn_x"], "Wk": a["L0_attn_Wk"], "Wv": a["L0_attn_Wv"], "Wf": a["L0_attn_Wf"],
        "wq": q[order].T, "wqs": q[swap].T, "wk1": k[order].T, "wks": k[swap].T, "wv1": v[order].T,
        "proj": a["L1_attn_proj_w"].T[order],
        "cos": np.tile(cos, (2 * HEADS, 1)),
        "sin": np.tile(np.concatenate([sin, -sin]), (HEADS, 1)),
        "L0_router": a["L0_ffn_router_w"].T, "L0_rbias": a["L0_ffn_router_bias"],
        "L0_shg": a["L0_ffn_sw1"], "L0_shu": a["L0_ffn_sw3"], "L0_shd": a["L0_ffn_sw2"],
        "L0_gate": a["L0_ffn_ew1"], "L0_down": a["L0_ffn_ew2"],
        "L1_router": a["L1_ffn_router_w"].T, "L1_rbias": a["L1_ffn_bias"],
        "L1_shg": a["L1_ffn_sh_gate_w"], "L1_shu": a["L1_ffn_sh_up_w"], "L1_shd": a["L1_ffn_sh_down_w"],
        "L1_gate": a["L1_ffn_gate_w"], "L1_up": a["L1_ffn_up_w"], "L1_down": a["L1_ffn_down_w"],
        "L0_wmod": a["L0_wmod"], "L1_wmod": a["L1_wmod"],
        "c": np.concatenate([a["L0_c"].T, a["L1_c"].T], axis=1),
        "curv": curv, "cols": cols, "rows": rows,
        "tri": np.tril(np.ones((16, 16), np.float32), -1),
        "ident": np.eye(P, dtype=np.float32),
        "heads8": np.kron(np.eye(HEADS, dtype=np.float32), np.ones((HD, HD), np.float32)),
        "maskt": np.where(r[:, None] > r[None, :], np.float32(MASK), np.float32(0.0)),
    }
    import ml_dtypes
    onerow = np.zeros((3, 4, N), ml_dtypes.bfloat16)
    onerow[0] = 1
    arrays["onerow"] = onerow
    arrays = {n: np.ascontiguousarray(v) for n, v in arrays.items()}
    nc = _bacc.Bacc("TRN2", target_bir_lowering=False, num_devices=1)
    ins = {n: nc.dram_tensor("in_" + n, v.shape, mybir.dt.from_np(v.dtype), kind="ExternalInput").ap()
           for n, v in arrays.items()}
    out = nc.dram_tensor("out_x", (B, N, D), F32, kind="ExternalOutput").ap()
    adaln_kernel(nc, ins, out)
    res = _run(nc, [{"in_" + n: v for n, v in arrays.items()}], core_ids=[0])
    return res.results[0]["out_x"]
```

```python
from contextlib import ExitStack

import numpy as np

import concourse.bass as bass
from concourse import mybir

P = 128
B, N, D = 4, 1024, 128
NT = N // P
CH = 512
NC = N // CH
HEADS, HD = 16, 8
UNITS = HEADS // 4
SLOTS = 3
PAIRS = 3 * HD * 3
MAXROW = PAIRS
TROW = PAIRS + 3
K_MAX, K_HYP = PAIRS + 3, PAIRS + 3 + 9
LN_EPS = 1e-5
MASK = -1e38
ARG_GAP = float(np.float32(1.0 + 1e-07) - np.float32(1.0))
HYP_EPS = 1e-06
HYP_UNIT = 3
HEAD_ORDER = [12, 13, 14, 15, 0, 1, 2, 3, 4, 5, 10, 11, 6, 7, 8, 9]

F32, BF16 = mybir.dt.float32, mybir.dt.bfloat16
ALU, ACT, AX = mybir.AluOpType, mybir.ActivationFunctionType, mybir.AxisListType

STEPS = []
for _c in range(NC):
    for _kb in range(4 * (_c + 1)):
        _q0 = max(_c * CH, _kb * P)
        STEPS.append((_c, _kb, _q0, (_c + 1) * CH - _q0, _kb >= 4 * _c))
NS = len(STEPS)
PIECES = []
for _qb in range(NT):
    for _half in range(_qb // 4 + 1):
        _w = min(CH, (_qb + 1) * P - _half * CH)
        PIECES.append((_qb, _half * CH, _w, 2 * _qb + _half))
NP_ = len(PIECES)


def plan_pieces(heads):
    every = [(j, p) for p in range(NP_) for j in heads]
    cost = [64 + PIECES[p][2] for _, p in every]
    widths = [st[3] if i < NS - 3 else 0 for i, st in enumerate(STEPS)]
    plan, n, spent = [], 0, 0
    for i in range(NS):
        share = sum(cost) * sum(widths[:i + 1]) / sum(widths)
        here = []
        while n < len(every) and (spent < share - 1e-6 or i == NS - 1):
            here.append(every[n])
            spent += cost[n]
            n += 1
        plan.append(here)
    return plan


OPS = 16 * 6
OPS_HYP = OPS + 16 * (1 + 12)


def has_max(l, u):
    return l == 0 or u > 0


def nth(l, u):
    return u - l


def is_hyp(l, u):
    return l == 1 and u == HYP_UNIT


def max_heads(l, u):
    return range(2) if (l, u) == (1, 2) else range(4)


PLANS = {k: plan_pieces(range(k)) for k in (2, 4)}


def beside(l, u, s):
    if u + 1 >= UNITS or not has_max(l, u + 1):
        return []
    plan = PLANS[len(max_heads(l, u + 1))]
    n = pieces_before(l, u + 1) + sum(len(x) for x in plan[:s])
    return [(u + 1, n + i, j, p) for i, (j, p) in enumerate(plan[s])]


def pieces_before(l, u):
    return sum(NP_ * len(max_heads(l, v)) for v in range(u) if has_max(l, v))


LAST_PIECES = NS - 4


class Ffn:

    def __init__(self, name, experts, gated):
        self.name, self.experts, self.gated = name, experts, gated
        self.work = [("shared", f, c) for f in range(2) for c in range(NC)]
        self.work += [("expert", e, c) for e in range(experts) for c in range(NC)]


FFN = [Ffn("f0", 8, False), Ffn("f1", 16, True)]


def adaln_kernel(nc, ins, out):
    with ExitStack() as ctx:
        def sb(name, shape, dt=F32):
            return ctx.enter_context(nc.sbuf_tensor(name, shape, dt))

        def sem(name):
            s = ctx.enter_context(nc.semaphore(name))
            loop_sems.append(s)
            return s

        loop_sems = []
        ps = ctx.enter_context(nc.psum_tensor("ps", [P, 8, CH], F32))

        w = {}
        setup_loads = []

        def weight(name, shape, src, dt=F32):
            w[name] = sb("w_" + name, shape, dt)
            setup_loads.append((w[name][:], src))

        def blocks(a):
            return a.rearrange("(k p) m -> p k m", p=P)

        def experts(a):
            return a.rearrange("e p m -> p e m")

        weight("wk", [P, D], ins["Wk"])
        weight("wv", [P, 512], ins["Wv"])
        weight("wf", [P, 4, D], blocks(ins["Wf"]))
        weight("q", [P, D], ins["wq"])
        weight("qs", [P, D], ins["wqs"])
        weight("k", [P, D], ins["wk1"])
        weight("ks", [P, D], ins["wks"])
        weight("v", [P, D], ins["wv1"])
        weight("proj", [P, D], ins["proj"])
        for l, p in ((0, "L0"), (1, "L1")):
            e = FFN[l].experts
            weight(f"router{l}", [P, e], ins[p + "_router"])
            weight(f"rbias{l}", [P, e], ins[p + "_rbias"].rearrange("(a e) -> a e", a=1).broadcast_to([P, e]))
            weight(f"shg{l}", [P, 256], ins[p + "_shg"])
            weight(f"shu{l}", [P, 256], ins[p + "_shu"])
            weight(f"shd{l}", [P, 2, D], blocks(ins[p + "_shd"]))
            weight(f"gate{l}", [P, e, P], experts(ins[p + "_gate"]))
            if l:
                weight("up1", [P, e, P], experts(ins["L1_up"]))
            weight(f"down{l}", [P, e, D], experts(ins[p + "_down"]))
        weight("cols", [P, 16], ins["cols"])
        weight("tri", [P, 16, 16], ins["tri"].rearrange("(a e) f -> a e f", a=1).broadcast_to([P, 16, 16]))
        weight("ident", [P, P], ins["ident"])
        weight("heads8", [P, P], ins["heads8"])
        weight("hsel", [P, 4], ins["hsel"])
        weight("maskt", [P, P], ins["maskt"])
        weight("c", [P, 2 * B], ins["c"])
        weight("rows", [96, 56], ins["rows"])
        cols = w["cols"]
        (C_BK, C_BF, C_PB, C_CURV, C_QS, C_COS, C_NOTCOS, C_BV, C_ONE) = (0, 1, 2, 3, 4, 5, 6, 8, 7)

        identb = sb("identb", [P, P], BF16)
        maskkq = sb("maskkq", [P, P], BF16)
        maskqk = sb("maskqk", [P, P], BF16)
        ones32 = sb("ones32", [P, 32])
        sel32 = sb("sel32", [96, 32, P], BF16)
        consts = sb("consts", [P, 8])
        mod = sb("mod", [P, 2, 6, B])
        modb = sb("modb", [P, 2, 6])
        hyp = sb("hyp", [P, 8])
        curvb = sb("curvb", [P, 4])

        xT = sb("xT", [P, N])
        hT = sb("hT", [P, N])
        xn = sb("xn", [P, NT, D])
        kT = sb("kT", [P, N])
        st = sb("st", [P, NT, 6])
        mv = sb("mv", [P, NT, 2])
        sd = sb("sd", [P, 2, NT])
        qop = sb("qop", [P, SLOTS, 4, N], BF16)
        kop = sb("kop", [P, SLOTS, 4, N], BF16)
        vt = sb("vt", [P, NT, HEADS * 32])
        pr = sb("pr", [P, 3, 4, CH])
        wb = sb("wb", [P, 2, 4, CH])
        osb = sb("osb", [P, 2, CH])
        rsb = sb("rsb", [P, 2, CH])
        on = sb("on", [P, UNITS, N])
        mx = sb("mx", [P, 2, 4, NT, 2])
        nm = sb("nm", [P, 2, 32])
        nr = sb("nr", [P, 3, 32])
        nmp = sb("nmp", [P, 96], BF16)
        mrow = sb("mrow", [96, P], BF16)
        rec = sb("rec", [P, 4, 4])
        wmod = pr[:].rearrange("p a b c -> p (a b c)")[:, 0:6 * D]
        cos, sin = on[:, 1, :], on[:, 2, :]
        lg = osb[:].rearrange("p a b -> p (a b)").rearrange("p (i t e) -> p i t e", i=8, t=NT)


        def selg(e):
            return wb[0:3 * e].rearrange("p a b c -> p (a b c)").bitcast(BF16)[:, 0:e * P].rearrange(
                "p (e n) -> p e n", n=P)

        gT = rsb[0:48, 0, :].bitcast(BF16)
        gp = rsb[:, 1, 0:NT * 24].bitcast(BF16).rearrange("p (t e) -> p t e", t=NT)
        parts = wb[:].rearrange("p a b c -> p (a b c)").bitcast(BF16)[:, 0:6 * N].rearrange(
            "p (s i n) -> p s i n", s=2, i=3)
        tmp = xn[:].rearrange("p t d -> p (t d)")
        cmpa = pr[:, 0].rearrange("p a b -> p (a b)")
        cmpb = pr[:, 1].rearrange("p a b -> p (a b)")


        def hyp_probs(s):
            c, _, q0, wd, _ = STEPS[s]
            n = s % 5
            if n < 2:
                z = qop[:, 1 + n].rearrange("p j n -> p (j n)").bitcast(F32).rearrange("p (j n) -> p j n", j=4)
            else:
                z = pr[:, n - 2]
            return z[:, :, q0 - c * CH:q0 - c * CH + wd]

        fa, fh = pr[:, 2, 0:2], pr[:, 2, 2:4]
        ft = on[:, 0, :].rearrange("p (a b) -> p a b", a=2)
        tA, tR, tT, tU = (on[:, 3, CH + 64 * i:CH + 64 * (i + 1)] for i in range(4))
        tp = on[:, 3, CH + 256:CH + 256 + 96].bitcast(BF16).rearrange("p (t s i h) -> p t s i h", t=NT, s=2, i=3)
        trow = on[0:24, 3, 0:CH].bitcast(BF16)

        nbc = on

        scratch = nc.dram_tensor("parts_scratch", [2, 2, 3, HD, HEADS, N], BF16, kind="Internal").ap()

        s_load = ctx.enter_context(nc.semaphore("s_load"))
        s_small = ctx.enter_context(nc.semaphore("s_small"))
        s_cast = ctx.enter_context(nc.semaphore("s_cast"))
        s_pool = ctx.enter_context(nc.semaphore("s_pool"))
        s_silu = ctx.enter_context(nc.semaphore("s_silu"))
        s_turn = ctx.enter_context(nc.semaphore("s_turn"))
        s_mm = ctx.enter_context(nc.semaphore("s_mm"))
        s_modc = ctx.enter_context(nc.semaphore("s_modc"))
        s_wmod = ctx.enter_context(nc.semaphore("s_wmod"))
        s_sdve = ctx.enter_context(nc.semaphore("s_sdve"))
        s_hyp = ctx.enter_context(nc.semaphore("s_hyp"))
        with nc.Block() as block:
            @block.sync
            def _(sp):
                for dst, src in setup_loads:
                    sp.dma_start(dst, src).then_inc(s_load, 16)
                sp.dma_start(curvb[:], ins["curv"].rearrange("(a e) -> a e", a=1).broadcast_to([P, 4])).then_inc(
                    s_small, 16)
                for l, name in ((0, "L0_wmod"), (1, "L1_wmod")):
                    if l:
                        sp.wait_ge(s_mm, 1)
                    sp.dma_start(wmod, ins[name]).then_inc(s_wmod, 16)

            @block.gpsimd
            def _(pool):
                nc.gpsimd.memset(ones32[:], 1.0)
                nc.gpsimd.memset(kop[:], 1.0)
                nc.gpsimd.memset(consts[:, 0:1], LN_EPS)
                nc.gpsimd.memset(consts[:, 2:3], HYP_EPS)
                nc.gpsimd.memset(consts[:, 1:2], 1.0).then_inc(s_pool, 1)
                pool.wait_ge(s_load, 16 * len(setup_loads))
                for e in range(32):
                    last = nc.gpsimd.tensor_copy(sel32[:, e, :], w["rows"][0:96, 24 + e:25 + e].broadcast_to([96, P]))
                last.then_inc(s_pool, 1)

            @block.scalar
            def _(act):
                act.wait_ge(s_load, 16 * len(setup_loads))
                nc.scalar.activation(w["c"][:], w["c"][:], ACT.Silu).then_inc(s_silu, 1)
                act.wait_ge(s_sdve, 1)
                nc.scalar.activation(hyp[:, 4:8], hyp[:, 0:4], ACT.Sqrt).then_inc(s_hyp, 1)

            @block.tensor
            def _(pe):
                pe.wait_ge(s_silu, 1)
                pe.wait_ge(s_load, 16 * len(setup_loads))
                pe.transpose(ps[:, 7, 0:P], w["maskt"][:], w["ident"][:]).then_inc(s_turn, 1)
                for l in range(2):
                    pe.wait_ge(s_wmod, 16 * (l + 1))
                    for j in range(6):
                        mm = pe.matmul(ps[:, l, B * j:B * j + B], wmod[:, j * D:(j + 1) * D],
                                       w["c"][:, l * B:(l + 1) * B], start=True, stop=True)
                    mm.then_inc(s_mm, 1)

            @block.vector
            def _(dve):
                chain = [0]

                def link(i):
                    chain[0] += 1
                    i.then_inc(s_modc, 1)
                    dve.wait_ge(s_modc, chain[0])

                dve.wait_ge(s_load, 16 * len(setup_loads))
                nc.vector.tensor_copy(identb[:], w["ident"][:])
                nc.vector.tensor_copy(maskkq[:], w["maskt"][:])
                dve.wait_ge(s_small, 16)
                nc.vector.reciprocal(hyp[:, 0:4], curvb[:]).then_inc(s_sdve, 1)
                dve.wait_ge(s_turn, 1)
                nc.vector.tensor_copy(maskqk[:], ps[:, 7, 0:P])
                for l in range(2):
                    dve.wait_ge(s_mm, l + 1)
                    m = mod[:, l].rearrange("p j b -> p (j b)")
                    link(nc.vector.tensor_copy(m, ps[:, l, 0:6 * B]))
                    for j in (1, 4):
                        link(nc.vector.tensor_scalar(mod[:, l, j], mod[:, l, j], 1.0, None, ALU.add))
                    for j in (2, 5):
                        g = mod[:, l, j]
                        link(nc.vector.tensor_scalar(nr[:, 0, 0:B], g, 0.0, 2.0, ALU.is_ge, ALU.mult))
                        link(nc.vector.tensor_scalar(nr[:, 1, 0:B], nr[:, 0, 0:B], -1.0, None, ALU.add))
                        link(nc.vector.tensor_scalar(nr[:, 2, 0:B], g, -1.0, None, ALU.mult))
                        link(nc.vector.tensor_tensor(nr[:, 0, 0:B], nr[:, 2, 0:B], g, ALU.max))
                        link(nc.vector.scalar_tensor_tensor(out=g, in0=nr[:, 0, 0:B], scalar=0.25,
                                                            in1=nr[:, 1, 0:B], op0=ALU.max, op1=ALU.mult))

        x_in, x_out, s_out_tok = sem("x_in"), sem("x_out"), sem("s_out_tok")
        x_tok, x_ready = sem("x_tok"), sem("x_ready")
        ln_tok = [sem(f"ln{n}_tok") for n in range(4)]
        ln_var = [sem(f"ln{n}_var") for n in range(4)]
        ln_std = [sem(f"ln{n}_std") for n in range(4)]
        ln_norm = [sem(f"ln{n}_norm") for n in range(4)]
        ln_back = [sem(f"ln{n}_back") for n in range(4)]
        h_ready = [sem(f"h{n}_ready") for n in range(4)]
        dve_chain, act_chain, pool_chain = sem("dve_chain"), sem("act_chain"), sem("pool_chain")
        mod_ready = sem("mod_ready")

        class Attn:

            def __init__(self, l):
                n = f"a{l}_"
                self.proj = sem(n + "proj")
                self.proj_used = sem(n + "proj_used")
                self.parts = sem(n + "parts")
                self.stored = [sem(n + f"stored{i}") for i in range(2)]
                self.v = sem(n + "v")
                self.vps = sem(n + "vps")
                self.ops = [sem(n + f"ops{u}") for u in range(UNITS)]
                self.maxrow = [sem(n + f"maxrow{u}") for u in range(UNITS)]
                self.piece = sem(n + "piece")
                self.reduced = sem(n + "reduced")
                self.nmp = sem(n + "nmp")
                self.mps = sem(n + "mps")
                self.mrow = sem(n + "mrow")
                self.scores = sem(n + "scores")
                self.exps = sem(n + "exps")
                self.pv = sem(n + "pv")
                self.o_out = sem(n + "o_out")
                self.s_out = sem(n + "s_out")
                self.rs = sem(n + "rs")
                self.on = sem(n + "on")
                self.gelu = sem(n + "gelu")
                self.final = sem(n + "final")
                self.x = sem(n + "x")

        at = [Attn(0), Attn(1)]
        v_ones, tables, sel_ready = sem("v_ones"), sem("tables"), sem("sel_ready")
        sq_ready, ss_ready, ss_cl = sem("sq_ready"), sem("ss_ready"), sem("ss_cl")
        norm_ready, factors, factors_used = sem("norm_ready"), sem("factors"), sem("factors_used")
        t_sum, t_inv, t_parts, t_ps, t_row = sem("t_sum"), sem("t_inv"), sem("t_parts"), sem("t_ps"), sem("t_row")
        hyp_mx, hyp_s, hyp_bc, hyp_bcout = sem("hyp_mx"), sem("hyp_s"), sem("hyp_bc"), sem("hyp_bcout")
        hyp_z, hyp_r, hyp_zr, hyp_inv, hyp_sc, hyp_sub = (
            sem("hyp_z"), sem("hyp_r"), sem("hyp_zr"), sem("hyp_inv"), sem("hyp_sc"), sem("hyp_sub"))
        o_turn, y_tok, y_turn, y_T = sem("o_turn"), sem("y_tok"), sem("y_turn"), sem("y_T")

        class FfnSems:
            def __init__(self, l):
                n = f"f{l}_"
                self.logits, self.score = sem(n + "logits"), sem(n + "score")
                self.parts, self.gps, self.gates = sem(n + "parts"), sem(n + "gps"), sem(n + "gates")
                self.up, self.act, self.hid, self.down = (
                    sem(n + "up"), sem(n + "act"), sem(n + "hid"), sem(n + "down"))
                self.shared, self.ucopy = sem(n + "shared"), sem(n + "ucopy")
                self.x = sem(n + "x")

        fs = [FfnSems(0), FfnSems(1)]

        x_for = [x_ready, at[0].x, fs[0].x, at[1].x]
        HALVES = 2 * NS

        def chunk(t, c):
            return t[:, c * CH:(c + 1) * CH]

        def tensor_program(pe):
            def turn_tiles(src, bank, done, first=None):
                for t in range(NT):
                    if first:
                        first(t)
                    mm = pe.transpose(ps[:, bank + t // 4, (t % 4) * P:(t % 4 + 1) * P], src(t), w["ident"][:])
                    if t % 4 == 3:
                        mm.then_inc(done, 1)

            def layer_norm(n):
                turn_tiles(lambda t: xT[:, t * P:(t + 1) * P], 0, ln_tok[n],
                           lambda t: pe.wait_ge(x_for[n], t // 4 + 1))
                turn_tiles(lambda t: xn[:, t, :], 2, ln_back[n],
                           lambda t: pe.wait_ge(ln_norm[n], t + 1))

            def project(wt, c, bank, done):
                pe.matmul(ps[:, bank, :], wt, chunk(hT, c), start=True, stop=True).then_inc(done, 1)

            def attention(l):
                a = at[l]
                if l == 0:
                    for c in range(NC):
                        pe.wait_ge(h_ready[0], c + 1)
                        project(w["wk"][:], c, 4 + c, a.proj)
                    for t in range(NT):
                        if t >= 2:
                            pe.wait_ge(a.v, t - 1)
                        pe.matmul(ps[:, 6 + t % 2, :], hT[:, t * P:(t + 1) * P], w["wv"][:],
                                  start=True, stop=True).then_inc(a.vps, 1)
                else:
                    for i, (n0, n1) in enumerate((("q", "qs"), ("k", "ks"))):
                        for c in range(NC):
                            if i:
                                pe.wait_ge(a.proj_used, c + 1)
                            else:
                                pe.wait_ge(h_ready[2], c + 1)
                            project(w[n0][:], c, 4 + c, a.proj)
                            project(w[n1][:], c, 6 + c, a.proj)
                    for i in range(2):
                        for c in range(NC):
                            pe.wait_ge(sq_ready, 2 * i + c + 1)
                            if i:
                                pe.wait_ge(ss_cl, c + 1)
                            pe.matmul(ps[:, c, :], w["heads8"][:], rsb[:, c, :], start=True, stop=True)
                            for t in range(4):
                                col = (i * NT + 4 * c + t) * 4
                                mm = pe.matmul(ps[:, 2, col:col + 4], rsb[:, c, t * P:(t + 1) * P], w["hsel"][:],
                                               start=True, stop=True)
                            mm.then_inc(ss_ready, 1)
                    for t in range(NT):
                        if t == 0:
                            pe.wait_ge(a.proj_used, 4)
                        mm = pe.matmul(ps[:, 4 + t // 4, (t % 4) * P:(t % 4 + 1) * P], hT[:, t * P:(t + 1) * P],
                                       w["v"][:], start=True, stop=True)
                        if t % 4 == 3:
                            mm.then_inc(a.vps, 1)
                    pe.wait_ge(t_parts, 1)
                    for t in range(NT):
                        mm = pe.matmul(ps[0:24, 2 + t // 4, (t % 4) * P:(t % 4 + 1) * P],
                                       tp[:, t].rearrange("p s i h -> p (s i h)"), identb[:], start=True, stop=True)
                    mm.then_inc(t_ps, 1)

                def piece(u, g, j, p):
                    qb, k0, wd, _ = PIECES[p]
                    if g == pieces_before(l, u):
                        pe.wait_ge(a.ops[u], OPS_HYP if is_hyp(l, u) else OPS)
                        if nth(l, u) == 0:
                            pe.wait_ge(a.v if l == 0 else a.proj_used, NT if l == 0 else 4)
                        else:
                            pe.wait_ge(a.mrow, nth(l, u))
                    if g >= 2:
                        pe.wait_ge(a.reduced, g - 1)
                    k = K_HYP if is_hyp(l, u) else PAIRS
                    o = ps[:, 6 + g % 2, 0:wd]
                    diag = k0 + wd == (qb + 1) * P
                    mm = pe.matmul(o, qop[0:k, u % SLOTS, j, qb * P:(qb + 1) * P],
                                   kop[0:k, u % SLOTS, j, k0:k0 + wd], start=True, stop=not diag)
                    if diag:
                        mm = pe.matmul(o[:, wd - P:wd], identb[:], maskqk[:], start=False, stop=True)
                    mm.then_inc(a.piece, 1)

                def turn_max(u):
                    pe.wait_ge(a.nmp, nth(l, u) + 1)
                    pe.matmul(ps[0:96, 6, 0:P], nmp[:], identb[:], start=True, stop=True).then_inc(a.mps, 1)

                def spread_max():
                    pe.wait_ge(a.mrow, nth(l, HYP_UNIT) + 1)
                    for i, (j, c) in enumerate([(j, c) for j in range(4) for c in range(NC)]):
                        if i >= 2:
                            pe.wait_ge(hyp_bcout, i - 1)
                        for q in range(4):
                            mm = pe.matmul(ps[:, 6 + i % 2, q * P:(q + 1) * P], sel32[:, NT * j + 4 * c + q, :],
                                           mrow[:], start=True, stop=True)
                        mm.then_inc(hyp_bc, 1)

                def scores(u, s, extra):
                    c, kb, q0, wd, diag = STEPS[s]
                    k = K_HYP if is_hyp(l, u) else K_MAX if has_max(l, u) else PAIRS
                    o0 = q0 - c * CH
                    g = NS * u + s
                    for j in range(4):
                        if j % 2 == 0:
                            if g == 0:
                                pe.wait_ge(h_ready[2 * l], NC)
                                if l:
                                    pe.wait_ge(t_row, 1)
                            elif l and HYP_UNIT * NS <= g - 1 < (HYP_UNIT + 1) * NS:
                                pe.wait_ge(hyp_z, 2 * (g - 1 - HYP_UNIT * NS) + j // 2 + 1)
                            else:
                                pe.wait_ge(a.exps, 2 * (g - 1) + j // 2 + 1)
                        o = ps[:, j, o0:o0 + wd]
                        masked = diag and not is_hyp(l, u)
                        mm = pe.matmul(o, kop[0:k, u % SLOTS, j, kb * P:(kb + 1) * P],
                                       qop[0:k, u % SLOTS, j, q0:q0 + wd], start=True, stop=not masked)
                        if masked:
                            mm = pe.matmul(o[:, 0:P], identb[:], maskkq[:], start=False, stop=True)
                        if j % 2:
                            mm.then_inc(a.scores, 1)
                            if extra:
                                piece(*extra.pop(0))

                def values(u, s, extra):
                    c, kb, q0, wd, _ = STEPS[s]
                    o0 = q0 - c * CH
                    g = NS * u + s
                    last = kb == 4 * c + 3
                    pe.wait_ge(a.exps, 2 * (g + 1))
                    if kb == 0:
                        if g == 0:
                            pe.wait_ge(a.v, NT if l == 0 else 2)
                        else:
                            pe.wait_ge(a.o_out, NC * u + c)
                            if l == 0:
                                pe.wait_ge(a.s_out, NC * u + c)
                    for j in range(4):
                        h = 4 * u + j
                        mm = pe.matmul(ps[32 * j:32 * j + 32, 4, o0:o0 + wd], vt[:, kb, 32 * h:32 * h + 32],
                                       hyp_probs(s)[:, j] if is_hyp(l, u) else pr[:, g % 3, j, o0:o0 + wd],
                                       start=kb == 0, stop=last, tile_position=(0, 32 * j))
                    if l:
                        mm.then_inc(a.pv, 1)
                    if extra:
                        piece(*extra.pop(0))
                    if l == 0:
                        for j in range(4):
                            mm = pe.matmul(ps[32 * j:32 * j + 32, 5, o0:o0 + wd], ones32[:],
                                           pr[:, g % 3, j, o0:o0 + wd], start=kb == 0, stop=last,
                                           tile_position=(0, 32 * j))
                        mm.then_inc(a.pv, 1)
                    while extra:
                        piece(*extra.pop(0))

                def turn_outputs(u, c):
                    i = NC * u + c
                    pe.wait_ge(a.o_out, i + 1)
                    if i:
                        pe.wait_ge(y_tok, i)
                    for t in range(4):
                        mm = pe.transpose(ps[:, 5, t * P:(t + 1) * P], osb[:, i % 2, t * P:(t + 1) * P],
                                          w["ident"][:])
                    mm.then_inc(o_turn, 1)

                if has_max(l, 0):
                    for i in range(4 * NP_):
                        piece(0, i, i % 4, i // 4)
                    turn_max(0)
                for u in range(UNITS):
                    if is_hyp(l, u):
                        spread_max()
                        pe.wait_ge(a.ops[u], OPS_HYP)
                    elif has_max(l, u):
                        pe.wait_ge(a.maxrow[u], 48)
                    else:
                        pe.wait_ge(a.ops[u], OPS)
                    ahead = 3 if is_hyp(l, u) else 1
                    for s in range(ahead):
                        scores(u, s, ())
                    for s in range(NS):
                        extra = beside(l, u, s)
                        if s + ahead < NS:
                            scores(u, s + ahead, extra)
                        values(u, s, extra)
                        if u + 1 < UNITS and has_max(l, u + 1) and s == (
                                NS - 2 if is_hyp(l, u + 1) else LAST_PIECES + 1):
                            turn_max(u + 1)
                        if l and s == 6:
                            turn_outputs(u, 0)
                        if l and s == 2 and u:
                            turn_outputs(u - 1, 1)
                if l:
                    turn_outputs(UNITS - 1, 1)
                    for t in range(NT):
                        pe.wait_ge(y_tok, 7 if t < 4 else 8)
                        if t == 0:
                            pe.wait_ge(a.exps, HALVES * UNITS)
                        mm = pe.transpose(ps[:, t // 4, (t % 4) * P:(t % 4 + 1) * P], kT[:, t * P:(t + 1) * P],
                                          w["ident"][:])
                        if t % 4 == 3:
                            mm.then_inc(y_turn, 1)
                    for c in range(NC):
                        pe.wait_ge(y_T, c + 1)
                        pe.matmul(ps[:, 2 + c, :], w["proj"][:], chunk(hT, c), start=True,
                                  stop=True).then_inc(a.final, 1)
                else:
                    pe.wait_ge(a.exps, HALVES * UNITS)
                    for c in range(NC):
                        for u in range(UNITS):
                            if c == 0:
                                pe.wait_ge(a.gelu, u + 1)
                            mm = pe.matmul(ps[:, c, :], w["wf"][:, u, :], on[:, u, c * CH:(c + 1) * CH],
                                           start=u == 0, stop=u == UNITS - 1)
                        mm.then_inc(a.final, 1)

            def ffn(l):
                f, g = FFN[l], fs[l]
                E = f.experts
                for t in range(NT):
                    pe.wait_ge(h_ready[2 * l + 1], t // 4 + 1)
                    mm = pe.matmul(ps[:, 7, t * E:(t + 1) * E], hT[:, t * P:(t + 1) * P], w[f"router{l}"][:],
                                   start=True, stop=True)
                mm.then_inc(g.logits, 1)

                def gates():
                    pe.wait_ge(g.parts, 1)
                    for t in range(NT):
                        mm = pe.matmul(ps[0:3 * E, 6 + t // 4, (t % 4) * P:(t % 4 + 1) * P], gp[:, t, 0:3 * E],
                                       identb[:], start=True, stop=True)
                    mm.then_inc(g.gps, 1)
                    pe.wait_ge(g.gates, 1)
                    pe.wait_ge(sel_ready, l + 1)

                def hidden_ready(i):
                    if 0 <= i < 2 * NC:
                        pe.wait_ge(g.shared, i + 1)
                    elif i >= 0:
                        pe.wait_ge(g.hid, i + 1 - 2 * NC)

                def up(i):
                    kind, e, c = f.work[i]
                    hidden_ready(i - 2)
                    h = chunk(hT, c)
                    if kind == "shared":
                        pe.matmul(ps[:, 2 + i % 2, :], w[f"shg{l}"][:, e * P:(e + 1) * P], h, start=True, stop=True)
                        mm = pe.matmul(ps[:, 4 + i % 2, :], w[f"shu{l}"][:, e * P:(e + 1) * P], h,
                                       start=True, stop=True)
                    else:
                        pe.matmul(ps[:, 2 + i % 2, :], w[f"gate{l}"][:, e, :], h, start=True, stop=True)
                        if f.gated:
                            pe.matmul(ps[:, 4 + i % 2, :], w["up1"][:, e, :], h, start=True, stop=True)
                        mm = pe.matmul(ps[:, 6 + i % 2, :], selg(E)[:, e, :], chunk(gT, c)[0:3 * E],
                                       start=True, stop=True)
                    mm.then_inc(g.up, 1)

                def down(i):
                    kind, e, c = f.work[i]
                    hidden_ready(i)
                    wt = w[f"shd{l}"][:, e, :] if kind == "shared" else w[f"down{l}"][:, e, :]
                    pe.matmul(ps[:, c, :], wt, fh[:, i % 2, :], start=i < NC,
                              stop=i >= len(f.work) - NC).then_inc(g.down, 1)

                up(0)
                up(1)
                for i in range(len(f.work)):
                    down(i)
                    if i + 2 < len(f.work):
                        if i + 2 == 2 * NC:
                            gates()
                        up(i + 2)

            pe.wait_ge(x_in, 16)
            turn_tiles(lambda t: xn[:, t, :], 0, x_tok)
            for l in range(2):
                layer_norm(2 * l)
                attention(l)
                layer_norm(2 * l + 1)
                ffn(l)
            pe.wait_ge(fs[1].x, 2)
            turn_tiles(lambda t: xT[:, t * P:(t + 1) * P], 2, s_out_tok)

        def scalar_program(act):
            chain = [0]

            def exp_tables():
                nc.scalar.preload_act_table_set("natural_log_exp_and_others")

            def link(i):
                chain[0] += 1
                i.then_inc(act_chain, 1)
                act.wait_ge(act_chain, chain[0])

            def layer_norm(n):
                l, j = n // 2, 3 * (n % 2)
                exp_tables()
                for c in range(NC):
                    y = sd[:, 0, 4 * c:4 * c + 4]
                    act.wait_ge(ln_var[n], c + 1)
                    link(nc.scalar.activation(y, mv[:, 4 * c:4 * c + 4, 1], ACT.Ln, bias=consts[:, 0:1]))
                    nc.scalar.activation(y, y, ACT.Exp, scale=-0.5).then_inc(ln_std[n], 1)
                if n == 0:
                    act.wait_ge(mod_ready, 1)
                for c in range(NC):
                    act.wait_ge(ln_back[n], c + 1)
                    nc.scalar.activation(chunk(hT, c), ps[:, 2 + c, :], ACT.Identity, scale=modb[:, l, j + 1:j + 2],
                                         bias=modb[:, l, j:j + 1]).then_inc(h_ready[n], 1)

            def prepare(l):
                a = at[l]
                if l == 0:
                    for c in range(NC):
                        act.wait_ge(a.proj, c + 1)
                        nc.scalar.activation(chunk(kT, c), ps[:, 4 + c, :], ACT.Identity,
                                             bias=cols[:, C_BK:C_BK + 1]).then_inc(a.proj_used, 1)
                    for t in range(NT):
                        act.wait_ge(a.vps, t + 1)
                        nc.scalar.copy(vt[:, t, :], ps[:, 6 + t % 2, :]).then_inc(a.v, 1)
                    return
                for i, src in enumerate((on[:, 0, :], kT[:])):
                    for c in range(NC):
                        act.wait_ge(norm_ready, 2 * i + c + 1)
                        if i:
                            act.wait_ge(ss_ready, c + 1)
                        nc.scalar.activation(rsb[:, c, :], chunk(src, c), ACT.Square).then_inc(sq_ready, 1)
                    for c in range(NC):
                        act.wait_ge(ss_cl, 2 * i + c + 1)
                        r = chunk(on[:, 2, :], c)
                        if i:
                            act.wait_ge(factors_used, 1)
                        link(nc.scalar.activation(r, chunk(on[:, 1, :], c), ACT.Ln))
                        nc.scalar.activation(r, r, ACT.Exp, scale=-0.5).then_inc(factors, 1)
                act.wait_ge(t_sum, 1)
                link(nc.scalar.activation(tR, tA, ACT.Ln))
                nc.scalar.activation(tR, tR, ACT.Exp, scale=-0.5).then_inc(t_inv, 1)

            def attention(l):
                a = at[l]

                def sums_out(u, c):
                    i = NC * u + c
                    act.wait_ge(a.pv, NS * u + 4 + 8 * c)
                    if i >= 2:
                        act.wait_ge(a.on, i - 1)
                    nc.scalar.activation(rsb[:, i % 2, :], ps[:, 5, :], ACT.Ln).then_inc(a.s_out, 1)
                    act.wait_ge(a.s_out, i + 1)
                    nc.scalar.activation(rsb[:, i % 2, :], rsb[:, i % 2, :], ACT.Exp, scale=-1.0).then_inc(a.rs, 1)

                def hyp_max():
                    z, x, y = nr[:, 0, :], nr[:, 1, :], nr[:, 2, :]
                    act.wait_ge(hyp_mx, 1)
                    link(nc.scalar.activation(z, z, ACT.Ln))
                    nc.scalar.activation(z, z, ACT.Exp, scale=0.5).then_inc(hyp_s, 1)
                    act.wait_ge(hyp_mx, 2)
                    link(nc.scalar.activation(z, z, ACT.Ln, bias=consts[:, 1:2]))
                    for j in range(4):
                        ins_ = nc.scalar.activation(z[:, NT * j:NT * (j + 1)], z[:, NT * j:NT * (j + 1)], ACT.Ln,
                                                    scale=hyp[:, 4 + j:5 + j], bias=consts[:, 2:3])
                    link(ins_)
                    nc.scalar.activation(z, z, ACT.Exp, scale=-1.0).then_inc(hyp_s, 1)

                def hyp_root(s):
                    z = hyp_probs(s)
                    act.wait_ge(hyp_r, s + 1)
                    link(nc.scalar.activation(z, z, ACT.Ln))
                    nc.scalar.activation(z, z, ACT.Exp, scale=0.5).then_inc(hyp_zr, 1)

                def hyp_score(s):
                    z = hyp_probs(s)
                    act.wait_ge(hyp_inv, s + 1)
                    link(nc.scalar.activation(z, z, ACT.Ln, bias=consts[:, 1:2]))
                    for j in range(4):
                        ins_ = nc.scalar.activation(z[:, j], z[:, j], ACT.Ln, scale=hyp[:, 4 + j:5 + j],
                                                    bias=consts[:, 2:3])
                    link(ins_)
                    nc.scalar.activation(z, z, ACT.Exp, scale=-1.0).then_inc(hyp_sc, 1)

                def hyp_exp(s):
                    z = hyp_probs(s)
                    act.wait_ge(hyp_sub, s + 1)
                    nc.scalar.activation(z, z, ACT.Exp).then_inc(a.exps, 2)

                for u in range(UNITS):
                    if is_hyp(l, u):
                        hyp_max()
                        for s in range(NS + 2):
                            if s < NS:
                                hyp_root(s)
                            if 1 <= s <= NS:
                                hyp_score(s - 1)
                            if s >= 2:
                                hyp_exp(s - 2)
                        continue
                    for s in range(NS):
                        g = NS * u + s
                        c, kb, q0, wd, _ = STEPS[s]
                        o0 = q0 - c * CH
                        for half in range(2):
                            act.wait_ge(a.scores, 2 * g + half + 1)
                            if g >= 3:
                                act.wait_ge(a.pv, g - 2)
                            j = 2 * half
                            nc.scalar.activation(pr[:, g % 3, j:j + 2, o0:o0 + wd], ps[:, j:j + 2, o0:o0 + wd],
                                                 ACT.Exp).then_inc(a.exps, 1)
                        if l == 0:
                            if s == 4:
                                sums_out(u, 0)
                            if s == 0 and u:
                                sums_out(u - 1, 1)
                if l == 0:
                    sums_out(UNITS - 1, 1)
                    for u in range(UNITS):
                        act.wait_ge(a.on, NC * (u + 1))
                        nc.scalar.activation(on[:, u, :], on[:, u, :], ACT.Gelu,
                                             bias=cols[:, C_BV + u:C_BV + u + 1]).then_inc(a.gelu, 1)
                else:
                    for c in range(NC):
                        act.wait_ge(y_turn, c + 1)
                        nc.scalar.copy(chunk(hT, c), ps[:, c, :]).then_inc(y_T, 1)

            def ffn(l):
                f, g = FFN[l], fs[l]
                E = f.experts
                act.wait_ge(g.logits, 1)
                nc.scalar.activation(lg[:, 0, :, 0:E], ps[:, 7, 0:NT * E].rearrange("p (t e) -> p t e", e=E),
                                     ACT.Exp, scale=-1.0).then_inc(g.score, 1)
                for i, (kind, e, c) in enumerate(f.work):
                    if i == 2 * NC:
                        act.wait_ge(g.gps, 1)
                        nc.scalar.copy(gT[0:3 * E, :].rearrange("p (a b) -> p a b", a=2),
                                       ps[0:3 * E, 6:8, :]).then_inc(g.gates, 1)
                    act.wait_ge(g.up, i + 1)
                    if 2 <= i < 2 * NC + 2:
                        act.wait_ge(g.shared, i - 1)
                    elif i >= 2:
                        act.wait_ge(g.hid, i - 1 - 2 * NC)
                    fn = ACT.Silu if l or kind == "shared" else ACT.Gelu
                    nc.scalar.activation(fa[:, i % 2, :], ps[:, 2 + i % 2, :], fn).then_inc(g.act, 1)
                    if kind == "shared":
                        nc.scalar.copy(ft[:, i % 2, :], ps[:, 4 + i % 2, :]).then_inc(g.ucopy, 1)

            for l in range(2):
                layer_norm(2 * l)
                prepare(l)
                attention(l)
                layer_norm(2 * l + 1)
                ffn(l)

        def vector_program(dve):
            chain = [0]

            def link(i):
                chain[0] += 1
                i.then_inc(dve_chain, 1)
                dve.wait_ge(dve_chain, chain[0])

            def layer_norm(n):
                def tile(t):
                    return ps[:, t // 4, (t % 4) * P:(t % 4 + 1) * P]

                for c in range(NC):
                    dve.wait_ge(ln_tok[n], c + 1)
                    for t in range(4 * c, 4 * c + 4):
                        ins_ = nc.vector.bn_stats(st[:, t, :], tile(t))
                    link(ins_)
                    for t in range(4 * c, 4 * c + 4):
                        ins_ = nc.vector.bn_aggr(mv[:, t, :], st[:, t, :])
                    ins_.then_inc(ln_var[n], 1)
                for c in range(NC):
                    y, z, v = sd[:, 0, 4 * c:4 * c + 4], sd[:, 1, 4 * c:4 * c + 4], mv[:, 4 * c:4 * c + 4, 1]
                    dve.wait_ge(ln_std[n], c + 1)
                    link(nc.vector.tensor_tensor(z, y, y, ALU.mult))
                    link(nc.vector.scalar_tensor_tensor(out=z, in0=v, scalar=LN_EPS, in1=z, op0=ALU.add,
                                                        op1=ALU.mult))
                    link(nc.vector.tensor_scalar(z, z, -0.5, 1.5, ALU.mult, ALU.add))
                    link(nc.vector.tensor_tensor(z, z, y, ALU.mult))
                    for t in range(4 * c, 4 * c + 4):
                        nc.vector.tensor_scalar(xn[:, t, :], tile(t), mv[:, t, 0:1], sd[:, 1, t:t + 1],
                                                ALU.subtract, ALU.mult).then_inc(ln_norm[n], 1)

            def split(src, dst, r):
                link(nc.vector.tensor_copy(dst(0), src))
                link(nc.vector.tensor_tensor(r, src, dst(0), ALU.subtract))
                link(nc.vector.tensor_copy(dst(1), r))
                return nc.vector.tensor_tensor(dst(2), r, dst(1), ALU.subtract)

            def operand_parts(l, side, src):
                done, p = at[l].parts, parts[:, side]
                nc.vector.tensor_copy(p[:, 0, :], src).then_inc(done, 1)
                dve.wait_ge(done, 3 * side + 1)
                link(nc.vector.tensor_tensor(tmp, src, p[:, 0, :], ALU.subtract))
                nc.vector.tensor_copy(p[:, 1, :], tmp).then_inc(done, 1)
                dve.wait_ge(done, 3 * side + 2)
                nc.vector.tensor_tensor(p[:, 2, :], tmp, p[:, 1, :], ALU.subtract).then_inc(done, 1)
                dve.wait_ge(done, 3 * side + 3)

            def prepare(l):
                a = at[l]
                if l == 0:
                    dve.wait_ge(h_ready[0], NC)
                    operand_parts(0, 0, hT[:])
                    dve.wait_ge(a.proj_used, NC)
                    operand_parts(0, 1, kT[:])
                    return
                q0, q1 = on[:, 0, :], on[:, 1, :]
                dsts = (q0, kT[:])
                dve.wait_ge(tables, 32)
                for i in range(2):
                    for c in range(NC):
                        dve.wait_ge(a.proj, 4 * i + 2 * c + 2)
                        nc.vector.tensor_tensor(chunk(dsts[i], c), ps[:, 4 + c, :], chunk(cos, c), ALU.mult)
                        ins_ = nc.vector.tensor_tensor(chunk(tmp, c), ps[:, 6 + c, :], chunk(sin, c), ALU.mult)
                        ins_.then_inc(a.proj_used, 1)
                        dve.wait_ge(a.proj_used, 2 * i + c + 1)
                        nc.vector.tensor_tensor(chunk(dsts[i], c), chunk(dsts[i], c), chunk(tmp, c),
                                                ALU.add).then_inc(norm_ready, 1)
                for i in range(2):
                    for c in range(NC):
                        dve.wait_ge(ss_ready, 2 * i + c + 1)
                        if i:
                            dve.wait_ge(factors_used, 1)
                        nc.vector.tensor_scalar(chunk(q1, c), ps[:, c, :], 1e-24, None, ALU.max).then_inc(ss_cl, 1)
                    dve.wait_ge(factors, 2 * i + 2)
                    F = on[:, 2, :]
                    link(nc.vector.tensor_scalar(F, F, cols[:, C_COS:C_COS + 1], cols[:, C_NOTCOS:C_NOTCOS + 1],
                                                 ALU.mult, ALU.add))
                    if i == 0:
                        ins_ = nc.vector.scalar_tensor_tensor(out=q0, in0=q0, scalar=cols[:, C_QS:C_QS + 1], in1=F,
                                                              op0=ALU.mult, op1=ALU.mult)
                    else:
                        ins_ = nc.vector.tensor_tensor(kT[:], kT[:], F, ALU.mult)
                    ins_.then_inc(factors_used, 1)
                    dve.wait_ge(factors_used, i + 1)
                    operand_parts(1, i, dsts[i])
                nc.vector.tensor_tensor(tA.rearrange("p (n h) -> p n h", h=4),
                                        ps[:, 2, 0:64].rearrange("p (n h) -> p n h", h=4),
                                        hyp[:, 0:4].unsqueeze(1).broadcast_to([P, 16, 4]), ALU.add).then_inc(t_sum, 1)
                dve.wait_ge(t_inv, 1)
                link(nc.vector.tensor_tensor(tT, tA, tR, ALU.mult))
                link(nc.vector.tensor_tensor(tU, tT, tT, ALU.mult))
                link(nc.vector.tensor_tensor(tU, tA, tU, ALU.subtract))
                link(nc.vector.scalar_tensor_tensor(out=tU, in0=tU, scalar=0.5, in1=tR, op0=ALU.mult, op1=ALU.mult))
                link(nc.vector.tensor_tensor(tT, tT, tU, ALU.add))
                tq = tT[:, 0:32].rearrange("p (n h) -> p n h", h=4)
                link(nc.vector.tensor_scalar(tq, tq, -1.0, None, ALU.mult))
                link(nc.vector.tensor_tensor(tq, tq, curvb[:].unsqueeze(1).broadcast_to([P, NT, 4]), ALU.mult))

                def by_tile(x):
                    return x.rearrange("p (s t h) -> p t s h", s=2, t=NT)

                split(by_tile(tT), lambda k: tp[:, :, :, k, :], by_tile(tU)).then_inc(t_parts, 1)
                dve.wait_ge(t_ps, 1)
                nc.vector.tensor_copy(trow.rearrange("p (a b) -> p a b", a=2), ps[0:24, 2:4, :]).then_inc(t_row, 1)
                dve.wait_ge(v_ones, 1)
                for c in range(NC):
                    dve.wait_ge(a.vps, c + 1)
                    for t in range(4):
                        ins_ = nc.vector.tensor_copy(
                            vt[:, 4 * c + t, :].rearrange("p (h e) -> p h e", e=32)[:, :, 0:HD],
                            ps[:, 4 + c, t * P:(t + 1) * P].rearrange("p (h e) -> p h e", e=HD))
                    ins_.then_inc(a.v, 1)

            def attention(l):
                a = at[l]

                def reduce(u, g, j, p):
                    qb, k0, wd, col = PIECES[p]
                    dve.wait_ge(a.piece, g + 1)
                    nc.vector.tensor_reduce(mx[:, u % 2, j, qb, col % 2:col % 2 + 1], ps[:, 6 + g % 2, 0:wd], AX.X,
                                            ALU.max, negate=True).then_inc(a.reduced, 1)

                def maxima(u):
                    m = nm[:, u % 2, :]
                    m3 = m.rearrange("p (j q) -> p j q", q=NT)
                    n, k = nth(l, u), len(max_heads(l, u))
                    dve.wait_ge(a.reduced, pieces_before(l, u + 1))
                    if k < 4:
                        nc.vector.memset(m3[:, k:4, :], 0.0)
                    nc.vector.tensor_copy(m3[:, 0:k, 0:4], mx[:, u % 2, 0:k, 0:4, 0])
                    link(nc.vector.tensor_tensor(m3[:, 0:k, 4:NT], mx[:, u % 2, 0:k, 4:NT, 0],
                                                 mx[:, u % 2, 0:k, 4:NT, 1], ALU.min))
                    if is_hyp(l, u):
                        x, y = nr[:, 1, :], nr[:, 2, :]
                        link(nc.vector.tensor_scalar(x, m, ARG_GAP, None, ALU.max))
                        nc.vector.scalar_tensor_tensor(out=nr[:, 0, :], in0=x, scalar=2.0, in1=x, op0=ALU.add,
                                                       op1=ALU.mult).then_inc(hyp_mx, 1)
                        dve.wait_ge(hyp_s, 1)
                        nc.vector.tensor_tensor(nr[:, 0, :], nr[:, 0, :], x, ALU.add).then_inc(hyp_mx, 1)
                        dve.wait_ge(hyp_s, 2)
                        link(nc.vector.tensor_scalar(m, nr[:, 0, :], -1.0, None, ALU.mult))
                    if n:
                        dve.wait_ge(a.mps, n)
                    split(m, lambda k: nmp[:, 32 * k:32 * k + 32], nr[:, 1, :]).then_inc(a.nmp, 1)
                    dve.wait_ge(a.mps, n + 1)
                    if n:
                        dve.wait_ge(a.maxrow[u - 1], 48)
                    nc.vector.tensor_copy(mrow[:], ps[0:96, 6, 0:P]).then_inc(a.mrow, 1)

                def outputs_out(u, c):
                    i = NC * u + c
                    dve.wait_ge(a.pv, NS * u + 4 + 8 * c)
                    if i >= 2:
                        dve.wait_ge(o_turn if l else a.on, i - 1)
                    nc.vector.tensor_copy(osb[:, i % 2, :], ps[:, 4, :]).then_inc(a.o_out, 1)

                def to_tokens(u, c):
                    i = NC * u + c
                    dve.wait_ge(o_turn, i + 1)
                    o = ps[:, 5, :].rearrange("p (t j e) -> p t j e", t=4, j=4)
                    link(nc.vector.reciprocal(rec[:], o[:, :, :, HD]))
                    y = kT[:].rearrange("p (t u j e) -> p t u j e", t=NT, u=UNITS, j=4)
                    for j in range(4):
                        ins_ = nc.vector.tensor_tensor(y[:, 4 * c:4 * c + 4, u, j, :], o[:, :, j, 0:HD],
                                                       rec[:, :, j:j + 1].broadcast_to([P, 4, HD]), ALU.mult)
                    ins_.then_inc(y_tok, 1)

                def hyp_step(s):
                    c, kb, q0, wd, diag = STEPS[s]
                    o0 = q0 - c * CH
                    g = NS * HYP_UNIT + s
                    z = hyp_probs(s)
                    x = wb[:, s % 2, :, o0:o0 + wd]
                    if s >= 2:
                        dve.wait_ge(hyp_inv, s - 1)
                    for half in range(2):
                        dve.wait_ge(a.scores, 2 * g + half + 1)
                        j = 2 * half
                        nc.vector.tensor_scalar(x[:, j:j + 2], ps[:, j:j + 2, o0:o0 + wd], -1.0, ARG_GAP, ALU.mult,
                                                ALU.max).then_inc(hyp_z, 1)
                    dve.wait_ge(hyp_z, 2 * s + 2)
                    if s < 2:
                        dve.wait_ge(a.scores, 2 * NS * HYP_UNIT)
                    else:
                        dve.wait_ge(a.pv, NS * HYP_UNIT + s - 4)
                    nc.vector.scalar_tensor_tensor(out=z, in0=x, scalar=2.0, in1=x, op0=ALU.add,
                                                   op1=ALU.mult).then_inc(hyp_r, 1)

                def hyp_shift(s):
                    c, kb, q0, wd, diag = STEPS[s]
                    o0 = q0 - c * CH
                    z = hyp_probs(s)
                    dve.wait_ge(hyp_sc, s + 1)
                    ins_ = nc.vector.tensor_tensor(z, z, nbc[:, :, q0:q0 + wd], ALU.add)
                    if diag:
                        link(ins_)
                        for j in range(4):
                            ins_ = nc.vector.tensor_tensor(z[:, j, 0:P], z[:, j, 0:P], w["maskt"][:], ALU.add)
                    ins_.then_inc(hyp_sub, 1)

                if has_max(l, 0):
                    for i in range(4 * NP_):
                        reduce(0, i, i % 4, i // 4)
                    maxima(0)
                for u in range(UNITS):
                    more = u + 1 < UNITS and has_max(l, u + 1)
                    if is_hyp(l, u):
                        for i, (j, c) in enumerate([(j, c) for j in range(4) for c in range(NC)]):
                            dve.wait_ge(hyp_bc, i + 1)
                            nc.vector.tensor_copy(nbc[:, j, c * CH:(c + 1) * CH],
                                                  ps[:, 6 + i % 2, :]).then_inc(hyp_bcout, 1)
                        dve.wait_ge(hyp_bcout, 8)
                        for s in range(3):
                            hyp_step(s)
                    for s in range(NS):
                        if s == 0 and u:
                            outputs_out(u - 1, 1)
                        if s == 4:
                            outputs_out(u, 0)
                        if is_hyp(l, u):
                            if s + 3 < NS:
                                hyp_step(s + 3)
                            hyp_shift(s)
                        if more:
                            for x in beside(l, u, s):
                                reduce(*x)
                            if s == LAST_PIECES + (1 if is_hyp(l, u + 1) else 0):
                                maxima(u + 1)
                        if l and s == 3 and u:
                            to_tokens(u - 1, 1)
                        if l and s == 7:
                            to_tokens(u, 0)
                outputs_out(UNITS - 1, 1)
                if l:
                    to_tokens(UNITS - 1, 1)
                j = 2
                for c in range(NC):
                    dve.wait_ge(a.final, c + 1)
                    y, res = ps[:, (2 if l else 0) + c, :], chunk(xT, c)
                    if l == 0:
                        link(nc.vector.scalar_tensor_tensor(out=chunk(tmp, c), in0=y, scalar=cols[:, C_BF:C_BF + 1],
                                                            in1=chunk(hT, c), op0=ALU.add, op1=ALU.add))
                        nc.vector.scalar_tensor_tensor(out=res, in0=chunk(tmp, c), scalar=modb[:, l, j:j + 1],
                                                       in1=res, op0=ALU.mult, op1=ALU.add).then_inc(a.x, 1)
                    else:
                        link(nc.vector.tensor_scalar(chunk(tmp, c), y, cols[:, C_PB:C_PB + 1], None, ALU.add))
                        nc.vector.scalar_tensor_tensor(out=res, in0=chunk(tmp, c), scalar=modb[:, l, j:j + 1],
                                                       in1=res, op0=ALU.mult, op1=ALU.add).then_inc(a.x, 1)

            def top(dst, src, T, E, k):
                a4 = cmpa[:, 0:T * E * E].rearrange("p (t e f) -> p t e f", t=T, e=E)
                b4 = cmpb[:, 0:T * E * E].rearrange("p (t e f) -> p t e f", t=T, e=E)
                other = src.unsqueeze(2).broadcast_to([P, T, E, E])
                own = src.unsqueeze(3).broadcast_to([P, T, E, E])
                nc.vector.tensor_tensor(a4, other, own, ALU.is_gt)
                link(nc.vector.tensor_tensor(b4, other, own, ALU.is_equal))
                link(nc.vector.tensor_tensor(b4, b4, w["tri"][:, 0:E, 0:E].unsqueeze(1).broadcast_to([P, T, E, E]),
                                             ALU.mult))
                link(nc.vector.tensor_tensor(a4, a4, b4, ALU.add))
                link(nc.vector.tensor_reduce(dst, a4, AX.X, ALU.add))
                link(nc.vector.tensor_scalar(dst, dst, k - 0.5, None, ALU.is_lt))

            def route(l):
                f, g = FFN[l], fs[l]
                E = f.experts
                s, sb_, m, t0, t1 = (lg[:, i, :, 0:E] for i in range(5))
                den, rc, ok = lg[:, 5, :, 0:1], lg[:, 6, :, 0:1], lg[:, 7, :, 0:1]

                def wide(x, e=E):
                    return x.broadcast_to([P, NT, e])

                dve.wait_ge(g.score, 1)
                link(nc.vector.tensor_scalar(s, s, 1.0, None, ALU.add))
                link(nc.vector.reciprocal(s, s))
                link(nc.vector.tensor_tensor(sb_, s, w[f"rbias{l}"][:].unsqueeze(1).broadcast_to([P, NT, E]),
                                             ALU.add))
                if l == 0:
                    top(m, sb_, NT, E, 2)
                else:
                    sg = lg[:, 1].rearrange("p t (g e) -> p (t g) e", e=4)
                    mg = lg[:, 2].rearrange("p t (g e) -> p (t g) e", e=4)
                    top(mg, sg, 4 * NT, 4, 2)
                    link(nc.vector.tensor_tensor(mg, mg, sg, ALU.mult))
                    gs = lg[:, 3, :, 0:4]
                    link(nc.vector.tensor_reduce(gs, lg[:, 2].rearrange("p t (g e) -> p t g e", e=4), AX.X, ALU.add))
                    gm = lg[:, 4, :, 0:4]
                    top(gm, gs, NT, 4, 2)
                    link(nc.vector.tensor_scalar(gs, gm, -1.0, None, ALU.add))
                    s4 = lg[:, 1].rearrange("p t (g e) -> p t g e", e=4)
                    link(nc.vector.tensor_tensor(s4, s4, gm.unsqueeze(3).broadcast_to([P, NT, 4, 4]), ALU.mult))
                    link(nc.vector.tensor_tensor(s4, s4, gs.unsqueeze(3).broadcast_to([P, NT, 4, 4]), ALU.add))
                    top(m, sb_, NT, E, 4)
                link(nc.vector.tensor_tensor(t0, s, m, ALU.mult))
                link(nc.vector.tensor_reduce(den, t0, AX.X, ALU.add))
                link(nc.vector.tensor_scalar(rc, den, 1e-20 if l else 1e-09, None, ALU.add))
                link(nc.vector.reciprocal(rc, rc))
                if l:
                    link(nc.vector.tensor_tensor(t0, t0, wide(rc), ALU.mult))
                    link(nc.vector.tensor_scalar(t0, t0, 2.5, None, ALU.mult))
                else:
                    link(nc.vector.tensor_scalar(ok, den, 1e-09, None, ALU.is_gt))
                    link(nc.vector.tensor_tensor(rc, rc, ok, ALU.mult))
                    link(nc.vector.tensor_tensor(t0, t0, wide(rc), ALU.mult))
                    link(nc.vector.tensor_scalar(ok, ok, -0.5, 0.5, ALU.mult, ALU.add))
                    link(nc.vector.tensor_tensor(m, m, wide(ok), ALU.mult))
                    link(nc.vector.tensor_tensor(t0, t0, m, ALU.add))
                split(t0, lambda k: gp[:, :, k * E:(k + 1) * E], t1).then_inc(g.parts, 1)

            def ffn(l):
                f, g = FFN[l], fs[l]
                route(l)
                for i, (kind, e, c) in enumerate(f.work):
                    if kind == "shared":
                        continue
                    dve.wait_ge(g.act, i + 1)
                    if i >= 2:
                        dve.wait_ge(g.down, i - 1)
                    hid, a_ = fh[:, i % 2, :], fa[:, i % 2, :]
                    if not f.gated:
                        nc.vector.tensor_tensor(hid, a_, ps[:, 6 + i % 2, :], ALU.mult).then_inc(g.hid, 1)
                    else:
                        link(nc.vector.tensor_tensor(ft[:, i % 2, :], a_, ps[:, 4 + i % 2, :], ALU.mult))
                        nc.vector.tensor_tensor(hid, ft[:, i % 2, :], ps[:, 6 + i % 2, :], ALU.mult).then_inc(
                            g.hid, 1)
                for c in range(NC):
                    dve.wait_ge(g.down, len(f.work) - NC + c + 1)
                    nc.vector.scalar_tensor_tensor(out=chunk(xT, c), in0=ps[:, c, :], scalar=modb[:, l, 5:6],
                                                   in1=chunk(xT, c), op0=ALU.mult, op1=ALU.add).then_inc(g.x, 1)

            for c in range(NC):
                dve.wait_ge(x_tok, c + 1)
                nc.vector.tensor_copy(chunk(xT, c), ps[:, c, :]).then_inc(x_ready, 1)
            for l in range(2):
                layer_norm(2 * l)
                prepare(l)
                attention(l)
                layer_norm(2 * l + 1)
                ffn(l)
            for c in range(NC):
                dve.wait_ge(s_out_tok, c + 1)
                nc.vector.tensor_copy(xn[:, 4 * c:4 * c + 4, :].rearrange("p t d -> p (t d)"),
                                      ps[:, 2 + c, :]).then_inc(x_out, 1)

        def pool_program(pool):
            def select_gates(l):
                pool.wait_ge(at[l].x, NC)
                e, at0 = FFN[l].experts, 8 * l
                for i in range(e):
                    ins_ = nc.gpsimd.tensor_copy(selg(e)[:, i, :],
                                                 w["rows"][0:3 * e, at0 + i:at0 + i + 1].broadcast_to([3 * e, P]))
                ins_.then_inc(sel_ready, 1)

            def shared_products(l):
                g = fs[l]
                for i in range(2 * NC):
                    pool.wait_ge(g.ucopy, i + 1)
                    if i >= 2:
                        pool.wait_ge(g.down, i - 1)
                    nc.gpsimd.tensor_tensor(fh[:, i % 2, :], fa[:, i % 2, :], ft[:, i % 2, :],
                                            ALU.mult).then_inc(g.shared, 1)

            for i in range(NC * UNITS):
                u, c = i // NC, i % NC
                pool.wait_ge(at[0].o_out, i + 1)
                pool.wait_ge(at[0].rs, i + 1)
                nc.gpsimd.tensor_tensor(on[:, u, c * CH:(c + 1) * CH], osb[:, i % 2, :], rsb[:, i % 2, :],
                                        ALU.mult).then_inc(at[0].on, 1)
            pool.wait_ge(at[0].pv, NS * UNITS)
            nc.gpsimd.memset(vt[:], 1.0).then_inc(v_ones, 1)
            select_gates(0)
            shared_products(0)
            for s in range(NS):
                c, kb, q0, wd, _ = STEPS[s]
                o0 = q0 - c * CH
                z = hyp_probs(s)
                pool.wait_ge(hyp_zr, s + 1)
                nc.gpsimd.tensor_tensor(z, z, wb[:, s % 2, :, o0:o0 + wd], ALU.add).then_inc(hyp_inv, 1)
            select_gates(1)
            shared_products(1)

        def sync_program(sp, b):
            sp.dma_start(xn[:], ins["x"][b].rearrange("(t p) d -> p t d", p=P)).then_inc(x_in, 16)

            def load_unit(l, u):
                a = at[l]
                for side, op in enumerate((qop, kop)):
                    if u == 0:
                        sp.wait_ge(a.stored[side], 48)
                    for i in range(3):
                        heads = scratch[l, side, :, :, 4 * u:4 * u + 4, :].rearrange("i d h n -> i d (h n)")
                        if side:
                            src = heads[i:i + 1].broadcast_to([3, HD, 4 * N])
                        else:
                            src = heads.rearrange("i d n -> (i d) n")
                        sp.dma_start(op[24 * i:24 * i + 24, u % SLOTS, :, :].rearrange("p h n -> p (h n)"),
                                     src).then_inc(a.ops[u], 16)
                if is_hyp(l, u):
                    sp.dma_start(qop[MAXROW:MAXROW + 3, u % SLOTS, :, :], ins["onerow"]).then_inc(a.ops[u], 16)
                    sp.wait_ge(t_row, 1)
                    for i in range(3):
                        r0 = TROW + 3 * i
                        sp.dma_start(qop[r0:r0 + 3, u % SLOTS, :, :], trow[0:12]).then_inc(a.ops[u], 16)
                        for j in range(3):
                            sp.dma_start(kop[r0 + j:r0 + j + 1, u % SLOTS, :, :],
                                         trow[12 + 4 * i:16 + 4 * i]).then_inc(a.ops[u], 16)

            for l in range(2):
                a = at[l]
                if l:
                    sp.wait_ge(at[0].x, NC)
                    sp.dma_start(cos, ins["cos"]).then_inc(tables, 16)
                    sp.dma_start(sin, ins["sin"]).then_inc(tables, 16)
                for side in range(2):
                    for i in range(3):
                        sp.wait_ge(a.parts, 3 * side + i + 1)
                        sp.dma_start(scratch[l, side, i].rearrange("d h n -> h d n"), parts[:, side, i]).then_inc(a.stored[side], 16)
                for u in range(3):
                    load_unit(l, u)
                for u in range(UNITS):
                    if has_max(l, u) and not is_hyp(l, u):
                        sp.wait_ge(a.mrow, nth(l, u) + 1)
                        for i in range(3):
                            sp.dma_start(qop[MAXROW + i:MAXROW + i + 1, u % SLOTS, :, :].rearrange(
                                "p j (q n) -> p (j q) n", n=P), mrow[32 * i:32 * i + 32, :]).then_inc(
                                    a.maxrow[u], 16)
                    if u == 1:
                        sp.wait_ge(a.pv, NS)
                        load_unit(l, 3)
            for c in range(NC):
                sp.wait_ge(x_out, c + 1)
                sp.dma_start(out[b, c * CH:(c + 1) * CH, :].rearrange("(t p) d -> p t d", p=P),
                             xn[:, 4 * c:4 * c + 4, :]).then_inc(x_in, 16)
            sp.wait_ge(x_in, 48)


        with nc.Fori(0, B) as b:
            with nc.Block() as block:
                @block.sync
                def _(sp):
                    sync_program(sp, b)

                @block.tensor
                def _(pe):
                    tensor_program(pe)

                @block.scalar
                def _(act):
                    scalar_program(act)

                @block.vector
                def _(dve):
                    nc.vector.tensor_copy(modb[:], mod[:, :, :, bass.ds(b, 1)].rearrange(
                        "p l j b -> p l (j b)")).then_inc(mod_ready, 1)
                    vector_program(dve)

                @block.gpsimd
                def _(pool):
                    pool_program(pool)
            first, last = loop_sems[0].num, loop_sems[-1].num
            assert last - first + 1 == len(loop_sems)
            nc.all_engine_barrier(sems_to_clear=range(first, last + 1))


def kernel(**inputs):
    import concourse.bacc as _bacc
    from concourse.bass_utils import run_bass_kernel_spmd as _run

    a = {k: np.asarray(v) for k, v in inputs.items()}
    order = np.array([h * HD + d for h in HEAD_ORDER for d in range(HD)])
    swap = order.reshape(HEADS, 2, HD // 2)[:, ::-1].reshape(-1)
    qkv = a["L1_attn_qkv_w"]
    q, k, v = qkv[0:D], qkv[D:2 * D], qkv[2 * D:3 * D]

    inv_freq = (np.float32(1.0) / np.float32(10000.0) ** (np.arange(0, HD, 2, dtype=np.float32) / np.float32(HD)))
    freqs = np.outer(inv_freq.astype(np.float32), np.arange(N, dtype=np.float32)).astype(np.float32)
    cos, sin = (f(freqs.astype(np.float64)).astype(np.float32) for f in (np.cos, np.sin))
    half = HD // 2

    cols = np.zeros((P, 16), np.float32)
    pos = np.arange(P) // HD
    heads = np.array(HEAD_ORDER)[pos]
    hyper = (heads >= 6) & (heads < 10)
    cosine = heads >= 10
    curv = a["L1_attn_curvature"].reshape(-1)
    cols[:, 0], cols[:, 1], cols[:, 2] = a["L0_attn_bk"], a["L0_attn_bf"], a["L1_attn_proj_b"]
    cols[:, 4] = 1.0 / np.sqrt(HD)
    cols[cosine, 4] = np.sqrt(HD)
    cols[hyper, 4] = np.repeat(curv, HD)
    cols[:, 5], cols[:, 6] = cosine, ~cosine
    cols[:, 8:12] = a["L0_attn_bv"].reshape(4, P).T

    r = np.arange(P)
    rows = np.zeros((96, 56), np.float32)
    for n, at0 in ((8, 0), (16, 8), (32, 24)):
        rows[:, at0:at0 + n] = np.arange(96)[:, None] % n == np.arange(n)[None, :]

    arrays = {
        "x": a["L0_attn_x"], "Wk": a["L0_attn_Wk"], "Wv": a["L0_attn_Wv"], "Wf": a["L0_attn_Wf"],
        "wq": q[order].T, "wqs": q[swap].T, "wk1": k[order].T, "wks": k[swap].T, "wv1": v[order].T,
        "proj": a["L1_attn_proj_w"].T[order],
        "cos": np.tile(cos, (2 * HEADS, 1)),
        "sin": np.tile(np.concatenate([sin, -sin]), (HEADS, 1)),
        "L0_router": a["L0_ffn_router_w"].T, "L0_rbias": a["L0_ffn_router_bias"],
        "L0_shg": a["L0_ffn_sw1"], "L0_shu": a["L0_ffn_sw3"], "L0_shd": a["L0_ffn_sw2"],
        "L0_gate": a["L0_ffn_ew1"], "L0_down": a["L0_ffn_ew2"],
        "L1_router": a["L1_ffn_router_w"].T, "L1_rbias": a["L1_ffn_bias"],
        "L1_shg": a["L1_ffn_sh_gate_w"], "L1_shu": a["L1_ffn_sh_up_w"], "L1_shd": a["L1_ffn_sh_down_w"],
        "L1_gate": a["L1_ffn_gate_w"], "L1_up": a["L1_ffn_up_w"], "L1_down": a["L1_ffn_down_w"],
        "L0_wmod": a["L0_wmod"], "L1_wmod": a["L1_wmod"],
        "c": np.concatenate([a["L0_c"].T, a["L1_c"].T], axis=1),
        "curv": curv, "cols": cols, "rows": rows,
        "tri": np.tril(np.ones((16, 16), np.float32), -1),
        "hsel": (heads[:, None] == 6 + np.arange(4)[None, :]).astype(np.float32),
        "ident": np.eye(P, dtype=np.float32),
        "heads8": np.kron(np.eye(HEADS, dtype=np.float32), np.ones((HD, HD), np.float32)),
        "maskt": np.where(r[:, None] > r[None, :], np.float32(MASK), np.float32(0.0)),
    }
    import ml_dtypes
    onerow = np.zeros((3, 4, N), ml_dtypes.bfloat16)
    onerow[0] = 1
    arrays["onerow"] = onerow
    arrays = {n: np.ascontiguousarray(v) for n, v in arrays.items()}
    nc = _bacc.Bacc("TRN2", target_bir_lowering=False, num_devices=1)
    ins = {n: nc.dram_tensor("in_" + n, v.shape, mybir.dt.from_np(v.dtype), kind="ExternalInput").ap()
           for n, v in arrays.items()}
    out = nc.dram_tensor("out_x", (B, N, D), F32, kind="ExternalOutput").ap()
    adaln_kernel(nc, ins, out)
    res = _run(nc, [{"in_" + n: v for n, v in arrays.items()}], core_ids=[0])
    return res.results[0]["out_x"]
```

```python
from contextlib import ExitStack

import numpy as np

import concourse.bass as bass
from concourse import mybir

P = 128
B, N, D = 4, 1024, 128
NT = N // P
CH = 512
NC = N // CH
HEADS, HD = 16, 8
UNITS = HEADS // 4
SLOTS = 3
HYP_RING = 5
PAIRS = 3 * HD * 3
MAXROW = PAIRS
TROW = PAIRS + 3
K_MAX, K_HYP = PAIRS + 3, PAIRS + 3 + 9
LN_EPS = 1e-5
MASK = -1e38
ARG_GAP = float(np.float32(1.0 + 1e-07) - np.float32(1.0))
HYP_EPS = 1e-06
HYP_UNIT = 3
HEAD_ORDER = [12, 13, 14, 15, 4, 5, 10, 11, 0, 1, 2, 3, 6, 7, 8, 9]

F32, BF16 = mybir.dt.float32, mybir.dt.bfloat16
ALU, ACT, AX = mybir.AluOpType, mybir.ActivationFunctionType, mybir.AxisListType

STEPS = []
for _c in range(NC):
    for _kb in range(4 * (_c + 1)):
        _q0 = max(_c * CH, _kb * P)
        STEPS.append((_c, _kb, _q0, (_c + 1) * CH - _q0, _kb >= 4 * _c))
NS = len(STEPS)
PIECES = []
for _qb in range(NT):
    for _half in range(_qb // 4 + 1):
        _w = min(CH, (_qb + 1) * P - _half * CH)
        PIECES.append((_qb, _half * CH, _w, 2 * _qb + _half))
NP_ = len(PIECES)


OPS = 16 * 6
OPS_HYP = OPS + 16 * (1 + 2)


def is_hyp(l, u):
    return l == 1 and u == HYP_UNIT


def has_max(l, u):
    return l == 0 or u > 0


def max_heads(l, u):
    return range(2) if (l, u) == (1, 1) else range(4)


def slot(l, u):
    return (0, 1, 0, 2)[u] if l else u % SLOTS


HYP_AT = 3
HYP_HALVES = 2 * NS
BOTH = tuple(range(NC))
MAXES = (((0, BOTH), (1, BOTH), (2, BOTH), (3, BOTH)),
         ((HYP_UNIT, (0,)), (HYP_UNIT, (1,)), (1, BOTH), (2, BOTH)))
STD_UNITS = (UNITS, UNITS - 1)
POSITIONS = (UNITS * NS, max(3 * NS, HYP_AT + HYP_HALVES + 3) + 1)


def nth(l, u):
    return ((0, 1, 2, 3), (HYP_UNIT, 1, 2))[l].index(u)


def score_jobs(l):
    steps = STD_UNITS[l] * NS
    jobs = [(False, 0, 0), (False, 0, 1)]
    for p in range(POSITIONS[l]):
        if p + 1 < steps:
            jobs += [(False, p + 1, 0), (False, p + 1, 1)]
        if l and 0 <= p - HYP_AT < HYP_HALVES:
            jobs.append((True, p - HYP_AT, (p - HYP_AT) % 2))
    return jobs


JOBS = [score_jobs(l) for l in range(2)]


def output_order(l):
    outs = [(NS * u + 4 + 8 * c, u, c) for u in range(STD_UNITS[l]) for c in range(NC)]
    if l:
        outs += [(HYP_AT + 2 * (4 + 8 * c) + 3, HYP_UNIT, c) for c in range(NC)]
    return sorted(outs)


OUTS = [output_order(l) for l in range(2)]


def side_plan(l):
    plan = {p: [] for p in range(-1, POSITIONS[l] + 1)}

    def pieces(u, first, last, chunks=BOTH):
        every = [("piece", (u, j, p)) for p in range(NP_) for j in max_heads(l, u) if PIECES[p][0] // 4 in chunks]
        cost = [64 + PIECES[what[2]][2] for _, what in every]
        widths = [1 if l else STEPS[p % NS][3] for p in range(first, last + 1)]
        n, spent = 0, 0
        for i, p in enumerate(range(first, last + 1)):
            share = sum(cost) * sum(widths[:i + 1]) / sum(widths)
            while n < len(every) and (spent < share - 1e-6 or p == last):
                plan[p].append(every[n])
                spent += cost[n]
                n += 1
        plan[last].append(("maxima", (u, chunks)))

    if l == 0:
        pieces(0, -1, -1)
        plan[-1].append(("max", (0, BOTH)))
        for u in range(1, UNITS):
            first = NS * (u - 1)
            pieces(u, first, first + NS - 4)
            plan[first + NS - 3].append(("max", (u, BOTH)))
    else:
        pieces(HYP_UNIT, 0, 1, (0,))
        plan[3].append(("max", (HYP_UNIT, (0,))))
        plan[3] += [("spread", (0, j)) for j in range(4)]
        pieces(HYP_UNIT, 2, 5, (1,))
        plan[7].append(("max", (HYP_UNIT, (1,))))
        plan[7] += [("spread", (1, j)) for j in range(4)]
        pieces(1, 6, 9)
        plan[10].append(("max", (1, BOTH)))
        pieces(2, 13, 21)
        plan[22].append(("max", (2, BOTH)))
        for i, (p, u, c) in enumerate(OUTS[l]):
            plan[min(p + 2, POSITIONS[l])].append(("turn", (i, u, c)))
    n = 0
    for p in sorted(plan):
        items = []
        for kind, what in plan[p]:
            items.append((kind, None if kind == "maxima" else n, what))
            n += kind != "maxima"
        plan[p] = items
    return plan


SIDE = [side_plan(l) for l in range(2)]


def side_ring(l, g):
    return 6 if l == 0 and g < 4 * NP_ else 2


def side_bank(l, g):
    return (6, 7, 0, 1, 2, 3)[g % side_ring(l, g)]


def side_count(l, kind, what):
    return [g for p in SIDE[l] for k, g, w_ in SIDE[l][p] if (k, w_) == (kind, what)][0] + 1


class Ffn:

    def __init__(self, name, experts, gated):
        self.name, self.experts, self.gated = name, experts, gated
        self.work = [("shared", f, c) for f in range(2) for c in range(NC)]
        self.work += [("expert", e, c) for c in range(NC) for e in range(experts)]
        self.first = [2 * NC + experts * c for c in range(NC)]
        self.last = [2 * NC + experts * (c + 1) - 1 for c in range(NC)]


FFN = [Ffn("f0", 8, False), Ffn("f1", 16, True)]


def adaln_kernel(nc, ins, out):
    with ExitStack() as ctx:
        def sb(name, shape, dt=F32):
            return ctx.enter_context(nc.sbuf_tensor(name, shape, dt))

        def sem(name):
            s = ctx.enter_context(nc.semaphore(name))
            loop_sems.append(s)
            return s

        loop_sems = []
        ps = ctx.enter_context(nc.psum_tensor("ps", [P, 8, CH], F32))

        w = {}
        setup_loads = []

        def weight(name, shape, src, dt=F32):
            w[name] = sb("w_" + name, shape, dt)
            setup_loads.append((w[name][:], src))

        def blocks(a):
            return a.rearrange("(k p) m -> p k m", p=P)

        def experts(a):
            return a.rearrange("e p m -> p e m")

        weight("wk", [P, D], ins["Wk"])
        weight("wv", [P, 512], ins["Wv"])
        weight("wf", [P, 4, D], blocks(ins["Wf"]))
        weight("q", [P, D], ins["wq"])
        weight("qs", [P, D], ins["wqs"])
        weight("k", [P, D], ins["wk1"])
        weight("ks", [P, D], ins["wks"])
        weight("v", [P, D], ins["wv1"])
        weight("proj", [P, D], ins["proj"])
        for l, p in ((0, "L0"), (1, "L1")):
            e = FFN[l].experts
            weight(f"router{l}", [P, e], ins[p + "_router"])
            weight(f"rbias{l}", [P, e], ins[p + "_rbias"].rearrange("(a e) -> a e", a=1).broadcast_to([P, e]))
            weight(f"shg{l}", [P, 256], ins[p + "_shg"])
            weight(f"shu{l}", [P, 256], ins[p + "_shu"])
            weight(f"shd{l}", [P, 2, D], blocks(ins[p + "_shd"]))
            weight(f"gate{l}", [P, e, P], experts(ins[p + "_gate"]))
            if l:
                weight("up1", [P, e, P], experts(ins["L1_up"]))
            weight(f"down{l}", [P, e, D], experts(ins[p + "_down"]))
        weight("cols", [P, 16], ins["cols"])
        weight("tri", [P, 16, 16], ins["tri"].rearrange("(a e) f -> a e f", a=1).broadcast_to([P, 16, 16]))
        weight("after", [P, 16], ins["after"].rearrange("(a e) -> a e", a=1).broadcast_to([P, 16]))
        weight("ident", [P, P], ins["ident"])
        weight("heads8", [P, P], ins["heads8"])
        weight("hsel", [P, 4], ins["hsel"])
        weight("maskt", [P, P], ins["maskt"])
        weight("c", [P, 2 * B], ins["c"])
        weight("rows", [96, 56], ins["rows"])
        cols = w["cols"]
        C_BK, C_BF, C_PB, C_QS, C_COS, C_NOTCOS, C_BV = 0, 1, 2, 4, 5, 6, 8

        identb = sb("identb", [P, P], BF16)
        maskkq = sb("maskkq", [P, P], BF16)
        maskqk = sb("maskqk", [P, P], BF16)
        ones32 = sb("ones32", [P, 32])
        sel32 = sb("sel32", [96, 32, P], BF16)
        consts = sb("consts", [P, 8])
        mod = sb("mod", [P, 2, 6, B])
        modb = sb("modb", [P, 2, 6])
        hyp = sb("hyp", [P, 8])
        curvb = sb("curvb", [P, 4])

        xT = sb("xT", [P, N])
        hT = sb("hT", [P, N])
        xn = sb("xn", [P, NT, D])
        kT = sb("kT", [P, N])
        st = sb("st", [P, NT, 6])
        mv = sb("mv", [P, NT, 2])
        sd = sb("sd", [P, 2, NT])
        qop = sb("qop", [P, SLOTS, 4, N], BF16)
        kop = sb("kop", [P, SLOTS, 4, N], BF16)
        vt = sb("vt", [P, NT, HEADS * 32])
        pr = sb("pr", [P, 3, 4, CH])
        wb = sb("wb", [P, 2, 4, CH])
        osb = sb("osb", [P, 2, CH])
        rsb = sb("rsb", [P, 2, CH])
        on = sb("on", [P, UNITS, N])
        mx = sb("mx", [P, 2, 4, NT, 2])
        nm = sb("nm", [P, 2, 32])
        nr = sb("nr", [P, 3, 32])
        nmp = sb("nmp", [P, 96], BF16)
        mrow = sb("mrow", [96, P], BF16)
        rec = sb("rec", [P, 4, 4])
        wmod = pr[:].rearrange("p a b c -> p (a b c)")[:, 0:6 * D]
        cos, sin = on[:, 1, :], on[:, 2, :]
        lg = osb[:].rearrange("p a b -> p (a b)").rearrange("p (i t e) -> p i t e", i=8, t=NT)


        def selg(e):
            return wb[0:3 * e].rearrange("p a b c -> p (a b c)").bitcast(BF16)[:, 0:e * P].rearrange(
                "p (e n) -> p e n", n=P)

        gT = rsb[0:48, 0, :].bitcast(BF16)
        gp = rsb[:, 1, 0:NT * 24].bitcast(BF16).rearrange("p (t e) -> p t e", t=NT)
        parts = wb[:].rearrange("p a b c -> p (a b c)").bitcast(BF16)[:, 0:6 * N].rearrange(
            "p (s i n) -> p s i n", s=2, i=3)
        tmp = xn[:].rearrange("p t d -> p (t d)")
        cmpa = pr[:, 0].rearrange("p a b -> p (a b)")


        def hyp_x(k):
            c, _, q0, wd, _ = STEPS[k // 2]
            return wb[:, 0, 2 * (k % 2):2 * (k % 2) + 2, q0 - c * CH:q0 - c * CH + wd]

        def hyp_z(k):
            c, _, q0, wd, _ = STEPS[k // 2]
            z = (hT[:].rearrange("p (j n) -> p j n", j=2), tmp.rearrange("p (j n) -> p j n", j=2), rsb[:],
                 wb[:, 1, 0:2], wb[:, 1, 2:4])[k % HYP_RING]
            return z[:, :, q0 - c * CH:q0 - c * CH + wd]

        fa, fh = pr[:, 2, 0:2], pr[:, 2, 2:4]
        ft = on[:, 0, :].rearrange("p (a b) -> p a b", a=2)
        tA, tR, tT, tU = (on[:, 3, CH + 64 * i:CH + 64 * (i + 1)] for i in range(4))
        tp = on[:, 3, CH + 256:CH + 256 + 96].bitcast(BF16).rearrange("p (t s i h) -> p t s i h", t=NT, s=2, i=3)
        tp9 = on[:, 1, 0:288].bitcast(BF16).rearrange("p (t s r) -> p t s r", t=NT, s=2)
        trow = [on[0:36, 3, 0:CH].bitcast(BF16), on[0:36, 2, 0:CH].bitcast(BF16)]

        nbc = on

        scratch = nc.dram_tensor("parts_scratch", [2, 2, 3, HD, HEADS, N], BF16, kind="Internal").ap()

        s_load = ctx.enter_context(nc.semaphore("s_load"))
        s_small = ctx.enter_context(nc.semaphore("s_small"))
        s_cast = ctx.enter_context(nc.semaphore("s_cast"))
        s_pool = ctx.enter_context(nc.semaphore("s_pool"))
        s_silu = ctx.enter_context(nc.semaphore("s_silu"))
        s_turn = ctx.enter_context(nc.semaphore("s_turn"))
        s_mm = ctx.enter_context(nc.semaphore("s_mm"))
        s_modc = ctx.enter_context(nc.semaphore("s_modc"))
        s_wmod = ctx.enter_context(nc.semaphore("s_wmod"))
        s_sdve = ctx.enter_context(nc.semaphore("s_sdve"))
        s_hyp = ctx.enter_context(nc.semaphore("s_hyp"))
        with nc.Block() as block:
            @block.sync
            def _(sp):
                for dst, src in setup_loads:
                    sp.dma_start(dst, src).then_inc(s_load, 16)
                sp.dma_start(curvb[:], ins["curv"].rearrange("(a e) -> a e", a=1).broadcast_to([P, 4])).then_inc(
                    s_small, 16)
                for l, name in ((0, "L0_wmod"), (1, "L1_wmod")):
                    if l:
                        sp.wait_ge(s_mm, 1)
                    sp.dma_start(wmod, ins[name]).then_inc(s_wmod, 16)

            @block.gpsimd
            def _(pool):
                nc.gpsimd.memset(ones32[:], 1.0)
                nc.gpsimd.memset(kop[:], 1.0)
                nc.gpsimd.memset(consts[:, 0:1], LN_EPS)
                nc.gpsimd.memset(consts[:, 2:3], HYP_EPS)
                nc.gpsimd.memset(consts[:, 1:2], 1.0).then_inc(s_pool, 1)
                pool.wait_ge(s_load, 16 * len(setup_loads))
                for e in range(32):
                    last = nc.gpsimd.tensor_copy(sel32[:, e, :], w["rows"][0:96, 24 + e:25 + e].broadcast_to([96, P]))
                last.then_inc(s_pool, 1)

            @block.scalar
            def _(act):
                act.wait_ge(s_load, 16 * len(setup_loads))
                nc.scalar.activation(w["c"][:], w["c"][:], ACT.Silu).then_inc(s_silu, 1)
                act.wait_ge(s_sdve, 1)
                nc.scalar.activation(hyp[:, 4:8], hyp[:, 0:4], ACT.Sqrt).then_inc(s_hyp, 1)

            @block.tensor
            def _(pe):
                pe.wait_ge(s_silu, 1)
                pe.wait_ge(s_load, 16 * len(setup_loads))
                pe.transpose(ps[:, 7, 0:P], w["maskt"][:], w["ident"][:]).then_inc(s_turn, 1)
                for l in range(2):
                    pe.wait_ge(s_wmod, 16 * (l + 1))
                    for j in range(6):
                        mm = pe.matmul(ps[:, l, B * j:B * j + B], wmod[:, j * D:(j + 1) * D],
                                       w["c"][:, l * B:(l + 1) * B], start=True, stop=True)
                    mm.then_inc(s_mm, 1)

            @block.vector
            def _(dve):
                chain = [0]

                def link(i):
                    chain[0] += 1
                    i.then_inc(s_modc, 1)
                    dve.wait_ge(s_modc, chain[0])

                dve.wait_ge(s_load, 16 * len(setup_loads))
                nc.vector.tensor_copy(identb[:], w["ident"][:])
                nc.vector.tensor_copy(maskkq[:], w["maskt"][:])
                dve.wait_ge(s_small, 16)
                nc.vector.reciprocal(hyp[:, 0:4], curvb[:]).then_inc(s_sdve, 1)
                dve.wait_ge(s_turn, 1)
                nc.vector.tensor_copy(maskqk[:], ps[:, 7, 0:P])
                for l in range(2):
                    dve.wait_ge(s_mm, l + 1)
                    m = mod[:, l].rearrange("p j b -> p (j b)")
                    link(nc.vector.tensor_copy(m, ps[:, l, 0:6 * B]))
                    for j in (1, 4):
                        link(nc.vector.tensor_scalar(mod[:, l, j], mod[:, l, j], 1.0, None, ALU.add))
                    for j in (2, 5):
                        g = mod[:, l, j]
                        link(nc.vector.tensor_scalar(nr[:, 0, 0:B], g, 0.0, 2.0, ALU.is_ge, ALU.mult))
                        link(nc.vector.tensor_scalar(nr[:, 1, 0:B], nr[:, 0, 0:B], -1.0, None, ALU.add))
                        link(nc.vector.tensor_scalar(nr[:, 2, 0:B], g, -1.0, None, ALU.mult))
                        link(nc.vector.tensor_tensor(nr[:, 0, 0:B], nr[:, 2, 0:B], g, ALU.max))
                        link(nc.vector.scalar_tensor_tensor(out=g, in0=nr[:, 0, 0:B], scalar=0.25,
                                                            in1=nr[:, 1, 0:B], op0=ALU.max, op1=ALU.mult))

        x_in, x_out, s_out_tok = sem("x_in"), sem("x_out"), sem("s_out_tok")
        x_tok, x_ready = sem("x_tok"), sem("x_ready")
        ln_tok = [sem(f"ln{n}_tok") for n in range(4)]
        ln_var = [sem(f"ln{n}_var") for n in range(4)]
        ln_std = [sem(f"ln{n}_std") for n in range(4)]
        ln_norm = [sem(f"ln{n}_norm") for n in range(4)]
        ln_back = [sem(f"ln{n}_back") for n in range(4)]
        h_ready = [sem(f"h{n}_ready") for n in range(4)]
        dve_chain, act_chain = sem("dve_chain"), sem("act_chain")
        mod_ready = sem("mod_ready")

        class Attn:

            def __init__(self, l):
                n = f"a{l}_"
                self.proj = sem(n + "proj")
                self.proj_used = sem(n + "proj_used")
                self.parts = sem(n + "parts")
                self.stored = [sem(n + f"stored{i}") for i in range(2)]
                self.v = sem(n + "v")
                self.vps = sem(n + "vps")
                self.ops = [sem(n + f"ops{u}") for u in range(UNITS)]
                self.maxrow = [sem(n + f"maxrow{u}") for u in range(UNITS)]
                self.side = sem(n + "side")
                self.side_out = sem(n + "side_out")
                self.nmp = sem(n + "nmp")
                self.scores = sem(n + "scores")
                self.exps = sem(n + "exps")
                self.pv = sem(n + "pv")
                self.o_out = sem(n + "o_out")
                self.s_out = sem(n + "s_out")
                self.rs = sem(n + "rs")
                self.on = sem(n + "on")
                self.gelu = sem(n + "gelu")
                self.final = sem(n + "final")
                self.x = sem(n + "x")

        at = [Attn(0), Attn(1)]
        v_ones, tables, sel_ready = sem("v_ones"), sem("tables"), sem("sel_ready")
        sq_ready, ss_ready, ss_cl = sem("sq_ready"), sem("ss_ready"), sem("ss_cl")
        norm_ready, factors, factors_used = sem("norm_ready"), sem("factors"), sem("factors_used")
        t_sum, t_inv, t_parts, t_ps, t_row, t_krow = (sem("t_" + n) for n in (
            "sum", "inv", "parts", "ps", "row", "krow"))
        hyp_mx, hyp_s = sem("hyp_mx"), sem("hyp_s")
        h_prod, h_arg, h_sq, h_root, h_sum, h_score, h_sub, h_exp, h_pv = (
            sem("h_" + n) for n in ("prod", "arg", "sq", "root", "sum", "score", "sub", "exp", "pv"))
        y_turn, y_T = sem("y_turn"), sem("y_T")

        class FfnSems:
            def __init__(self, l):
                n = f"f{l}_"
                self.logits, self.score = sem(n + "logits"), sem(n + "score")
                self.parts, self.gps, self.gates = sem(n + "parts"), sem(n + "gps"), sem(n + "gates")
                self.up, self.act, self.hid, self.down = (
                    sem(n + "up"), sem(n + "act"), sem(n + "hid"), sem(n + "down"))
                self.shared, self.ucopy = sem(n + "shared"), sem(n + "ucopy")
                self.x = sem(n + "x")

        fs = [FfnSems(0), FfnSems(1)]

        x_for = [x_ready, at[0].x, fs[0].x, at[1].x]

        def chunk(t, c):
            return t[:, c * CH:(c + 1) * CH]

        def tensor_program(pe):
            def turn_tiles(src, bank, done, first=None):
                for t in range(NT):
                    if first:
                        first(t)
                    mm = pe.transpose(ps[:, bank + t // 4, (t % 4) * P:(t % 4 + 1) * P], src(t), w["ident"][:])
                    if t % 4 == 3:
                        mm.then_inc(done, 1)

            def layer_norm(n):
                turn_tiles(lambda t: xT[:, t * P:(t + 1) * P], 0, ln_tok[n],
                           lambda t: pe.wait_ge(x_for[n], t // 4 + 1))
                turn_tiles(lambda t: xn[:, t, :], 2, ln_back[n],
                           lambda t: pe.wait_ge(ln_norm[n], t + 1))

            def project(wt, c, bank, done):
                pe.matmul(ps[:, bank, :], wt, chunk(hT, c), start=True, stop=True).then_inc(done, 1)

            def attention(l):
                a = at[l]
                if l == 0:
                    for c in range(NC):
                        pe.wait_ge(h_ready[0], c + 1)
                        project(w["wk"][:], c, 4 + c, a.proj)
                    for t in range(NT):
                        if t >= 2:
                            pe.wait_ge(a.v, t - 1)
                        pe.matmul(ps[:, 6 + t % 2, :], hT[:, t * P:(t + 1) * P], w["wv"][:],
                                  start=True, stop=True).then_inc(a.vps, 1)
                else:
                    for i, (n0, n1) in enumerate((("q", "qs"), ("k", "ks"))):
                        for c in range(NC):
                            if i:
                                pe.wait_ge(a.proj_used, c + 1)
                            else:
                                pe.wait_ge(h_ready[2], c + 1)
                            project(w[n0][:], c, 4 + c, a.proj)
                            project(w[n1][:], c, 6 + c, a.proj)
                    for i in range(2):
                        for c in range(NC):
                            pe.wait_ge(sq_ready, 2 * i + c + 1)
                            if i:
                                pe.wait_ge(ss_cl, c + 1)
                            pe.matmul(ps[:, c, :], w["heads8"][:], rsb[:, c, :], start=True, stop=True)
                            for t in range(4):
                                col = (i * NT + 4 * c + t) * 4
                                mm = pe.matmul(ps[:, 2, col:col + 4], rsb[:, c, t * P:(t + 1) * P], w["hsel"][:],
                                               start=True, stop=True)
                            mm.then_inc(ss_ready, 1)
                    for t in range(NT):
                        if t == 0:
                            pe.wait_ge(a.proj_used, 4)
                        mm = pe.matmul(ps[:, 4 + t // 4, (t % 4) * P:(t % 4 + 1) * P], hT[:, t * P:(t + 1) * P],
                                       w["v"][:], start=True, stop=True)
                        if t % 4 == 3:
                            mm.then_inc(a.vps, 1)
                    pe.wait_ge(t_parts, 1)
                    for side in range(2):
                        for t in range(NT):
                            mm = pe.matmul(ps[0:36, (6 if side else 2) + t // 4, (t % 4) * P:(t % 4 + 1) * P],
                                           tp9[:, t, side], identb[:], start=True, stop=True)
                        mm.then_inc(t_ps, 1)

                def side_job(kind, g, what):
                    if g == 0:
                        pe.wait_ge(a.v if l == 0 else a.proj_used, NT if l == 0 else 4)
                    elif g >= side_ring(l, g):
                        pe.wait_ge(a.side_out, g - side_ring(l, g) + 1)
                    bank = side_bank(l, g)
                    if kind == "piece":
                        u, j, p = what
                        qb, k0, wd, _ = PIECES[p]
                        if (j, p) == (0, 0):
                            pe.wait_ge(a.ops[u], OPS_HYP if is_hyp(l, u) else OPS)
                        k = K_HYP if is_hyp(l, u) else PAIRS
                        o = ps[:, bank, 0:wd]
                        diag = k0 + wd == (qb + 1) * P
                        mm = pe.matmul(o, qop[0:k, slot(l, u), j, qb * P:(qb + 1) * P],
                                       kop[0:k, slot(l, u), j, k0:k0 + wd], start=True, stop=not diag)
                        if diag:
                            mm = pe.matmul(o[:, wd - P:wd], identb[:], maskqk[:], start=False, stop=True)
                    elif kind == "max":
                        pe.wait_ge(a.nmp, MAXES[l].index(what) + 1)
                        mm = pe.matmul(ps[0:96, bank, 0:P], nmp[:], identb[:], start=True, stop=True)
                    elif kind == "spread":
                        c, j = what
                        if j == 0:
                            pe.wait_ge(a.side_out, side_count(l, "max", (HYP_UNIT, (c,))))
                        for q in range(4):
                            mm = pe.matmul(ps[:, bank, q * P:(q + 1) * P], sel32[:, NT * j + 4 * c + q, :],
                                           mrow[:], start=True, stop=True)
                    else:
                        i = what[0]
                        pe.wait_ge(a.o_out, i + 1)
                        for t in range(4):
                            mm = pe.transpose(ps[:, bank, t * P:(t + 1) * P], osb[:, i % 2, t * P:(t + 1) * P],
                                              w["ident"][:])
                    mm.then_inc(a.side, 1)

                score_job = [0]

                def take_banks():
                    n = score_job[0]
                    score_job[0] += 1
                    if n == 0:
                        pe.wait_ge(h_ready[2 * l], NC)
                        if l:
                            pe.wait_ge(t_row, 1)
                            pe.wait_ge(t_krow, 1)
                    if n >= 2:
                        hyperbolic, i, pair = JOBS[l][n - 2]
                        if hyperbolic:
                            pe.wait_ge(h_arg, i + 1)
                        else:
                            pe.wait_ge(a.exps, 2 * i + pair + 1)
                    return 2 * (n % 2)

                def scores(g, extra):
                    u, s = divmod(g, NS)
                    c, kb, q0, wd, diag = STEPS[s]
                    k = K_MAX if has_max(l, u) else PAIRS
                    o0 = q0 - c * CH
                    if s == 0:
                        if has_max(l, u):
                            pe.wait_ge(a.maxrow[u], 48)
                        else:
                            pe.wait_ge(a.ops[u], OPS)
                    for pair in range(2):
                        bank = take_banks()
                        for j in range(2):
                            o = ps[:, bank + j, o0:o0 + wd]
                            mm = pe.matmul(o, kop[0:k, slot(l, u), 2 * pair + j, kb * P:(kb + 1) * P],
                                           qop[0:k, slot(l, u), 2 * pair + j, q0:q0 + wd], start=True, stop=not diag)
                            if diag:
                                mm = pe.matmul(o[:, 0:P], identb[:], maskkq[:], start=False, stop=True)
                            if j == 0 and extra and pair:
                                side_job(*extra.pop(0))
                        mm.then_inc(a.scores, 1)
                        if extra:
                            side_job(*extra.pop(0))

                def hyp_scores(k):
                    c, kb, q0, wd, diag = STEPS[k // 2]
                    o0 = q0 - c * CH
                    if k == 0:
                        pe.wait_ge(a.ops[HYP_UNIT], OPS_HYP)
                    bank = take_banks()
                    for j in range(2):
                        mm = pe.matmul(ps[:, bank + j, o0:o0 + wd],
                                       kop[0:K_HYP, slot(l, HYP_UNIT), 2 * (k % 2) + j, kb * P:(kb + 1) * P],
                                       qop[0:K_HYP, slot(l, HYP_UNIT), 2 * (k % 2) + j, q0:q0 + wd],
                                       start=True, stop=True)
                    mm.then_inc(h_prod, 1)

                def out_before(u, c):
                    same = [i for i, (_, v, d) in enumerate(OUTS[l]) if is_hyp(l, v) == is_hyp(l, u)
                            and (v, d) < (u, c)]
                    return max(same, default=-1) + 1

                def values(g, extra):
                    u, s = divmod(g, NS)
                    c, kb, q0, wd, _ = STEPS[s]
                    o0 = q0 - c * CH
                    last = kb == 4 * c + 3
                    pe.wait_ge(a.exps, 2 * (g + 1))
                    if kb == 0:
                        if g == 0:
                            pe.wait_ge(a.v, NT if l == 0 else 2)
                        else:
                            pe.wait_ge(a.o_out, out_before(u, c))
                            if l == 0:
                                pe.wait_ge(a.s_out, NC * u + c)
                    for j in range(4):
                        h = 4 * u + j
                        mm = pe.matmul(ps[32 * j:32 * j + 32, 4, o0:o0 + wd], vt[:, kb, 32 * h:32 * h + 32],
                                       pr[:, g % 3, j, o0:o0 + wd], start=kb == 0, stop=last,
                                       tile_position=(0, 32 * j))
                        if l and j == 3:
                            mm.then_inc(a.pv, 1)
                        if j % 2 and extra:
                            side_job(*extra.pop(0))
                    if l == 0:
                        for j in range(4):
                            mm = pe.matmul(ps[32 * j:32 * j + 32, 5, o0:o0 + wd], ones32[:],
                                           pr[:, g % 3, j, o0:o0 + wd], start=kb == 0, stop=last,
                                           tile_position=(0, 32 * j))
                        mm.then_inc(a.pv, 1)

                def hyp_values(k):
                    c, kb, q0, wd, _ = STEPS[k // 2]
                    o0 = q0 - c * CH
                    pe.wait_ge(h_exp, k + 1)
                    if kb == 0 and c and k % 2 == 0:
                        pe.wait_ge(a.o_out, out_before(HYP_UNIT, c))
                    z = hyp_z(k)
                    for i in range(2):
                        j = 2 * (k % 2) + i
                        h = 4 * HYP_UNIT + j
                        mm = pe.matmul(ps[32 * j:32 * j + 32, 5, o0:o0 + wd], vt[:, kb, 32 * h:32 * h + 32],
                                       z[:, i], start=kb == 0, stop=kb == 4 * c + 3, tile_position=(0, 32 * j))
                    mm.then_inc(h_pv, 1)

                def jobs_at(p):
                    return [x for x in SIDE[l][p] if x[0] != "maxima"]

                for x in jobs_at(-1):
                    side_job(*x)
                steps = STD_UNITS[l] * NS
                scores(0, [])
                for p in range(POSITIONS[l] + 1):
                    extra = jobs_at(p)
                    if p + 1 < steps:
                        scores(p + 1, extra)
                    if p < steps:
                        values(p, extra)
                    if l and 0 <= p - HYP_AT - 3 < HYP_HALVES:
                        hyp_values(p - HYP_AT - 3)
                    for x in extra:
                        side_job(*x)
                    if l and 0 <= p - HYP_AT < HYP_HALVES:
                        hyp_scores(p - HYP_AT)
                if l:
                    turns = [side_count(l, "turn", (i, u, c)) for i, (_, u, c) in enumerate(OUTS[l])]
                    for t in range(NT):
                        pe.wait_ge(a.side_out, max(n for n, x in zip(turns, OUTS[l]) if x[2] == t // 4))
                        mm = pe.transpose(ps[:, t // 4, (t % 4) * P:(t % 4 + 1) * P], kT[:, t * P:(t + 1) * P],
                                          w["ident"][:])
                        if t % 4 == 3:
                            mm.then_inc(y_turn, 1)
                    for c in range(NC):
                        pe.wait_ge(y_T, c + 1)
                        pe.matmul(ps[:, 2 + c, :], w["proj"][:], chunk(hT, c), start=True,
                                  stop=True).then_inc(a.final, 1)
                else:
                    pe.wait_ge(a.exps, 2 * NS * UNITS)
                    for c in range(NC):
                        for u in range(UNITS):
                            pe.wait_ge(a.gelu, UNITS * c + u + 1)
                            mm = pe.matmul(ps[:, c, :], w["wf"][:, u, :], on[:, u, c * CH:(c + 1) * CH],
                                           start=u == 0, stop=u == UNITS - 1)
                        mm.then_inc(a.final, 1)

            def ffn(l):
                f, g = FFN[l], fs[l]
                E = f.experts
                for t in range(NT):
                    pe.wait_ge(h_ready[2 * l + 1], t // 4 + 1)
                    mm = pe.matmul(ps[:, 7, t * E:(t + 1) * E], hT[:, t * P:(t + 1) * P], w[f"router{l}"][:],
                                   start=True, stop=True)
                mm.then_inc(g.logits, 1)

                def gates(c, bank):
                    pe.wait_ge(g.parts, c + 1)
                    for t in range(4):
                        mm = pe.matmul(ps[0:3 * E, bank, t * P:(t + 1) * P], gp[:, 4 * c + t, 0:3 * E],
                                       identb[:], start=True, stop=True)
                    mm.then_inc(g.gps, 1)

                def hidden_ready(i):
                    if 0 <= i < 2 * NC:
                        pe.wait_ge(g.shared, i + 1)
                    elif i >= 0:
                        pe.wait_ge(g.hid, i + 1 - 2 * NC)

                def up(i):
                    kind, e, c = f.work[i]
                    hidden_ready(i - 2)
                    h = chunk(hT, c)
                    if kind == "shared":
                        pe.matmul(ps[:, 2 + i % 2, :], w[f"shg{l}"][:, e * P:(e + 1) * P], h, start=True, stop=True)
                        mm = pe.matmul(ps[:, 4 + i % 2, :], w[f"shu{l}"][:, e * P:(e + 1) * P], h,
                                       start=True, stop=True)
                    else:
                        if i in f.first:
                            gates(c, 6 + i % 2)
                        pe.matmul(ps[:, 2 + i % 2, :], w[f"gate{l}"][:, e, :], h, start=True, stop=True)
                        if f.gated:
                            pe.matmul(ps[:, 4 + i % 2, :], w["up1"][:, e, :], h, start=True, stop=True)
                        if i in f.first:
                            pe.wait_ge(g.gates, c + 1)
                            pe.wait_ge(sel_ready, l + 1)
                        mm = pe.matmul(ps[:, 6 + i % 2, :], selg(E)[:, e, :], chunk(gT, c)[0:3 * E],
                                       start=True, stop=True)
                    mm.then_inc(g.up, 1)

                def down(i):
                    kind, e, c = f.work[i]
                    hidden_ready(i)
                    wt = w[f"shd{l}"][:, e, :] if kind == "shared" else w[f"down{l}"][:, e, :]
                    pe.matmul(ps[:, c, :], wt, fh[:, i % 2, :], start=i < NC,
                              stop=i == f.last[c]).then_inc(g.down, 1)

                up(0)
                up(1)
                for i in range(len(f.work)):
                    down(i)
                    if i + 2 < len(f.work):
                        up(i + 2)

            pe.wait_ge(x_in, 16)
            turn_tiles(lambda t: xn[:, t, :], 0, x_tok)
            for l in range(2):
                layer_norm(2 * l)
                attention(l)
                layer_norm(2 * l + 1)
                ffn(l)
            turn_tiles(lambda t: xT[:, t * P:(t + 1) * P], 2, s_out_tok, lambda t: pe.wait_ge(fs[1].x, t // 4 + 1))

        def scalar_program(act):
            chain = [0]

            def exp_tables():
                nc.scalar.preload_act_table_set("natural_log_exp_and_others")

            def link(i):
                chain[0] += 1
                i.then_inc(act_chain, 1)
                act.wait_ge(act_chain, chain[0])

            def layer_norm(n):
                l, j = n // 2, 3 * (n % 2)
                exp_tables()
                for c in range(NC):
                    y = sd[:, 0, 4 * c:4 * c + 4]
                    act.wait_ge(ln_var[n], c + 1)
                    link(nc.scalar.activation(y, mv[:, 4 * c:4 * c + 4, 1], ACT.Ln, bias=consts[:, 0:1]))
                    nc.scalar.activation(y, y, ACT.Exp, scale=-0.5).then_inc(ln_std[n], 1)
                if n == 0:
                    act.wait_ge(mod_ready, 1)
                for c in range(NC):
                    act.wait_ge(ln_back[n], c + 1)
                    nc.scalar.activation(chunk(hT, c), ps[:, 2 + c, :], ACT.Identity, scale=modb[:, l, j + 1:j + 2],
                                         bias=modb[:, l, j:j + 1]).then_inc(h_ready[n], 1)

            def prepare(l):
                a = at[l]
                if l == 0:
                    for c in range(NC):
                        act.wait_ge(a.proj, c + 1)
                        nc.scalar.activation(chunk(kT, c), ps[:, 4 + c, :], ACT.Identity,
                                             bias=cols[:, C_BK:C_BK + 1]).then_inc(a.proj_used, 1)
                    for t in range(NT):
                        act.wait_ge(a.vps, t + 1)
                        nc.scalar.copy(vt[:, t, :], ps[:, 6 + t % 2, :]).then_inc(a.v, 1)
                    return
                for i, src in enumerate((on[:, 0, :], kT[:])):
                    for c in range(NC):
                        act.wait_ge(norm_ready, 2 * i + c + 1)
                        if i:
                            act.wait_ge(ss_ready, c + 1)
                        nc.scalar.activation(rsb[:, c, :], chunk(src, c), ACT.Square).then_inc(sq_ready, 1)
                    for c in range(NC):
                        act.wait_ge(ss_cl, 2 * i + c + 1)
                        r = chunk(on[:, 2, :], c)
                        if i:
                            act.wait_ge(factors_used, 1)
                        link(nc.scalar.activation(r, chunk(on[:, 1, :], c), ACT.Ln))
                        nc.scalar.activation(r, r, ACT.Exp, scale=-0.5).then_inc(factors, 1)
                act.wait_ge(t_sum, 1)
                link(nc.scalar.activation(tR, tA, ACT.Ln))
                nc.scalar.activation(tR, tR, ACT.Exp, scale=-0.5).then_inc(t_inv, 1)
                act.wait_ge(t_ps, 2)
                nc.scalar.copy(trow[1].rearrange("p (a b) -> p a b", a=2), ps[0:36, 6:8, :]).then_inc(t_krow, 1)

            def attention(l):
                a = at[l]

                def sums_out(u, c):
                    i = NC * u + c
                    act.wait_ge(a.pv, NS * u + 4 + 8 * c)
                    if i >= 2:
                        act.wait_ge(a.on, i - 1)
                    nc.scalar.activation(rsb[:, i % 2, :], ps[:, 5, :], ACT.Ln).then_inc(a.s_out, 1)
                    act.wait_ge(a.s_out, i + 1)
                    nc.scalar.activation(rsb[:, i % 2, :], rsb[:, i % 2, :], ACT.Exp, scale=-1.0).then_inc(a.rs, 1)

                def hyp_max(c):
                    z = nr[:, 0, :].rearrange("p (j q) -> p j q", q=NT)[:, :, 4 * c:4 * c + 4]
                    act.wait_ge(hyp_mx, 2 * c + 1)
                    link(nc.scalar.activation(z, z, ACT.Ln))
                    nc.scalar.activation(z, z, ACT.Exp, scale=0.5).then_inc(hyp_s, 1)
                    act.wait_ge(hyp_mx, 2 * c + 2)
                    link(nc.scalar.activation(z, z, ACT.Ln, bias=consts[:, 1:2]))
                    for j in range(4):
                        ins_ = nc.scalar.activation(z[:, j], z[:, j], ACT.Ln, scale=hyp[:, 4 + j:5 + j],
                                                    bias=consts[:, 2:3])
                    link(ins_)
                    nc.scalar.activation(z, z, ACT.Exp, scale=-1.0).then_inc(hyp_s, 1)

                def hyp_root(k):
                    z = hyp_z(k)
                    act.wait_ge(h_sq, k + 1)
                    link(nc.scalar.activation(z, z, ACT.Ln))
                    nc.scalar.activation(z, z, ACT.Exp, scale=0.5).then_inc(h_root, 1)

                def hyp_score(k):
                    z = hyp_z(k)
                    act.wait_ge(h_sum, k + 1)
                    link(nc.scalar.activation(z, z, ACT.Ln, bias=consts[:, 1:2]))
                    for i in range(2):
                        j = 2 * (k % 2) + i
                        ins_ = nc.scalar.activation(z[:, i], z[:, i], ACT.Ln, scale=hyp[:, 4 + j:5 + j],
                                                    bias=consts[:, 2:3])
                    link(ins_)
                    nc.scalar.activation(z, z, ACT.Exp, scale=-1.0).then_inc(h_score, 1)

                def hyp_exp(k):
                    z = hyp_z(k)
                    act.wait_ge(h_sub, k + 1)
                    nc.scalar.activation(z, z, ACT.Exp).then_inc(h_exp, 1)

                def std_exp(g):
                    u, s = divmod(g, NS)
                    c, kb, q0, wd, _ = STEPS[s]
                    o0 = q0 - c * CH
                    for pair in range(2):
                        bank = 2 * (JOBS[l].index((False, g, pair)) % 2)
                        act.wait_ge(a.scores, 2 * g + pair + 1)
                        if g >= 3:
                            act.wait_ge(a.pv, g - 2)
                        nc.scalar.activation(pr[:, g % 3, 2 * pair:2 * pair + 2, o0:o0 + wd],
                                             ps[:, bank:bank + 2, o0:o0 + wd], ACT.Exp).then_inc(a.exps, 1)

                steps = STD_UNITS[l] * NS
                for p in range(POSITIONS[l]):
                    if p < steps:
                        std_exp(p)
                    if l:
                        k = p - HYP_AT
                        if 0 <= k - 3 < HYP_HALVES:
                            hyp_exp(k - 3)
                        if 0 <= k - 2 < HYP_HALVES:
                            hyp_score(k - 2)
                        if 0 <= k - 1 < HYP_HALVES:
                            hyp_root(k - 1)
                        for c in range(NC):
                            if ("maxima", None, (HYP_UNIT, (c,))) in SIDE[l][p]:
                                hyp_max(c)
                    else:
                        u, s = divmod(p, NS)
                        if s == 4:
                            sums_out(u, 0)
                        if s == 0 and u:
                            sums_out(u - 1, 1)
                if l == 0:
                    sums_out(UNITS - 1, 1)
                    for c in range(NC):
                        for u in range(UNITS):
                            act.wait_ge(a.on, NC * u + c + 1)
                            nc.scalar.activation(chunk(on[:, u, :], c), chunk(on[:, u, :], c), ACT.Gelu,
                                                 bias=cols[:, C_BV + u:C_BV + u + 1]).then_inc(a.gelu, 1)
                else:
                    for c in range(NC):
                        act.wait_ge(y_turn, c + 1)
                        nc.scalar.copy(chunk(hT, c), ps[:, c, :]).then_inc(y_T, 1)

            def ffn(l):
                f, g = FFN[l], fs[l]
                E = f.experts
                act.wait_ge(g.logits, 1)
                nc.scalar.activation(lg[:, 0, :, 0:E], ps[:, 7, 0:NT * E].rearrange("p (t e) -> p t e", e=E),
                                     ACT.Exp, scale=-1.0).then_inc(g.score, 1)
                for i, (kind, e, c) in enumerate(f.work):
                    if i in f.first:
                        act.wait_ge(g.gps, c + 1)
                        nc.scalar.copy(chunk(gT, c)[0:3 * E], ps[0:3 * E, 6 + i % 2, :]).then_inc(g.gates, 1)
                    act.wait_ge(g.up, i + 1)
                    if 2 <= i < 2 * NC + 2:
                        act.wait_ge(g.shared, i - 1)
                    elif i >= 2:
                        act.wait_ge(g.hid, i - 1 - 2 * NC)
                    fn = ACT.Silu if l or kind == "shared" else ACT.Gelu
                    nc.scalar.activation(fa[:, i % 2, :], ps[:, 2 + i % 2, :], fn).then_inc(g.act, 1)
                    if kind == "shared":
                        nc.scalar.copy(ft[:, i % 2, :], ps[:, 4 + i % 2, :]).then_inc(g.ucopy, 1)

            for l in range(2):
                layer_norm(2 * l)
                prepare(l)
                attention(l)
                layer_norm(2 * l + 1)
                ffn(l)

        def vector_program(dve):
            chain = [0]

            def link(i):
                chain[0] += 1
                i.then_inc(dve_chain, 1)
                dve.wait_ge(dve_chain, chain[0])

            def layer_norm(n):
                def tile(t):
                    return ps[:, t // 4, (t % 4) * P:(t % 4 + 1) * P]

                for c in range(NC):
                    dve.wait_ge(ln_tok[n], c + 1)
                    for t in range(4 * c, 4 * c + 4):
                        ins_ = nc.vector.bn_stats(st[:, t, :], tile(t))
                    link(ins_)
                    for t in range(4 * c, 4 * c + 4):
                        ins_ = nc.vector.bn_aggr(mv[:, t, :], st[:, t, :])
                    ins_.then_inc(ln_var[n], 1)
                for c in range(NC):
                    y, z, v = sd[:, 0, 4 * c:4 * c + 4], sd[:, 1, 4 * c:4 * c + 4], mv[:, 4 * c:4 * c + 4, 1]
                    dve.wait_ge(ln_std[n], c + 1)
                    link(nc.vector.tensor_tensor(z, y, y, ALU.mult))
                    link(nc.vector.scalar_tensor_tensor(out=z, in0=v, scalar=LN_EPS, in1=z, op0=ALU.add,
                                                        op1=ALU.mult))
                    link(nc.vector.tensor_scalar(z, z, -0.5, 1.5, ALU.mult, ALU.add))
                    link(nc.vector.tensor_tensor(z, z, y, ALU.mult))
                    for t in range(4 * c, 4 * c + 4):
                        nc.vector.tensor_scalar(xn[:, t, :], tile(t), mv[:, t, 0:1], sd[:, 1, t:t + 1],
                                                ALU.subtract, ALU.mult).then_inc(ln_norm[n], 1)

            def split(src, dst, r):
                link(nc.vector.tensor_copy(dst(0), src))
                link(nc.vector.tensor_tensor(r, src, dst(0), ALU.subtract))
                link(nc.vector.tensor_copy(dst(1), r))
                return nc.vector.tensor_tensor(dst(2), r, dst(1), ALU.subtract)

            def operand_parts(l, side, src):
                done, p = at[l].parts, parts[:, side]
                nc.vector.tensor_copy(p[:, 0, :], src).then_inc(done, 1)
                dve.wait_ge(done, 3 * side + 1)
                link(nc.vector.tensor_tensor(tmp, src, p[:, 0, :], ALU.subtract))
                nc.vector.tensor_copy(p[:, 1, :], tmp).then_inc(done, 1)
                dve.wait_ge(done, 3 * side + 2)
                nc.vector.tensor_tensor(p[:, 2, :], tmp, p[:, 1, :], ALU.subtract).then_inc(done, 1)
                dve.wait_ge(done, 3 * side + 3)

            def prepare(l):
                a = at[l]
                if l == 0:
                    dve.wait_ge(h_ready[0], NC)
                    operand_parts(0, 0, hT[:])
                    dve.wait_ge(a.proj_used, NC)
                    operand_parts(0, 1, kT[:])
                    return
                q0, q1 = on[:, 0, :], on[:, 1, :]
                dsts = (q0, kT[:])
                dve.wait_ge(tables, 32)
                for i in range(2):
                    for c in range(NC):
                        dve.wait_ge(a.proj, 4 * i + 2 * c + 2)
                        nc.vector.tensor_tensor(chunk(dsts[i], c), ps[:, 4 + c, :], chunk(cos, c), ALU.mult)
                        ins_ = nc.vector.tensor_tensor(chunk(tmp, c), ps[:, 6 + c, :], chunk(sin, c), ALU.mult)
                        ins_.then_inc(a.proj_used, 1)
                        dve.wait_ge(a.proj_used, 2 * i + c + 1)
                        nc.vector.tensor_tensor(chunk(dsts[i], c), chunk(dsts[i], c), chunk(tmp, c),
                                                ALU.add).then_inc(norm_ready, 1)
                for i in range(2):
                    for c in range(NC):
                        dve.wait_ge(ss_ready, 2 * i + c + 1)
                        if i:
                            dve.wait_ge(factors_used, 1)
                        nc.vector.tensor_scalar(chunk(q1, c), ps[:, c, :], 1e-24, None, ALU.max).then_inc(ss_cl, 1)
                    dve.wait_ge(factors, 2 * i + 2)
                    F = on[:, 2, :]
                    link(nc.vector.tensor_scalar(F, F, cols[:, C_COS:C_COS + 1], cols[:, C_NOTCOS:C_NOTCOS + 1],
                                                 ALU.mult, ALU.add))
                    if i == 0:
                        ins_ = nc.vector.scalar_tensor_tensor(out=q0, in0=q0, scalar=cols[:, C_QS:C_QS + 1], in1=F,
                                                              op0=ALU.mult, op1=ALU.mult)
                    else:
                        ins_ = nc.vector.tensor_tensor(kT[:], kT[:], F, ALU.mult)
                    ins_.then_inc(factors_used, 1)
                    dve.wait_ge(factors_used, i + 1)
                    operand_parts(1, i, dsts[i])
                nc.vector.tensor_tensor(tA.rearrange("p (n h) -> p n h", h=4),
                                        ps[:, 2, 0:64].rearrange("p (n h) -> p n h", h=4),
                                        hyp[:, 0:4].unsqueeze(1).broadcast_to([P, 16, 4]), ALU.add).then_inc(t_sum, 1)
                dve.wait_ge(t_inv, 1)
                link(nc.vector.tensor_tensor(tT, tA, tR, ALU.mult))
                link(nc.vector.tensor_tensor(tU, tT, tT, ALU.mult))
                link(nc.vector.tensor_tensor(tU, tA, tU, ALU.subtract))
                link(nc.vector.scalar_tensor_tensor(out=tU, in0=tU, scalar=0.5, in1=tR, op0=ALU.mult, op1=ALU.mult))
                link(nc.vector.tensor_tensor(tT, tT, tU, ALU.add))
                tq = tT[:, 0:32].rearrange("p (n h) -> p n h", h=4)
                link(nc.vector.tensor_scalar(tq, tq, -1.0, None, ALU.mult))
                link(nc.vector.tensor_tensor(tq, tq, curvb[:].unsqueeze(1).broadcast_to([P, NT, 4]), ALU.mult))

                def by_tile(x):
                    return x.rearrange("p (s t h) -> p t s h", s=2, t=NT)

                link(split(by_tile(tT), lambda k: tp[:, :, :, k, :], by_tile(tU)))
                q9, k9 = (tp9[:, :, side].rearrange("p t (i j h) -> p t i j h", i=3, j=3) for side in range(2))
                for i in range(3):
                    nc.vector.tensor_copy(q9[:, :, i], tp[:, :, 0])
                    ins_ = nc.vector.tensor_copy(k9[:, :, i], tp[:, :, 1, i].unsqueeze(2).broadcast_to([P, NT, 3, 4]))
                ins_.then_inc(t_parts, 1)
                dve.wait_ge(t_ps, 1)
                nc.vector.tensor_copy(trow[0].rearrange("p (a b) -> p a b", a=2), ps[0:36, 2:4, :]).then_inc(t_row, 1)
                dve.wait_ge(v_ones, 1)
                for c in range(NC):
                    dve.wait_ge(a.vps, c + 1)
                    for t in range(4):
                        ins_ = nc.vector.tensor_copy(
                            vt[:, 4 * c + t, :].rearrange("p (h e) -> p h e", e=32)[:, :, 0:HD],
                            ps[:, 4 + c, t * P:(t + 1) * P].rearrange("p (h e) -> p h e", e=HD))
                    ins_.then_inc(a.v, 1)

            def attention(l):
                a = at[l]

                def maxima(u, chunks):
                    n, k = nth(l, u), len(max_heads(l, u))
                    lo, hi = 4 * chunks[0], 4 * chunks[-1] + 4

                    def of(t):
                        return t.rearrange("p (j q) -> p j q", q=NT)[:, :, lo:hi]

                    m3 = nm[:, n % 2, :].rearrange("p (j q) -> p j q", q=NT)
                    m, z, x = of(nm[:, n % 2, :]), of(nr[:, 0, :]), of(nr[:, 1, :])
                    x2 = mx[:, n % 2]
                    last = max(p for p in range(NP_) if PIECES[p][0] < hi)
                    dve.wait_ge(a.side_out, max(side_count(l, "piece", (u, j, last)) for j in max_heads(l, u)))
                    if k < 4:
                        nc.vector.memset(m3[:, k:4, :], 0.0)
                    if 0 in chunks:
                        ins_ = nc.vector.tensor_copy(m3[:, 0:k, 0:4], x2[:, 0:k, 0:4, 0])
                    if 1 in chunks:
                        ins_ = nc.vector.tensor_tensor(m3[:, 0:k, 4:NT], x2[:, 0:k, 4:NT, 0], x2[:, 0:k, 4:NT, 1],
                                                       ALU.min)
                    link(ins_)
                    if is_hyp(l, u):
                        c = chunks[0]
                        link(nc.vector.tensor_scalar(x, m, ARG_GAP, None, ALU.max))
                        nc.vector.scalar_tensor_tensor(out=z, in0=x, scalar=2.0, in1=x, op0=ALU.add,
                                                       op1=ALU.mult).then_inc(hyp_mx, 1)
                        dve.wait_ge(hyp_s, 2 * c + 1)
                        nc.vector.tensor_tensor(z, z, x, ALU.add).then_inc(hyp_mx, 1)
                        dve.wait_ge(hyp_s, 2 * c + 2)
                        link(nc.vector.tensor_scalar(m, z, -1.0, None, ALU.mult))
                    i = MAXES[l].index((u, chunks))
                    if i:
                        dve.wait_ge(a.side, side_count(l, "max", MAXES[l][i - 1]))
                    if chunks != BOTH:
                        link(nc.vector.memset(nmp[:], 0.0))
                    split(m, lambda k: of(nmp[:, 32 * k:32 * k + 32]), x).then_inc(a.nmp, 1)

                def side_job(kind, g, what):
                    if kind == "maxima":
                        maxima(*what)
                        return
                    dve.wait_ge(a.side, g + 1)
                    bank = side_bank(l, g)
                    if kind == "piece":
                        u, j, p = what
                        qb, k0, wd, col = PIECES[p]
                        ins_ = nc.vector.tensor_reduce(mx[:, nth(l, u) % 2, j, qb, col % 2:col % 2 + 1],
                                                       ps[:, bank, 0:wd], AX.X, ALU.max, negate=True)
                    elif kind == "max":
                        i = MAXES[l].index(what)
                        if i:
                            v, chunks = MAXES[l][i - 1]
                            if is_hyp(l, v):
                                dve.wait_ge(a.side, side_count(l, "spread", (chunks[-1], 3)))
                            else:
                                dve.wait_ge(a.maxrow[v], 48)
                        ins_ = nc.vector.tensor_copy(mrow[:], ps[0:96, bank, 0:P])
                    elif kind == "spread":
                        c, j = what
                        ins_ = nc.vector.tensor_copy(nbc[:, j, c * CH:(c + 1) * CH], ps[:, bank, :])
                    else:
                        i, u, c = what
                        if i:
                            dve.wait_ge(a.side_out, side_count(l, "turn", (i - 1,) + OUTS[l][i - 1][1:]))
                        o = ps[:, bank, :].rearrange("p (t j e) -> p t j e", t=4, j=4)
                        link(nc.vector.reciprocal(rec[:], o[:, :, :, HD]))
                        y = kT[:].rearrange("p (t u j e) -> p t u j e", t=NT, u=UNITS, j=4)
                        for j in range(4):
                            ins_ = nc.vector.tensor_tensor(y[:, 4 * c:4 * c + 4, u, j, :], o[:, :, j, 0:HD],
                                                           rec[:, :, j:j + 1].broadcast_to([P, 4, HD]), ALU.mult)
                    ins_.then_inc(a.side_out, 1)

                def outputs_out(i):
                    _, u, c = OUTS[l][i]
                    if is_hyp(l, u):
                        dve.wait_ge(h_pv, 2 * (4 + 8 * c))
                    else:
                        dve.wait_ge(a.pv, NS * u + 4 + 8 * c)
                    if i >= 2:
                        if l:
                            dve.wait_ge(a.side, side_count(l, "turn", (i - 2,) + OUTS[l][i - 2][1:]))
                        else:
                            dve.wait_ge(a.on, i - 1)
                    nc.vector.tensor_copy(osb[:, i % 2, :], ps[:, 5 if is_hyp(l, u) else 4, :]).then_inc(a.o_out, 1)

                def hyp_arg(k):
                    c, kb, q0, wd, _ = STEPS[k // 2]
                    o0 = q0 - c * CH
                    bank = 2 * (JOBS[l].index((True, k, k % 2)) % 2)
                    if k >= 2:
                        dve.wait_ge(h_sum, k - 1)
                    dve.wait_ge(h_prod, k + 1)
                    nc.vector.tensor_scalar(hyp_x(k), ps[:, bank:bank + 2, o0:o0 + wd], -1.0, ARG_GAP, ALU.mult,
                                            ALU.max).then_inc(h_arg, 1)
                    dve.wait_ge(h_arg, k + 1)
                    if k >= HYP_RING:
                        dve.wait_ge(h_pv, k - HYP_RING + 1)
                    nc.vector.scalar_tensor_tensor(out=hyp_z(k), in0=hyp_x(k), scalar=2.0, in1=hyp_x(k), op0=ALU.add,
                                                   op1=ALU.mult).then_inc(h_sq, 1)

                def hyp_shift(k):
                    c, kb, q0, wd, diag = STEPS[k // 2]
                    z, j0 = hyp_z(k), 2 * (k % 2)
                    dve.wait_ge(a.side_out, side_count(l, "spread", (c, 3)))
                    dve.wait_ge(h_score, k + 1)
                    ins_ = nc.vector.tensor_tensor(z, z, nbc[:, j0:j0 + 2, q0:q0 + wd], ALU.add)
                    if diag:
                        link(ins_)
                        for i in range(2):
                            ins_ = nc.vector.tensor_tensor(z[:, i, 0:P], z[:, i, 0:P], w["maskt"][:], ALU.add)
                    ins_.then_inc(h_sub, 1)

                for x in SIDE[l][-1]:
                    side_job(*x)
                for p in range(POSITIONS[l] + 1):
                    for i in range(len(OUTS[l])):
                        if OUTS[l][i][0] == p:
                            outputs_out(i)
                    k = p - HYP_AT
                    if l and 0 <= k - 1 < HYP_HALVES:
                        hyp_arg(k - 1)
                    first = (len(SIDE[l][p]) + 1) // 2 if l and k >= 0 else 99
                    for x in SIDE[l][p][:first]:
                        side_job(*x)
                    if l and 0 <= k - 2 < HYP_HALVES:
                        hyp_shift(k - 2)
                    for x in SIDE[l][p][first:]:
                        side_job(*x)
                j = 2
                for c in range(NC):
                    dve.wait_ge(a.final, c + 1)
                    y, res = ps[:, (2 if l else 0) + c, :], chunk(xT, c)
                    if l == 0:
                        link(nc.vector.scalar_tensor_tensor(out=chunk(tmp, c), in0=y, scalar=cols[:, C_BF:C_BF + 1],
                                                            in1=chunk(hT, c), op0=ALU.add, op1=ALU.add))
                        nc.vector.scalar_tensor_tensor(out=res, in0=chunk(tmp, c), scalar=modb[:, l, j:j + 1],
                                                       in1=res, op0=ALU.mult, op1=ALU.add).then_inc(a.x, 1)
                    else:
                        link(nc.vector.tensor_scalar(chunk(tmp, c), y, cols[:, C_PB:C_PB + 1], None, ALU.add))
                        nc.vector.scalar_tensor_tensor(out=res, in0=chunk(tmp, c), scalar=modb[:, l, j:j + 1],
                                                       in1=res, op0=ALU.mult, op1=ALU.add).then_inc(a.x, 1)

            def top(dst, src, t_, T, E, k):
                a4 = cmpa[:, 0:T * E * E].rearrange("p (t e f) -> p t e f", t=T, e=E)
                link(nc.vector.tensor_tensor(a4, src.unsqueeze(2).broadcast_to([P, T, E, E]),
                                             src.unsqueeze(3).broadcast_to([P, T, E, E]), ALU.is_ge))
                link(nc.vector.tensor_tensor(a4, a4, w["tri"][:, 0:E, 0:E].unsqueeze(1).broadcast_to([P, T, E, E]),
                                             ALU.mult))
                nc.vector.tensor_reduce(dst, a4, AX.X, ALU.add)
                link(nc.vector.tensor_reduce(t_, a4.rearrange("p t e f -> p t f e"), AX.X, ALU.add))
                link(nc.vector.tensor_tensor(dst, dst, t_, ALU.subtract))
                link(nc.vector.tensor_tensor(dst, dst, w["after"][:, 16 - E:16].unsqueeze(1).broadcast_to([P, T, E]),
                                             ALU.add))
                link(nc.vector.tensor_scalar(dst, dst, k - 0.5, None, ALU.is_lt))

            def route(l, c, stage):
                f, g = FFN[l], fs[l]
                E, T = f.experts, 4
                tiles = slice(T * c, T * c + T)
                s, sb_, m, t0, t1 = (lg[:, i, tiles, 0:E] for i in range(5))
                den, rc, ok = lg[:, 5, tiles, 0:1], lg[:, 6, tiles, 0:1], lg[:, 7, tiles, 0:1]

                def wide(x, e=E):
                    return x.broadcast_to([P, T, e])

                if stage == 0:
                    dve.wait_ge(g.score, 1)
                    link(nc.vector.tensor_scalar(s, s, 1.0, None, ALU.add))
                    link(nc.vector.reciprocal(s, s))
                    link(nc.vector.tensor_tensor(sb_, s, w[f"rbias{l}"][:].unsqueeze(1).broadcast_to([P, T, E]),
                                                 ALU.add))
                    if l:
                        sg, mg, xg = (lg[:, i, tiles].rearrange("p t (g e) -> p (t g) e", e=4) for i in (1, 2, 4))
                        top(mg, sg, xg, 4 * T, 4, 2)
                        link(nc.vector.tensor_tensor(mg, mg, sg, ALU.mult))
                elif stage == 1:
                    if l:
                        gs, gm, xg = (lg[:, i, tiles, 0:4] for i in (3, 4, 5))
                        link(nc.vector.tensor_reduce(gs, lg[:, 2, tiles].rearrange("p t (g e) -> p t g e", e=4), AX.X,
                                                     ALU.add))
                        top(gm, gs, xg, T, 4, 2)
                        link(nc.vector.tensor_scalar(gs, gm, -1.0, None, ALU.add))
                        s4 = lg[:, 1, tiles].rearrange("p t (g e) -> p t g e", e=4)
                        link(nc.vector.tensor_tensor(s4, s4, gm.unsqueeze(3).broadcast_to([P, T, 4, 4]), ALU.mult))
                        link(nc.vector.tensor_tensor(s4, s4, gs.unsqueeze(3).broadcast_to([P, T, 4, 4]), ALU.add))
                elif stage == 2:
                    top(m, sb_, t0, T, E, 4 if l else 2)
                else:
                    link(nc.vector.tensor_tensor(t0, s, m, ALU.mult))
                    link(nc.vector.tensor_reduce(den, t0, AX.X, ALU.add))
                    link(nc.vector.tensor_scalar(rc, den, 1e-20 if l else 1e-09, None, ALU.add))
                    link(nc.vector.reciprocal(rc, rc))
                    if l:
                        link(nc.vector.tensor_tensor(t0, t0, wide(rc), ALU.mult))
                        link(nc.vector.tensor_scalar(t0, t0, 2.5, None, ALU.mult))
                    else:
                        link(nc.vector.tensor_scalar(ok, den, 1e-09, None, ALU.is_gt))
                        link(nc.vector.tensor_tensor(rc, rc, ok, ALU.mult))
                        link(nc.vector.tensor_tensor(t0, t0, wide(rc), ALU.mult))
                        link(nc.vector.tensor_scalar(ok, ok, -0.5, 0.5, ALU.mult, ALU.add))
                        link(nc.vector.tensor_tensor(m, m, wide(ok), ALU.mult))
                        link(nc.vector.tensor_tensor(t0, t0, m, ALU.add))
                    split(t0, lambda k: gp[:, tiles, k * E:(k + 1) * E], t1).then_inc(g.parts, 1)

            def ffn(l):
                f, g = FFN[l], fs[l]

                def update(c):
                    dve.wait_ge(g.down, f.last[c] + 1)
                    nc.vector.scalar_tensor_tensor(out=chunk(xT, c), in0=ps[:, c, :], scalar=modb[:, l, 5:6],
                                                   in1=chunk(xT, c), op0=ALU.mult, op1=ALU.add).then_inc(g.x, 1)

                for stage in range(4):
                    route(l, 0, stage)
                for i, (kind, e, c) in enumerate(f.work):
                    if kind == "shared":
                        continue
                    dve.wait_ge(g.act, i + 1)
                    if i >= 2:
                        dve.wait_ge(g.down, i - 1)
                    hid, a_ = fh[:, i % 2, :], fa[:, i % 2, :]
                    if not f.gated:
                        nc.vector.tensor_tensor(hid, a_, ps[:, 6 + i % 2, :], ALU.mult).then_inc(g.hid, 1)
                    else:
                        link(nc.vector.tensor_tensor(ft[:, i % 2, :], a_, ps[:, 4 + i % 2, :], ALU.mult))
                        nc.vector.tensor_tensor(hid, ft[:, i % 2, :], ps[:, 6 + i % 2, :], ALU.mult).then_inc(
                            g.hid, 1)
                    if i - f.first[0] < 4:
                        route(l, 1, i - f.first[0])
                    if i == f.last[0] + 2:
                        update(0)
                update(1)

            for c in range(NC):
                dve.wait_ge(x_tok, c + 1)
                nc.vector.tensor_copy(chunk(xT, c), ps[:, c, :]).then_inc(x_ready, 1)
            for l in range(2):
                layer_norm(2 * l)
                prepare(l)
                attention(l)
                layer_norm(2 * l + 1)
                ffn(l)
            for c in range(NC):
                dve.wait_ge(s_out_tok, c + 1)
                nc.vector.tensor_copy(xn[:, 4 * c:4 * c + 4, :].rearrange("p t d -> p (t d)"),
                                      ps[:, 2 + c, :]).then_inc(x_out, 1)

        def pool_program(pool):
            def select_gates(l):
                pool.wait_ge(at[l].x, NC)
                e, at0 = FFN[l].experts, 8 * l
                for i in range(e):
                    ins_ = nc.gpsimd.tensor_copy(selg(e)[:, i, :],
                                                 w["rows"][0:3 * e, at0 + i:at0 + i + 1].broadcast_to([3 * e, P]))
                ins_.then_inc(sel_ready, 1)

            def shared_products(l):
                g = fs[l]
                for i in range(2 * NC):
                    pool.wait_ge(g.ucopy, i + 1)
                    if i >= 2:
                        pool.wait_ge(g.down, i - 1)
                    nc.gpsimd.tensor_tensor(fh[:, i % 2, :], fa[:, i % 2, :], ft[:, i % 2, :],
                                            ALU.mult).then_inc(g.shared, 1)

            for i in range(NC * UNITS):
                u, c = i // NC, i % NC
                pool.wait_ge(at[0].o_out, i + 1)
                pool.wait_ge(at[0].rs, i + 1)
                nc.gpsimd.tensor_tensor(on[:, u, c * CH:(c + 1) * CH], osb[:, i % 2, :], rsb[:, i % 2, :],
                                        ALU.mult).then_inc(at[0].on, 1)
            pool.wait_ge(at[0].pv, NS * UNITS)
            nc.gpsimd.memset(vt[:], 1.0).then_inc(v_ones, 1)
            select_gates(0)
            shared_products(0)
            for k in range(HYP_HALVES):
                pool.wait_ge(h_root, k + 1)
                nc.gpsimd.tensor_tensor(hyp_z(k), hyp_z(k), hyp_x(k), ALU.add).then_inc(h_sum, 1)
            select_gates(1)
            shared_products(1)

        def sync_program(sp, b):
            sp.dma_start(xn[:], ins["x"][b].rearrange("(t p) d -> p t d", p=P)).then_inc(x_in, 16)

            def load_unit(l, u):
                a = at[l]
                for side, op in enumerate((qop, kop)):
                    if u == 0:
                        sp.wait_ge(a.stored[side], 48)
                    for i in range(3):
                        heads = scratch[l, side, :, :, 4 * u:4 * u + 4, :].rearrange("i d h n -> i d (h n)")
                        if side:
                            src = heads[i:i + 1].broadcast_to([3, HD, 4 * N])
                        else:
                            src = heads.rearrange("i d n -> (i d) n")
                        sp.dma_start(op[24 * i:24 * i + 24, slot(l, u), :, :].rearrange("p h n -> p (h n)"),
                                     src).then_inc(a.ops[u], 16)
                if is_hyp(l, u):
                    for op, rows, ready in ((qop, trow[0], t_row), (kop, trow[1], t_krow)):
                        sp.wait_ge(ready, 1)
                        sp.dma_start(op[TROW:TROW + 9, slot(l, u), :, :], rows).then_inc(a.ops[u], 16)

            for l in range(2):
                a = at[l]
                if l:
                    sp.wait_ge(at[0].x, NC)
                    sp.dma_start(cos, ins["cos"]).then_inc(tables, 16)
                    sp.dma_start(qop[MAXROW:MAXROW + 3, slot(l, HYP_UNIT), :, :], ins["onerow"]).then_inc(
                        a.ops[HYP_UNIT], 16)
                    sp.dma_start(sin, ins["sin"]).then_inc(tables, 16)
                for side in range(2):
                    for i in range(3):
                        sp.wait_ge(a.parts, 3 * side + i + 1)
                        sp.dma_start(scratch[l, side, i].rearrange("d h n -> h d n"),
                                     parts[:, side, i]).then_inc(a.stored[side], 16)
                first, late = ((0, HYP_UNIT, 1), 2) if l else ((0, 1, 2), 3)
                for u in first:
                    load_unit(l, u)

                def send_maxima(u, chunks):
                    sp.wait_ge(a.side_out, side_count(l, "max", (u, chunks)))
                    for i in range(3):
                        r = MAXROW + i
                        sp.dma_start(qop[r:r + 1, slot(l, u), :, :].rearrange("p j (q n) -> p (j q) n", n=P),
                                     mrow[32 * i:32 * i + 32, :]).then_inc(a.maxrow[u], 16)

                for u, chunks in MAXES[l]:
                    if u < 2:
                        send_maxima(u, chunks)
                sp.wait_ge(a.pv, NS)
                load_unit(l, late)
                for u, chunks in MAXES[l]:
                    if u >= 2 and not is_hyp(l, u):
                        send_maxima(u, chunks)
            for c in range(NC):
                sp.wait_ge(x_out, c + 1)
                sp.dma_start(out[b, c * CH:(c + 1) * CH, :].rearrange("(t p) d -> p t d", p=P),
                             xn[:, 4 * c:4 * c + 4, :]).then_inc(x_in, 16)
            sp.wait_ge(x_in, 48)


        with nc.Fori(0, B) as b:
            with nc.Block() as block:
                @block.sync
                def _(sp):
                    sync_program(sp, b)

                @block.tensor
                def _(pe):
                    tensor_program(pe)

                @block.scalar
                def _(act):
                    scalar_program(act)

                @block.vector
                def _(dve):
                    nc.vector.tensor_copy(modb[:], mod[:, :, :, bass.ds(b, 1)].rearrange(
                        "p l j b -> p l (j b)")).then_inc(mod_ready, 1)
                    vector_program(dve)

                @block.gpsimd
                def _(pool):
                    pool_program(pool)
            first, last = loop_sems[0].num, loop_sems[-1].num
            assert last - first + 1 == len(loop_sems)
            nc.all_engine_barrier(sems_to_clear=range(first, last + 1))


def kernel(**inputs):
    import concourse.bacc as _bacc
    from concourse.bass_utils import run_bass_kernel_spmd as _run

    a = {k: np.asarray(v) for k, v in inputs.items()}
    order = np.array([h * HD + d for h in HEAD_ORDER for d in range(HD)])
    swap = order.reshape(HEADS, 2, HD // 2)[:, ::-1].reshape(-1)
    qkv = a["L1_attn_qkv_w"]
    q, k, v = qkv[0:D], qkv[D:2 * D], qkv[2 * D:3 * D]

    inv_freq = (np.float32(1.0) / np.float32(10000.0) ** (np.arange(0, HD, 2, dtype=np.float32) / np.float32(HD)))
    freqs = np.outer(inv_freq.astype(np.float32), np.arange(N, dtype=np.float32)).astype(np.float32)
    cos, sin = (f(freqs.astype(np.float64)).astype(np.float32) for f in (np.cos, np.sin))
    half = HD // 2

    cols = np.zeros((P, 16), np.float32)
    pos = np.arange(P) // HD
    heads = np.array(HEAD_ORDER)[pos]
    hyper = (heads >= 6) & (heads < 10)
    cosine = heads >= 10
    curv = a["L1_attn_curvature"].reshape(-1)
    cols[:, 0], cols[:, 1], cols[:, 2] = a["L0_attn_bk"], a["L0_attn_bf"], a["L1_attn_proj_b"]
    cols[:, 4] = 1.0 / np.sqrt(HD)
    cols[cosine, 4] = np.sqrt(HD)
    cols[hyper, 4] = np.repeat(curv, HD)
    cols[:, 5], cols[:, 6] = cosine, ~cosine
    cols[:, 8:12] = a["L0_attn_bv"].reshape(4, P).T

    r = np.arange(P)
    rows = np.zeros((96, 56), np.float32)
    for n, at0 in ((8, 0), (16, 8), (32, 24)):
        rows[:, at0:at0 + n] = np.arange(96)[:, None] % n == np.arange(n)[None, :]

    arrays = {
        "x": a["L0_attn_x"], "Wk": a["L0_attn_Wk"], "Wv": a["L0_attn_Wv"], "Wf": a["L0_attn_Wf"],
        "wq": q[order].T, "wqs": q[swap].T, "wk1": k[order].T, "wks": k[swap].T, "wv1": v[order].T,
        "proj": a["L1_attn_proj_w"].T[order],
        "cos": np.tile(cos, (2 * HEADS, 1)),
        "sin": np.tile(np.concatenate([sin, -sin]), (HEADS, 1)),
        "L0_router": a["L0_ffn_router_w"].T, "L0_rbias": a["L0_ffn_router_bias"],
        "L0_shg": a["L0_ffn_sw1"], "L0_shu": a["L0_ffn_sw3"], "L0_shd": a["L0_ffn_sw2"],
        "L0_gate": a["L0_ffn_ew1"], "L0_down": a["L0_ffn_ew2"],
        "L1_router": a["L1_ffn_router_w"].T, "L1_rbias": a["L1_ffn_bias"],
        "L1_shg": a["L1_ffn_sh_gate_w"], "L1_shu": a["L1_ffn_sh_up_w"], "L1_shd": a["L1_ffn_sh_down_w"],
        "L1_gate": a["L1_ffn_gate_w"], "L1_up": a["L1_ffn_up_w"], "L1_down": a["L1_ffn_down_w"],
        "L0_wmod": a["L0_wmod"], "L1_wmod": a["L1_wmod"],
        "c": np.concatenate([a["L0_c"].T, a["L1_c"].T], axis=1),
        "curv": curv, "cols": cols, "rows": rows,
        "after": np.arange(15, -1, -1).astype(np.float32),
        "tri": np.tril(np.ones((16, 16), np.float32), -1),
        "hsel": (heads[:, None] == 6 + np.arange(4)[None, :]).astype(np.float32),
        "ident": np.eye(P, dtype=np.float32),
        "heads8": np.kron(np.eye(HEADS, dtype=np.float32), np.ones((HD, HD), np.float32)),
        "maskt": np.where(r[:, None] > r[None, :], np.float32(MASK), np.float32(0.0)),
    }
    import ml_dtypes
    onerow = np.zeros((3, 4, N), ml_dtypes.bfloat16)
    onerow[0] = 1
    arrays["onerow"] = onerow
    arrays = {n: np.ascontiguousarray(v) for n, v in arrays.items()}
    nc = _bacc.Bacc("TRN2", target_bir_lowering=False, num_devices=1)
    ins = {n: nc.dram_tensor("in_" + n, v.shape, mybir.dt.from_np(v.dtype), kind="ExternalInput").ap()
           for n, v in arrays.items()}
    out = nc.dram_tensor("out_x", (B, N, D), F32, kind="ExternalOutput").ap()
    adaln_kernel(nc, ins, out)
    res = _run(nc, [{"in_" + n: v for n, v in arrays.items()}], core_ids=[0])
    return res.results[0]["out_x"]
```
